# Optimizing a Trainium2 kernel written in Bass

```python
import numpy as np
import jax
import jax.numpy as jnp

def _softmax(x, axis=-1):
    return jax.nn.softmax(x, axis=axis)

def _gelu(x):
    return jax.nn.gelu(x, approximate=True)

def _silu(x):
    return jax.nn.silu(x)

def _sigmoid(x):
    return jax.nn.sigmoid(x)

def _layernorm(x, axis=-1, eps=1e-05):
    m = jnp.mean(x, axis=axis, keepdims=True)
    v = jnp.var(x, axis=axis, keepdims=True)
    return (x - m) / jnp.sqrt(v + eps)

def _scatter_add(tgt, idx, src, axis=0):
    return tgt.at[idx].add(src)

def _segment_sum(src, seg, n):
    return jax.ops.segment_sum(src, seg, n)
kernel_name = 'mk_recurrent_d2_jaxref_r8_b9d7a4'

def setup_inputs(seed: int=0):
    np.random.seed(seed)
    _w = jnp.asarray

    def _L0_attn_setup():
        import jax, jax.numpy as jnp
        import numpy as np
        B, S, DM = (2, 256, 256)
        H, KVH, HD = (16, 4, 128)
        REP = H // KVH
        ROPE_BASE = 10000.0
        EPS = 1e-06

        def _rope_tables(seq_len, dim):
            inv_freq = 1.0 / ROPE_BASE ** (jnp.arange(0, dim, 2, dtype=jnp.float32) / dim)
            t = jnp.arange(seq_len, dtype=jnp.float32)
            freqs = jnp.outer(t, inv_freq)
            emb = jnp.concatenate([freqs, freqs], -1)
            return (jnp.cos(emb), jnp.sin(emb))

        def _rotate_half(x):
            d = x.shape[-1] // 2
            return jnp.concatenate([-x[..., d:], x[..., :d]], axis=-1)
        key = jax.random.key(seed)
        k0, k1, k2, k3, k4 = jax.random.split(key, 5)
        w = lambda k, o, i: jax.random.normal(k, (o, i), jnp.float32) * (1.0 / np.sqrt(i))
        return {'x': jax.random.normal(k0, (B, S, DM), jnp.float32), 'Wq': w(k1, H * HD, DM), 'Wk': w(k2, KVH * HD, DM), 'Wv': w(k3, KVH * HD, DM), 'Wo': w(k4, DM, H * HD)}
    _L0_attn_in = _L0_attn_setup()

    def _L0_ffn_setup():
        import jax, jax.numpy as jnp
        import numpy as np
        TOP_K = 2
        key = jax.random.key(seed)
        ks = jax.random.split(key, 6)
        B, S, H, F, E = (1, 256, 256, 176, 8)
        Fs = 2 * F
        std = jnp.float32(0.02)
        return {'hidden_states': jax.random.normal(ks[0], (B, S, H), jnp.float32), 'gate_weight': jax.random.normal(ks[1], (E, H), jnp.float32) * std, 'gate_up_weights': jax.random.normal(ks[2], (E, 2 * F, H), jnp.float32) * std, 'down_weights': jax.random.normal(ks[3], (E, H, F), jnp.float32) * std, 'shared_gate_up': jax.random.normal(ks[4], (2 * Fs, H), jnp.float32) * std, 'shared_down': jax.random.normal(ks[5], (H, Fs), jnp.float32) * std}
    _L0_ffn_in = _L0_ffn_setup()

    def _L1_attn_setup():
        import jax, jax.numpy as jnp
        import numpy as np
        B, L, DM = (2, 256, 256)
        H, P, N = (32, 64, 64)
        D_INNER = H * P
        PROJ = 2 * D_INNER + 2 * H * N + H
        EPS = 1e-05
        key = jax.random.key(seed)
        k0, k1, k2 = jax.random.split(key, 3)
        return {'x': jax.random.normal(k0, (B, L, DM), jnp.float32), 'W_in': jax.random.normal(k1, (PROJ, DM), jnp.float32) * DM ** (-0.5), 'W_out': jax.random.normal(k2, (DM, D_INNER), jnp.float32) * D_INNER ** (-0.5), 'gamma': jnp.ones((D_INNER,), jnp.float32), 'beta': jnp.zeros((D_INNER,), jnp.float32), 'D': jnp.ones((H, P), jnp.float32)}
    _L1_attn_in = _L1_attn_setup()

    def _L1_ffn_setup():
        import jax, jax.numpy as jnp
        import numpy as np
        DIM = 256
        HID = 704
        ZERO_POINT = 128.0

        def _qlinear(x, wq, scale):
            W = (wq.astype(jnp.float32) - ZERO_POINT) * scale[:, None]
            return jnp.einsum('bsd,hd->bsh', x, W)
        key = jax.random.key(seed)
        ks = jax.random.split(key, 7)
        B, S = (4, 256)
        sg = jax.random.uniform(ks[1], (HID,)) * (0.02 / np.sqrt(DIM)) + 0.0001
        su = jax.random.uniform(ks[3], (HID,)) * (0.02 / np.sqrt(DIM)) + 0.0001
        sd = jax.random.uniform(ks[5], (DIM,)) * (0.02 / np.sqrt(HID)) + 0.0001
        return {'x': jax.random.normal(ks[0], (B, S, DIM), dtype=jnp.float32), 'wq_gate': jax.random.randint(ks[2], (HID, DIM), 0, 32, dtype=jnp.int32), 's_gate': sg, 'wq_up': jax.random.randint(ks[4], (HID, DIM), 0, 32, dtype=jnp.int32), 's_up': su, 'wq_down': jax.random.randint(ks[6], (DIM, HID), 0, 32, dtype=jnp.int32), 's_down': sd}
    _L1_ffn_in = _L1_ffn_setup()
    _d = {'L0_attn_x': _L0_attn_in['x'], 'L0_attn_Wq': _L0_attn_in['Wq'], 'L0_attn_Wk': _L0_attn_in['Wk'], 'L0_attn_Wv': _L0_attn_in['Wv'], 'L0_attn_Wo': _L0_attn_in['Wo'], 'L0_ffn_gate_weight': _L0_ffn_in['gate_weight'], 'L0_ffn_gate_up_weights': _L0_ffn_in['gate_up_weights'], 'L0_ffn_down_weights': _L0_ffn_in['down_weights'], 'L0_ffn_shared_gate_up': _L0_ffn_in['shared_gate_up'], 'L0_ffn_shared_down': _L0_ffn_in['shared_down'], 'L1_attn_W_in': _L1_attn_in['W_in'], 'L1_attn_W_out': _L1_attn_in['W_out'], 'L1_attn_gamma': _L1_attn_in['gamma'], 'L1_attn_beta': _L1_attn_in['beta'], 'L1_attn_D': _L1_attn_in['D'], 'L1_ffn_wq_gate': _L1_ffn_in['wq_gate'], 'L1_ffn_s_gate': _L1_ffn_in['s_gate'], 'L1_ffn_wq_up': _L1_ffn_in['wq_up'], 'L1_ffn_s_up': _L1_ffn_in['s_up'], 'L1_ffn_wq_down': _L1_ffn_in['wq_down'], 'L1_ffn_s_down': _L1_ffn_in['s_down']}
    _x0 = _d['L0_attn_x']
    _d['L0_attn_x'] = jax.random.normal(jax.random.fold_in(jax.random.key(seed), 1), (2, 1024, 256), dtype=_x0.dtype)
    del _x0
    return _d

def reference(L0_attn_x, L0_attn_Wq, L0_attn_Wk, L0_attn_Wv, L0_attn_Wo, L0_ffn_gate_weight, L0_ffn_gate_up_weights, L0_ffn_down_weights, L0_ffn_shared_gate_up, L0_ffn_shared_down, L1_attn_W_in, L1_attn_W_out, L1_attn_gamma, L1_attn_beta, L1_attn_D, L1_ffn_wq_gate, L1_ffn_s_gate, L1_ffn_wq_up, L1_ffn_s_up, L1_ffn_wq_down, L1_ffn_s_down):

    def _L0_attn_ref(x, Wq, Wk, Wv, Wo):
        import jax, jax.numpy as jnp
        import numpy as np
        B, S, DM = (2, 256, 256)
        H, KVH, HD = (16, 4, 128)
        REP = H // KVH
        ROPE_BASE = 10000.0
        EPS = 1e-06

        def _rope_tables(seq_len, dim):
            inv_freq = 1.0 / ROPE_BASE ** (jnp.arange(0, dim, 2, dtype=jnp.float32) / dim)
            t = jnp.arange(seq_len, dtype=jnp.float32)
            freqs = jnp.outer(t, inv_freq)
            emb = jnp.concatenate([freqs, freqs], -1)
            return (jnp.cos(emb), jnp.sin(emb))

        def _rotate_half(x):
            d = x.shape[-1] // 2
            return jnp.concatenate([-x[..., d:], x[..., :d]], axis=-1)
        bsz, seq_len, _ = x.shape
        q = (x @ Wq.T).reshape(bsz, seq_len, H, HD).transpose(0, 2, 1, 3)
        k = (x @ Wk.T).reshape(bsz, seq_len, KVH, HD).transpose(0, 2, 1, 3)
        v = (x @ Wv.T).reshape(bsz, seq_len, KVH, HD).transpose(0, 2, 1, 3)
        cos, sin = _rope_tables(seq_len, HD)
        cos, sin = (cos[None, None], sin[None, None])
        q = q * cos + _rotate_half(q) * sin
        k = k * cos + _rotate_half(k) * sin
        k = jnp.repeat(k, REP, axis=1)
        v = jnp.repeat(v, REP, axis=1)
        qf = jax.nn.elu(q) + 1.0
        kf = jax.nn.elu(k) + 1.0
        qf_t = qf.transpose(2, 0, 1, 3)
        kf_t = kf.transpose(2, 0, 1, 3)
        v_t = v.transpose(2, 0, 1, 3)

        def step(carry, inp):
            state, z = carry
            q_s, k_s, v_s = inp
            state = state + k_s[..., :, None] * v_s[..., None, :]
            z = z + k_s
            num = jnp.einsum('bhe,bhed->bhd', q_s, state)
            den = jnp.einsum('bhe,bhe->bh', q_s, z)[..., None] + EPS
            return ((state, z), num / den)
        init = (jnp.zeros((bsz, H, HD, HD), x.dtype), jnp.zeros((bsz, H, HD), x.dtype))
        _, out = jax.lax.scan(step, init, (qf_t, kf_t, v_t))
        out = out.transpose(1, 0, 2, 3).reshape(bsz, seq_len, H * HD)
        return out @ Wo.T

    def _L0_ffn_ref(hidden_states, gate_weight, gate_up_weights, down_weights, shared_gate_up, shared_down):
        import jax, jax.numpy as jnp
        import numpy as np
        TOP_K = 2
        B, S, H = hidden_states.shape
        E, twoF, _ = gate_up_weights.shape
        F = twoF // 2
        T = B * S
        x = hidden_states.reshape(T, H)
        logits = x @ gate_weight.T
        scores = jax.nn.softmax(logits, axis=-1)
        topk_w, topk_idx = jax.lax.top_k(scores, TOP_K)
        combine = jnp.zeros((T, E), x.dtype).at[jnp.arange(T)[:, None], topk_idx].add(topk_w)
        gu = jnp.einsum('th,efh->tef', x, gate_up_weights)
        act = jax.nn.silu(gu[..., :F]) * gu[..., F:]
        y = jnp.einsum('tef,te,ehf->th', act, combine, down_weights)
        Fs = shared_gate_up.shape[0] // 2
        sgu = x @ shared_gate_up.T
        sact = jax.nn.silu(sgu[:, :Fs]) * sgu[:, Fs:]
        y = y + sact @ shared_down.T
        return y.reshape(B, S, H)

    def _L1_attn_ref(x, W_in, W_out, gamma, beta, D):
        import jax, jax.numpy as jnp
        import numpy as np
        B, L, DM = (2, 256, 256)
        H, P, N = (32, 64, 64)
        D_INNER = H * P
        PROJ = 2 * D_INNER + 2 * H * N + H
        EPS = 1e-05
        Bz, Lz, _ = x.shape
        zxbca = x @ W_in.T
        x_t, z_t, b_t, c_t, a_log = jnp.split(zxbca, [D_INNER, 2 * D_INNER, 2 * D_INNER + H * N, 2 * D_INNER + 2 * H * N], axis=-1)
        x_t = x_t.reshape(Bz, Lz, H, P)
        b_t = b_t.reshape(Bz, Lz, H, N)
        c_t = c_t.reshape(Bz, Lz, H, N)
        decay = jnp.exp(-jnp.exp(a_log))

        def step(states, inp):
            xt, bt, ct, dec = inp
            states = states * dec[:, :, None, None] + xt[..., None] * bt[:, :, None, :]
            yt = jnp.einsum('bhpn,bhn->bhp', states, ct) + xt * D
            return (states, yt)
        init = jnp.zeros((Bz, H, P, N), x.dtype)
        xs = (jnp.moveaxis(x_t, 1, 0), jnp.moveaxis(b_t, 1, 0), jnp.moveaxis(c_t, 1, 0), jnp.moveaxis(decay, 1, 0))
        _, ys = jax.lax.scan(step, init, xs)
        y = jnp.moveaxis(ys, 0, 1).reshape(Bz, Lz, D_INNER)
        y = y * jax.nn.silu(z_t)
        mu = y.mean(-1, keepdims=True)
        var = y.var(-1, keepdims=True)
        y = (y - mu) * jax.lax.rsqrt(var + EPS) * gamma + beta
        return y @ W_out.T

    def _L1_ffn_ref(x, wq_gate, s_gate, wq_up, s_up, wq_down, s_down):
        import jax, jax.numpy as jnp
        import numpy as np
        DIM = 256
        HID = 704
        ZERO_POINT = 128.0

        def _qlinear(x, wq, scale):
            W = (wq.astype(jnp.float32) - ZERO_POINT) * scale[:, None]
            return jnp.einsum('bsd,hd->bsh', x, W)
        gate = _qlinear(x, wq_gate, s_gate)
        gate = jax.nn.silu(gate)
        up = _qlinear(x, wq_up, s_up)
        return _qlinear(gate * up, wq_down, s_down)
    x = L0_attn_x
    xn = _layernorm(x, axis=-1)
    s = _L0_attn_ref(xn, L0_attn_Wq, L0_attn_Wk, L0_attn_Wv, L0_attn_Wo)
    g = _silu(_L0_ffn_ref(xn, L0_ffn_gate_weight, L0_ffn_gate_up_weights, L0_ffn_down_weights, L0_ffn_shared_gate_up, L0_ffn_shared_down))
    x = x + s * g
    xn = _layernorm(x, axis=-1)
    s = _L1_attn_ref(xn, L1_attn_W_in, L1_attn_W_out, L1_attn_gamma, L1_attn_beta, L1_attn_D)
    g = _silu(_L1_ffn_ref(xn, L1_ffn_wq_gate, L1_ffn_s_gate, L1_ffn_wq_up, L1_ffn_s_up, L1_ffn_wq_down, L1_ffn_s_down))
    x = x + s * g
    return x

_drawn_inputs = setup_inputs


def setup_inputs(seed=0):
    import zlib

    import numpy as np

    out = dict(_drawn_inputs(seed))
    spreads = {'L1_attn_gamma': (1.0, 0.6), 'L1_attn_beta': (0.0, 0.8), 'L1_attn_D': (1.0, 0.6)}
    factors = {'L0_attn_Wq': 8.0,
     'L0_attn_Wk': 8.0,
     'L0_attn_Wv': 8.0,
     'L0_attn_Wo': 8.0,
     'L0_ffn_gate_weight': 8.0,
     'L0_ffn_gate_up_weights': 8.0,
     'L0_ffn_down_weights': 8.0,
     'L0_ffn_shared_gate_up': 8.0,
     'L0_ffn_shared_down': 8.0,
     'L1_attn_W_in': 8.0,
     'L1_attn_W_out': 8.0,
     'L1_ffn_s_gate': 8.0,
     'L1_ffn_s_up': 8.0,
     'L1_ffn_s_down': 8.0}
    for name, (base, spread) in spreads.items():
        noise = np.random.default_rng([zlib.crc32(name.encode()), seed]).standard_normal(out[name].shape)
        drawn = base * np.exp(spread * noise) if base else spread * noise
        out[name] = jnp.asarray(drawn.astype(out[name].dtype))
    for name, factor in factors.items():
        out[name] = (out[name] * factor).astype(out[name].dtype)
    return out
```

```python
from contextlib import ExitStack

import numpy as np

import concourse.bass as bass
from concourse import mybir

P = 128
F32 = mybir.dt.float32
F32R = mybir.dt.float32r
I32 = mybir.dt.int32
ALU = mybir.AluOpType
ACT = mybir.ActivationFunctionType
AX = mybir.AxisListType

B = 2
T = 1024
DM = 256
KT = DM // P
NC = T // P
HALF = 512
INNER = 2048
NT = INNER // P

KVH, REP = 4, 4
QKV = (REP + 2) * P
NE = 8
FE = 176
FG = 2 * FE
G0, G1 = NE // 2 + 1, 2
GRP = G0 + G1
DT = 3

HP = 16
XZBC = 4 * P
SH = 32

LN_EPS = 1e-5
DEN_EPS = 1e-6
ZERO_POINT = 128.0
SPLITS = ((0, 0), (0, 1), (1, 0))
PHASES = 7
CONSTS = 7
RAWS = G0 + KVH + G1 + HP


class Event:

    def __init__(self, sem, credit):
        self.sem, self.credit = sem, credit

    def done(self, n):
        return n + 1 + self.credit

    def free(self, n, depth):
        return n + 1 + self.credit - depth


def build(nc, a):
    with ExitStack() as ctx:
        events = {}

        def event(name, owner, credit=16):
            e = Event(ctx.enter_context(nc.semaphore(name)), credit)
            events.setdefault(owner, []).append(e)
            return e

        def sem(name):
            return ctx.enter_context(nc.semaphore(name))

        def fixed(name, shape, dt=F32):
            return ctx.enter_context(nc.sbuf_tensor(name, shape, dt))

        x_res = fixed("x_res", [P, NC, DM])
        gate = fixed("gate", [P, NC, DM])
        xnT = [fixed(f"xnT_{s}", [P, KT, T], F32R) for s in ("hi", "lo")]
        ident8 = fixed("ident8", [P, T])
        causal4 = fixed("causal4", [P, REP * P])
        earlier = fixed("earlier", [P, NE * NE])
        w_out = fixed("w_out", [P, NT, DM])
        w_raw = fixed("w_raw", [P, KT * QKV])
        dn_raw = fixed("dn_raw", [P, 2, DT, DM])
        xn = fixed("xn", [P, 2, DM])
        router = [fixed(f"router_{s}", [P, KT, NE], F32R) for s in ("hi", "lo")]
        w_dec = [fixed(f"w_dec_{s}", [P, KT, P], F32R) for s in ("hi", "lo")]
        combine = fixed("combine", [P, 2 * G0, NC])
        combine_g = fixed("combine_g", [P, 2, 2, NC])
        den = fixed("den", [P, NC, KVH * REP])
        att_state = fixed("att_state", [P, 2, P + 1])
        ssm_state = fixed("ssm_state", [P, 2, P])
        ln_eps = fixed("ln_eps", [P, 1])
        ln_st = fixed("ln_st", [P, 2, 6])
        ln_mv = fixed("ln_mv", [P, 2, 2])
        ln_sd = fixed("ln_sd", [P, 2, 1])
        ln_rs = fixed("ln_rs", [P, 2, 1])
        in_st = fixed("in_st", [P, 2, 4 * 6])
        in_mv = fixed("in_mv", [P, 2, 2])
        in_sd = fixed("in_sd", [P, 2, 1])
        in_rs = fixed("in_rs", [P, 2, 1])
        gamma = fixed("gamma", [P, NT])
        beta = fixed("beta", [P, NT])

        def group():
            made = ExitStack()

            def shared(name, shape, dt=F32):
                return made.enter_context(nc.sbuf_tensor(name, shape, dt))
            return made, shared

        done, shared = group()
        y = shared("y", [P, NC, INNER])
        y_bytes_end = nc.sbuf_base
        done.close()
        done, shared = group()
        gu = [[shared(f"gu_{s}{k}", [P, KT, 2 * FG], F32R) for s in ("hi", "lo")] for k in range(2)]
        gu_f = shared("gu_f", [P, KT, 2 * FG])
        dn_f = shared("dn_f", [P, 2, DT, DM])
        s_gu = shared("s_gu", [P, 2, 2 * FG])
        s_dn = shared("s_dn", [P, DM])
        silu_g = shared("silu_g", [P, 2, FG])
        hid = shared("hid", [P, 2, DT * P])
        hidT = shared("hidT", [P, 2, DT * P])
        rt_l = shared("rt_l", [P, NC, NE])
        rt_m = shared("rt_m", [P, NC])
        rt_s = shared("rt_s", [P, NC])
        rt_gt = shared("rt_gt", [P, NC * NE, NE])
        rt_eq = shared("rt_eq", [P, NC * NE, NE])
        rt_rank = shared("rt_rank", [P, NC * NE])
        assert nc.sbuf_base <= y_bytes_end
        done.close()
        ctx.enter_context(nc.sbuf_tensor("y_fence", [P, NC * INNER], F32))

        done, shared = group()
        w_qkv = [shared(f"w_qkv_{s}", [P, KT, QKV], F32R) for s in ("hi", "lo")]
        qT = shared("qT", [P, REP, T])
        kT = shared("kT", [P, T])
        k_tok = shared("k_tok", [P, NC, P])
        v_tok = shared("v_tok", [P, NC, P + 1])
        vT = shared("vT", [P, HALF])
        cos = shared("cos", [P, T])
        sin = shared("sin", [P, T])
        ra = shared("ra", [P, 2, HALF])
        rb = shared("rb", [P, 2, HALF])
        mt = shared("mt", [P, 2, REP * P])
        done.close()
        done, shared = group()
        w_in = [[shared(f"w_in_{s}{k}", [P, KT, XZBC], F32R) for s in ("hi", "lo")] for k in range(2)]
        bT = shared("bT", [P, T])
        cTz = shared("cTz", [P, 2, T])
        cTp = shared("cTp", [P, T])
        b_tok = shared("b_tok", [P, NC, P])
        dec = shared("dec", [P, 2, T])
        lmat = shared("lmat", [P, 2, T])
        pdec = shared("pdec", [P, T])
        dstart = shared("dstart", [P, T])
        xz_x = shared("xz_x", [P, 2, 2 * P])
        sz = shared("sz", [P, 2, P])
        xw = shared("xw", [P, 2, P])
        xd = shared("xd", [P, 2, P])
        yg = shared("yg", [P, 2, P])
        mt1 = shared("mt1", [P, 2, 2 * P])
        d_row = shared("d_row", [P, 2, P])
        done.close()
        done, shared = group()
        dec_e = shared("dec_e", [SH, T])
        dec_t = shared("dec_t", [SH, T])
        done.close()
        done, shared = group()
        yn = shared("yn", [P, 2, INNER])
        yT = shared("yT", [P, 2, NT, P])
        sg = shared("sg", [P, 2, DM])
        rin = shared("rin", [P, 2, NT])
        rin2 = shared("rin2", [P, 2, NT])
        done.close()

        ps = ctx.enter_context(nc.psum_tensor("ps", [P, 8, 512], F32))
        dec_dram = nc.dram_tensor("dec_dram", (SH, T), F32, kind="Internal").ap()

        consts_in, x_in, w_raw_in, tables_in = sem("consts_in"), sem("x_in"), sem("w_raw_in"), sem("tables_in")
        dn_in = [sem("dn_in0"), sem("dn_in1")]
        w_out_in, scales_in = sem("w_out_in"), sem("scales_in")
        dec_in, dec_out, d_in = sem("dec_in"), sem("dec_out"), [sem("d_in0"), sem("d_in1")]
        stored = sem("stored")
        phase_end = sem("phase_end")
        init_step, settled = sem("init_step"), sem("settled")
        own_dve, own_act, own_pool = sem("own_dve"), sem("own_act"), sem("own_pool")
        rin_step, rin_step2, s_prep = sem("den_step"), sem("inner_ln_step"), sem("dec_prep")

        w_split = event("w_split", "pool")
        w_hi = event("w_hi", "act")
        ln_stat, ln_var = event("ln_stat", "dve"), event("ln_var", "dve")
        ln_std, ln_rstd = event("ln_std", "act"), event("ln_rstd", "dve")
        ln_xn, ln_tr = event("ln_xn", "dve"), event("ln_tr", "pe")
        ln_hi, ln_lo = event("ln_hi", "act"), event("ln_lo", "dve")
        rt_logits, rt_dve, rt_exp = event("rt_logits", "pe"), event("rt_dve", "dve"), event("rt_exp", "act")
        gate_zero = event("gate_zero", "pool")
        f_wf = event("f_wf", "dve")
        f_gu, f_silu, f_hid = event("f_gu", "pe"), event("f_silu", "act"), event("f_hid", "dve")
        f_tr, f_hidT, f_dn, f_acc = event("f_tr", "pe"), event("f_hidT", "act"), event("f_dn", "pe"), event("f_acc", "dve")
        f_cg = event("f_cg", "dve")
        dn_made = event("dn_made", "dve")
        a_proj = event("a_proj", "pe")
        a_mul, a_rot, a_act, a_qk = event("a_mul", "dve"), event("a_rot", "pool"), event("a_act", "act"), event("a_qk", "dve")
        a_neg = event("a_neg", "act")
        a_vT, a_trk, a_trv, a_kv = event("a_vT", "act"), event("a_trk", "pe"), event("a_trv", "pe"), event("a_kv", "act")
        a_sc, a_mt, a_up, a_st = event("a_sc", "pe"), event("a_mt", "dve"), event("a_up", "pe"), event("a_st", "dve")
        a_nd, a_out = event("a_nd", "pe"), event("a_out", "act")
        s_loga, s_dec = event("s_loga", "pe"), event("s_dec", "act")
        s_scan = event("s_scan", "dve")
        s_pb, s_pc, s_b, s_c = event("s_pb", "pe"), event("s_pc", "pe"), event("s_b", "act"), event("s_c", "act")
        s_cp, s_trb, s_btok = event("s_cp", "dve"), event("s_trb", "pe"), event("s_btok", "act")
        s_xz, s_xcopy, s_xw, s_xd = event("s_xz", "pe"), event("s_xcopy", "act"), event("s_xw", "dve"), event("s_xd", "pool")
        s_sc, s_mt, s_up, s_st = event("s_sc", "pe"), event("s_mt", "dve"), event("s_up", "pe"), event("s_st", "dve")
        s_y, s_yg, s_out = event("s_y", "pe"), event("s_yg", "dve"), event("s_out", "pool")
        o_stat, o_std = event("o_stat", "dve"), event("o_std", "act")
        o_yn, o_tr, o_yT = event("o_yn", "dve"), event("o_tr", "pe"), event("o_yT", "act")
        o_mm, o_sg, o_res = event("o_mm", "pe"), event("o_sg", "dve"), event("o_res", "dve")

        def start(eng, owner):
            for e in events[owner]:
                eng.sem_inc(e.sem, e.credit)

        def end_phase(eng, b, phase):
            eng.drain().then_inc(phase_end, 1)
            eng.wait_ge(phase_end, 4 * (b * PHASES + phase + 1))
            settle(eng)

        def settle(eng):
            eng.sem_inc(settled, 1)

        block = ctx.enter_context(nc.Block())

        @block.sync
        def _(sp):
            def weights(n, src, cols):
                sp.wait_ge(w_split.sem, w_split.free(n, 1))
                sp.dma_start(w_raw[:, 0:cols], src).then_inc(w_raw_in, 16)

            def down(slot, src):
                sp.dma_start(dn_raw[:, slot], src).then_inc(dn_in[slot], 16)

            def down_used(b, g):
                sp.wait_ge(f_dn.sem, f_dn.done((b * GRP + g) * NC + NC - 1))

            def phase_over(b, phase):
                sp.wait_ge(phase_end, 4 * (b * PHASES + phase + 1))
                settle(sp)

            sp.sem_inc(stored, 16)
            for dst, src in ((ident8, a["ident8"]), (causal4, a["causal4"]), (earlier, a["earlier"]),
                             (gamma, a["gamma"]), (beta, a["beta"])):
                sp.dma_start(dst[:], src).then_inc(consts_in, 16)
            sp.dma_start(x_res[:, 0, :], a["router"]).then_inc(consts_in, 16)
            sp.dma_start(x_res[:, 1, :], a["w_dec"]).then_inc(consts_in, 16)
            sp.wait_ge(init_step, 2)
            with sp.Fori(0, B) as b:
                sp.wait_ge(stored, 16 * (b + 1))
                settle(sp)
                sp.dma_start(x_res[:], a["x"][bass.ds(b, 1)].rearrange("b (c p) d -> p (b c) d", p=P)).then_inc(x_in, 16)
                sp.wait_ge(dn_made.sem, dn_made.done(b * G1 - 1))
                settle(sp)
                with sp.Fori(0, G0 // 2) as i:
                    for k in range(2):
                        weights(b * RAWS + 2 * i + k, a["gu0"][bass.ds(2 * i + k, 1)].rearrange("g p c -> p (g c)"), KT * 2 * FG)
                        down_used(b, 2 * i + k - 2)
                        down(k, a["dn0"][bass.ds(2 * i + k, 1)].rearrange("g p (t c) -> p (g t) c", t=DT))
                weights(b * RAWS + G0 - 1, a["gu0"][G0 - 1], KT * 2 * FG)
                down_used(b, G0 - 3)
                down(0, a["dn0"][G0 - 1].rearrange("p (t c) -> p t c", t=DT))
                phase_over(b, 1)
                sp.dma_start(w_out[:], a["w_o"]).then_inc(w_out_in, 16)
                sp.dma_start(cos[:], a["cos"]).then_inc(tables_in, 16)
                sp.dma_start(sin[:], a["sin"]).then_inc(tables_in, 16)
                with sp.Fori(0, KVH) as i:
                    weights(b * RAWS + G0 + i, a["w_qkv"][bass.ds(i, 1)].rearrange("g p c -> p (g c)"), KT * QKV)
                for k in range(G1):
                    if k == 0:
                        weights(b * RAWS + G0 + KVH, a["gu1"][0].bitcast(F32), KT * 2 * FG)
                        phase_over(b, 3)
                        sp.dma_start(w_out[:], a["w_out"]).then_inc(w_out_in, 16)
                        for g in range(G1):
                            sp.dma_start(s_gu[:, g, :], a["s_gu"][g:g + 1, :].broadcast_to([P, 2 * FG])).then_inc(scales_in, 16)
                        sp.dma_start(s_dn[:], a["s_dn"].broadcast_to([P, DM])).then_inc(scales_in, 16)
                    else:
                        weights(b * RAWS + G0 + KVH + 1, a["gu1"][1].bitcast(F32), KT * 2 * FG)
                    down_used(b, G0 - 1 - k)
                    down(k, a["dn1"][k].rearrange("p (t c) -> p t c", t=DT).bitcast(F32))
                sp.wait_ge(s_dec.sem, s_dec.done(b))
                sp.dma_start(dec_dram, dec_t[:]).then_inc(dec_out, 16)
                sp.wait_ge(dec_out, 16 * (b + 1))
                settle(sp)
                with sp.Fori(0, HP // 2) as i:
                    for k in range(2):
                        h = 2 * i + k
                        n = b * HP + h
                        weights(b * RAWS + G0 + KVH + G1 + h, a["w_in"][bass.ds(h, 1)].rearrange("g p c -> p (g c)"), KT * XZBC)
                        sp.wait_ge(s_scan.sem, s_scan.free(n, 1))
                        sp.dma_start(dec[:], dec_dram[bass.ds(2 * h, 2), :].partition_broadcast(P)).then_inc(dec_in, 16)
                        sp.wait_ge(s_xd.sem, s_xd.free(n * NC + NC - 1, 2 * NC) - 0)
                        sp.dma_start(d_row[:, k, :], a["d_skip"][bass.ds(h, 1), :].broadcast_to([P, P])).then_inc(d_in[k], 16)
                phase_over(b, 6)
                sp.dma_start(a["out"][bass.ds(b, 1)].rearrange("b (c p) d -> p (b c) d", p=P), x_res[:]).then_inc(stored, 16)
            sp.wait_ge(stored, 16 * (B + 1))

        @block.gpsimd
        def _(pool):
            start(pool, "pool")

            def split_lo(n, lo, raw, hi):
                pool.wait_ge(w_hi.sem, w_hi.done(n))
                nc.gpsimd.tensor_tensor(lo, raw, hi, ALU.subtract).then_inc(w_split.sem, 1)

            with pool.Fori(0, B) as b:
                end_phase(pool, b, 0)

                nc.gpsimd.memset(gate[:], 0.0)
                nc.gpsimd.memset(hid[:, :, FG:DT * P], 0.0).then_inc(gate_zero.sem, 1)
                raw = w_raw[:, 0:KT * 2 * FG].rearrange("p (k c) -> p k c", k=KT)
                with pool.Fori(0, G0 // 2) as i:
                    for k in range(2):
                        split_lo(b * RAWS + 2 * i + k, gu[k][1][:], raw, gu[k][0][:])
                split_lo(b * RAWS + G0 - 1, gu[0][1][:], raw, gu[0][0][:])
                end_phase(pool, b, 1)

                nc.gpsimd.memset(v_tok[:, :, P:P + 1], 1.0)
                raw = w_raw[:].rearrange("p (k c) -> p k c", k=KT)
                with pool.Fori(0, KVH) as i:
                    split_lo(b * RAWS + G0 + i, w_qkv[1][:], raw, w_qkv[0][:])
                    for hf in range(2):
                        for t in range(REP + 1):
                            r = ((b * KVH + i) * 2 + hf) * (REP + 1) + t
                            k = (hf * (REP + 1) + t) % 2
                            pool.wait_ge(a_mul.sem, a_mul.done(r))
                            nc.gpsimd.tensor_tensor(rb[:, k], ra[:, k], rb[:, k], ALU.add).then_inc(a_rot.sem, 1)
                end_phase(pool, b, 2)
                end_phase(pool, b, 3)

                nc.gpsimd.memset(gate[:], 0.0)
                nc.gpsimd.memset(hid[:, :, FG:DT * P], 0.0).then_inc(gate_zero.sem, 1)
                for k in range(G1):
                    split_lo(b * RAWS + G0 + KVH + k, gu[k][1][:], gu_f[:], gu[k][0][:])
                end_phase(pool, b, 4)

                nc.gpsimd.memset(cTz[:], 0.0)
                nc.gpsimd.memset(xz_x[:, :, 64:192], 0.0)
                nc.gpsimd.memset(dstart[:], 0.0)
                pool.drain().then_inc(own_pool, 1)
                raw = w_raw[:, 0:KT * XZBC].rearrange("p (k c) -> p k c", k=KT)
                with pool.Fori(0, HP // 2) as i:
                    for k in range(2):
                        n = b * HP + 2 * i + k
                        split_lo(b * RAWS + G0 + KVH + G1 + 2 * i + k, w_in[k][1][:], raw, w_in[k][0][:])
                        for c in range(NC + 1):
                            m = n * NC + c
                            s = c % 2
                            if c < NC:
                                pool.wait_ge(s_xcopy.sem, s_xcopy.done(m))
                                if c == 0:
                                    pool.wait_ge(d_in[k], 16 * (b * (HP // 2) + i + 1))
                                pool.wait_ge(s_yg.sem, s_yg.free(m, 2))
                                xs = xz_x[:, s, :].rearrange("p (h c) -> p h c", c=64)[:, 0:4:3, :]
                                nc.gpsimd.tensor_tensor(xd[:, s].rearrange("p (h c) -> p h c", c=64), xs,
                                                        d_row[:, k].rearrange("p (h c) -> p h c", c=64),
                                                        ALU.mult).then_inc(s_xd.sem, 1)
                            if c >= 1:
                                m, s = m - 1, 1 - s
                                pool.wait_ge(s_yg.sem, s_yg.done(m))
                                nc.gpsimd.tensor_tensor(y[:, c - 1, bass.ds((2 * i + k) * P, P)], yg[:, s], sz[:, s],
                                                        ALU.mult).then_inc(s_out.sem, 1)
                end_phase(pool, b, 5)
                end_phase(pool, b, 6)

        @block.tensor
        def _(pe):
            start(pe, "pe")

            def three_passes(out, left, right):
                steps = [(k, l, r) for k in range(KT) for l, r in SPLITS]
                for j, (k, l, r) in enumerate(steps):
                    mm = nc.tensor.matmul(out, left(l, k), right(r, k), start=(j == 0), stop=(j == len(steps) - 1))
                return mm

            def ln_transposes(n, s):
                pe.wait_ge(ln_xn.sem, ln_xn.done(n))
                pe.wait_ge(ln_lo.sem, ln_lo.free(n, 2))
                for k in range(KT):
                    mm = nc.tensor.transpose(ps[:, 6 + s, k * P:(k + 1) * P], xn[:, s, k * P:(k + 1) * P], ident8[:, 0:P])
                mm.then_inc(ln_tr.sem, 1)

            def ffn_group(b, g, slot, dn, raw_n, uses):
                def gate_up(c):
                    n = (b * GRP + g) * NC + c
                    if c == 0:
                        pe.wait_ge(w_hi.sem, w_hi.done(raw_n))
                        pe.wait_ge(w_split.sem, w_split.done(raw_n))
                    pe.wait_ge(f_hid.sem, f_hid.free(n, 2))
                    for j in range(2):
                        mm = three_passes(ps[:, 2 * (c % 2) + j, 0:FG],
                                          lambda l, k: xnT[l][:, k, c * P:(c + 1) * P],
                                          lambda r, k: gu[slot][r][:, k, j * FG:(j + 1) * FG])
                    mm.then_inc(f_gu.sem, 1)

                def turn(c):
                    n = (b * GRP + g) * NC + c
                    pe.wait_ge(f_hid.sem, f_hid.done(n))
                    pe.wait_ge(f_hidT.sem, f_hidT.free(n, 2))
                    for t in range(DT):
                        mm = nc.tensor.transpose(ps[:, 4 + c % 2, t * P:(t + 1) * P], hid[:, c % 2, t * P:(t + 1) * P], ident8[:, 0:P])
                    mm.then_inc(f_tr.sem, 1)

                def down(c):
                    n = (b * GRP + g) * NC + c
                    pe.wait_ge(f_hidT.sem, f_hidT.done(n))
                    pe.wait_ge(f_acc.sem, f_acc.free(n, 2))
                    for t in range(DT):
                        mm = nc.tensor.matmul(ps[:, 6 + c % 2, 0:DM], hidT[:, c % 2, t * P:(t + 1) * P], dn[:, slot, t, :],
                                              start=(t == 0), stop=(t == DT - 1))
                    mm.then_inc(f_dn.sem, 1)

                for c in range(NC + 2):
                    if c < NC:
                        gate_up(c)
                    if 1 <= c <= NC:
                        turn(c - 1)
                    if c >= 2:
                        if c == 2:
                            uses()
                        down(c - 2)

            def out_proj(b, layer, extra):
                with pe.Fori(0, NC // 2) as j:
                    for s in range(2):
                        n = (b * 2 + layer) * NC + 2 * j + s
                        for q in range(4):
                            pe.wait_ge(o_yn.sem, o_yn.done(4 * n + q))
                            pe.wait_ge(o_yT.sem, o_yT.free(4 * n + q, 4))
                            for t in range(4):
                                mm = nc.tensor.transpose(ps[:, q, t * P:(t + 1) * P], yn[:, s, (4 * q + t) * P:(4 * q + t + 1) * P], ident8[:, 0:P])
                            mm.then_inc(o_tr.sem, 1)
                    for s in range(2):
                        n = (b * 2 + layer) * NC + 2 * j + s
                        pe.wait_ge(o_yT.sem, o_yT.done(4 * n + 3))
                        pe.wait_ge(o_sg.sem, o_sg.free(n, 2))
                        for t in range(NT):
                            mm = nc.tensor.matmul(ps[:, 4 + s, 0:DM], yT[:, s, t, :], w_out[:, t, :], start=(t == 0), stop=(t == NT - 1))
                        mm.then_inc(o_mm.sem, 1)
                    extra(j)

            pe.wait_ge(consts_in, 16 * CONSTS)
            with pe.Fori(0, B) as b:
                with pe.Fori(0, NC // 2) as j:
                    for s in range(2):
                        ln_transposes(b * 2 * NC + 2 * j + s, s)
                end_phase(pe, b, 0)

                for c in range(NC):
                    mm = three_passes(ps[:, 7, c * NE:(c + 1) * NE], lambda l, k: xnT[l][:, k, c * P:(c + 1) * P],
                                      lambda r, k: router[r][:, k, :])
                mm.then_inc(rt_logits.sem, 1)

                def loaded(slot, count):
                    return lambda: pe.wait_ge(dn_in[slot], 16 * count)
                pe.wait_ge(rt_dve.sem, rt_dve.done(b * 9))
                settle(pe)
                with pe.Fori(0, G0 // 2) as i:
                    for k in range(2):
                        ffn_group(b, 2 * i + k, k, dn_raw, b * RAWS + 2 * i + k, loaded(k, b * (4 - k) + i + 1))
                ffn_group(b, G0 - 1, 0, dn_raw, b * RAWS + G0 - 1, loaded(0, b * 4 + 3))
                end_phase(pe, b, 1)

                with pe.Fori(0, KVH) as i:
                    def proj(hf, t):
                        u = (b * KVH + i) * 2 + hf
                        r = u * (REP + 1) + t
                        if hf == 0 and t == 0:
                            pe.wait_ge(w_hi.sem, w_hi.done(b * RAWS + G0 + i))
                            pe.wait_ge(w_split.sem, w_split.done(b * RAWS + G0 + i))
                        if t == 1:
                            pe.wait_ge(a_vT.sem, a_vT.free(u, 1))
                        elif t == 0:
                            pe.wait_ge(a_mul.sem, a_mul.free(r, 1))
                        else:
                            pe.wait_ge(a_mul.sem, a_mul.free(r, 2))
                        three_passes(ps[:, t % 2, :], lambda l, k: w_qkv[l][:, k, t * P:(t + 1) * P],
                                     lambda r, k: xnT[r][:, k, hf * HALF:(hf + 1) * HALF]).then_inc(a_proj.sem, 1)

                    def kv_turn(hf):
                        u = (b * KVH + i) * 2 + hf
                        pe.wait_ge(a_qk.sem, a_qk.done(u * (REP + 1) + REP))
                        pe.wait_ge(a_kv.sem, a_kv.free(2 * u, 2))
                        for c in range(4):
                            mm = nc.tensor.transpose(ps[:, 7, c * P:(c + 1) * P], kT[:, (4 * hf + c) * P:(4 * hf + c + 1) * P], ident8[:, 0:P])
                        mm.then_inc(a_trk.sem, 1)
                        pe.wait_ge(a_vT.sem, a_vT.done(u))
                        pe.wait_ge(a_st.sem, a_st.done((b * KVH + i) * NC + 4 * hf - 1))
                        for c in range(4):
                            mm = nc.tensor.transpose(ps[:, 6, c * P:(c + 1) * P], vT[:, c * P:(c + 1) * P], ident8[:, 0:P])
                        mm.then_inc(a_trv.sem, 1)

                    def score(c):
                        u, m = (b * KVH + i) * 2 + c // 4, (b * KVH + i) * NC + c
                        if c % 4 == 0:
                            pe.wait_ge(a_qk.sem, a_qk.done(u * (REP + 1) + REP))
                        pe.wait_ge(a_mt.sem, a_mt.free(m, 2))
                        nc.tensor.matmul(ps[:, 2 + c % 2, :], kT[:, c * P:(c + 1) * P], qT[:, :, c * P:(c + 1) * P],
                                         start=True, stop=True).then_inc(a_sc.sem, 1)

                    def update(c):
                        u, m = (b * KVH + i) * 2 + c // 4, (b * KVH + i) * NC + c
                        pe.wait_ge(a_kv.sem, a_kv.done(2 * u + 1))
                        if c == NC - 1:
                            return
                        pe.wait_ge(a_st.sem, a_st.free(m, 1))
                        nc.tensor.matmul(ps[:, 6, 0:P + 1], k_tok[:, c, :], v_tok[:, c, :], start=True, stop=True).then_inc(a_up.sem, 1)

                    def numerator(c):
                        m = (b * KVH + i) * NC + c
                        pe.wait_ge(a_mt.sem, a_mt.done(m))
                        pe.wait_ge(a_st.sem, a_st.free(m, 1))
                        pe.wait_ge(a_out.sem, a_out.free(m, 1))
                        for h in range(REP):
                            out = ps[:, 4 + h // 2, (h % 2) * (P + 1):(h % 2 + 1) * (P + 1)]
                            nc.tensor.matmul(out, mt[:, c % 2, h * P:(h + 1) * P], v_tok[:, c, :], start=True, stop=False)
                            mm = nc.tensor.matmul(out, qT[:, h, c * P:(c + 1) * P], att_state[:, c % 2, :], start=False, stop=True)
                        mm.then_inc(a_nd.sem, 1)

                    for t in range(REP + 2):
                        proj(0, t)
                    kv_turn(0)
                    score(0)
                    for c in range(NC):
                        if c < 3:
                            proj(1, 2 * c)
                            proj(1, 2 * c + 1)
                        if c >= 4 and c < NC - 1:
                            score(c + 1)
                        update(c)
                        numerator(c)
                        if c < 3:
                            score(c + 1)
                        if c == 3:
                            kv_turn(1)
                            score(4)
                end_phase(pe, b, 2)

                pe.wait_ge(w_out_in, 16 * (2 * b + 1))

                settle(pe)

                def next_ln(j):
                    for s in range(2):
                        ln_transposes((b * 2 + 1) * NC + 2 * j + s, s)
                out_proj(b, 0, next_ln)
                end_phase(pe, b, 3)

                def made(k):
                    return lambda: pe.wait_ge(dn_made.sem, dn_made.done(b * G1 + k))
                for k in range(G1):
                    ffn_group(b, G0 + k, k, dn_f, b * RAWS + G0 + KVH + k, made(k))
                end_phase(pe, b, 4)

                for hf in range(2):
                    mm = three_passes(ps[:, hf, :], lambda l, k: w_dec[l][:, k, :],
                                      lambda r, k: xnT[r][:, k, hf * HALF:(hf + 1) * HALF])
                mm.then_inc(s_loga.sem, 1)
                pe.wait_ge(s_dec.sem, s_dec.done(b))
                pe.wait_ge(own_pool, b + 1)
                settle(pe)
                with pe.Fori(0, HP // 2) as i:
                    for w in range(2):
                        n = b * HP + 2 * i + w
                        raw_n = b * RAWS + G0 + KVH + G1 + 2 * i + w

                        def proj_bc(hf):
                            u = n * 2 + hf
                            if hf == 0:
                                pe.wait_ge(w_hi.sem, w_hi.done(raw_n))
                                pe.wait_ge(w_split.sem, w_split.done(raw_n))
                            pe.wait_ge(s_b.sem, s_b.free(u, 1))
                            three_passes(ps[:, 0, :], lambda l, k: w_in[w][l][:, k, 2 * P:3 * P],
                                         lambda r, k: xnT[r][:, k, hf * HALF:(hf + 1) * HALF]).then_inc(s_pb.sem, 1)
                            pe.wait_ge(s_cp.sem, s_cp.free(u, 1))
                            three_passes(ps[:, 1, :], lambda l, k: w_in[w][l][:, k, 3 * P:4 * P],
                                         lambda r, k: xnT[r][:, k, hf * HALF:(hf + 1) * HALF]).then_inc(s_pc.sem, 1)

                        def b_turn(hf):
                            u = n * 2 + hf
                            pe.wait_ge(s_b.sem, s_b.done(u))
                            pe.wait_ge(s_st.sem, s_st.done(n * NC + 4 * hf - 1))
                            for c in range(4):
                                mm = nc.tensor.transpose(ps[:, 7, c * P:(c + 1) * P], bT[:, (4 * hf + c) * P:(4 * hf + c + 1) * P], ident8[:, 0:P])
                            mm.then_inc(s_trb.sem, 1)

                        def proj_xz(c):
                            m = n * NC + c
                            pe.wait_ge(s_xw.sem, s_xw.free(m, 2))
                            mm = three_passes(ps[:, 2 + c % 2, 0:2 * P], lambda l, k: xnT[l][:, k, c * P:(c + 1) * P],
                                              lambda r, k: w_in[w][r][:, k, 0:2 * P])
                            mm.then_inc(s_xz.sem, 1)

                        def score(c):
                            u, m = n * 2 + c // 4, n * NC + c
                            pe.wait_ge(s_c.sem, s_c.done(u))
                            pe.wait_ge(s_b.sem, s_b.done(u))
                            pe.wait_ge(s_mt.sem, s_mt.free(m, 2))
                            nc.tensor.matmul(ps[:, 4 + c % 2, 0:2 * P], bT[:, c * P:(c + 1) * P], cTz[:, :, c * P:(c + 1) * P],
                                             start=True, stop=True).then_inc(s_sc.sem, 1)

                        def update(c):
                            u, m = n * 2 + c // 4, n * NC + c
                            pe.wait_ge(s_btok.sem, s_btok.done(u))
                            if c == NC - 1:
                                return
                            pe.wait_ge(s_xw.sem, s_xw.done(m))
                            pe.wait_ge(s_st.sem, s_st.free(m, 1))
                            nc.tensor.matmul(ps[:, 7, 0:P], b_tok[:, c, :], xw[:, c % 2, :], start=True, stop=True).then_inc(s_up.sem, 1)

                        def outputs(c):
                            u, m = n * 2 + c // 4, n * NC + c
                            out = ps[:, 6, 0:P]
                            pe.wait_ge(s_mt.sem, s_mt.done(m))
                            pe.wait_ge(s_xcopy.sem, s_xcopy.done(m))
                            pe.wait_ge(s_cp.sem, s_cp.done(u))
                            pe.wait_ge(s_st.sem, s_st.free(m, 1))
                            pe.wait_ge(s_yg.sem, s_yg.free(m, 1))
                            for h in range(2):
                                nc.tensor.matmul(out, mt1[:, c % 2, h * P:(h + 1) * P], xz_x[:, c % 2, h * P:(h + 1) * P],
                                                 start=(h == 0), stop=False)
                            nc.tensor.matmul(out, cTp[:, c * P:(c + 1) * P], ssm_state[:, c % 2, :], start=False, stop=True).then_inc(s_y.sem, 1)

                        proj_bc(0)
                        proj_xz(0)
                        score(0)
                        b_turn(0)
                        for c in range(NC):
                            if c < NC - 1:
                                proj_xz(c + 1)
                                if c != 3:
                                    score(c + 1)
                            update(c)
                            outputs(c)
                            if c == 0:
                                proj_bc(1)
                            if c == 3:
                                b_turn(1)
                                score(4)
                end_phase(pe, b, 5)

                pe.wait_ge(w_out_in, 16 * (2 * b + 2))
                settle(pe)
                out_proj(b, 1, lambda j: None)
                end_phase(pe, b, 6)

        @block.scalar
        def _(act):
            start(act, "act")

            def split_hi(n, hi, raw):
                nc.scalar.activation(hi, raw, ACT.Copy).then_inc(w_hi.sem, 1)

            def ln_std_of(n, s):
                act.wait_ge(ln_var.sem, ln_var.done(n))
                act.wait_ge(ln_rstd.sem, ln_rstd.free(n, 2))
                nc.scalar.activation(ln_sd[:, s, :], ln_mv[:, s, 1:2], ACT.Sqrt, bias=ln_eps[:, 0:1]).then_inc(ln_std.sem, 1)

            def ln_hi_of(n, c, s):
                act.wait_ge(ln_tr.sem, ln_tr.done(n))
                nc.scalar.activation(xnT[0][:, :, bass.ds(c * P, P)], ps[:, 6 + s, 0:DM].rearrange("p (k c) -> p k c", k=KT),
                                     ACT.Copy).then_inc(ln_hi.sem, 1)

            def ffn_group(b, g, slot, prep):
                for c in range(NC + 1):
                    if c < NC:
                        n = (b * GRP + g) * NC + c
                        act.wait_ge(f_gu.sem, f_gu.done(n))
                        act.wait_ge(f_hid.sem, f_hid.free(n, 2))
                        nc.scalar.activation(silu_g[:, c % 2], ps[:, 2 * (c % 2), 0:FG], ACT.Silu).then_inc(f_silu.sem, 1)
                    if c >= 1:
                        n = (b * GRP + g) * NC + c - 1
                        act.wait_ge(f_tr.sem, f_tr.done(n))
                        act.wait_ge(f_dn.sem, f_dn.free(n, 2))
                        nc.scalar.activation(hidT[:, (c - 1) % 2], ps[:, 4 + (c - 1) % 2, 0:DT * P], ACT.Copy).then_inc(f_hidT.sem, 1)
                    if c == 3:
                        prep()

            def gate_silu(b, g):
                act.wait_ge(f_acc.sem, f_acc.done((b * GRP + g) * NC + NC - 1))
                nc.scalar.activation(gate[:], gate[:], ACT.Silu)

            def out_proj(b, layer, extra):
                with act.Fori(0, NC // 2) as j:
                    if layer == 1:
                        for s in range(2):
                            n = b * NC + 2 * j + s
                            act.wait_ge(o_stat.sem, o_stat.done(n))
                            nc.scalar.activation(in_sd[:, s, :], in_mv[:, s, 1:2], ACT.Sqrt, bias=ln_eps[:, 0:1]).then_inc(o_std.sem, 1)
                    for s in range(2):
                        n = (b * 2 + layer) * NC + 2 * j + s
                        act.wait_ge(o_mm.sem, o_mm.free(n, 2))
                        for q in range(4):
                            act.wait_ge(o_tr.sem, o_tr.done(4 * n + q))
                            if layer == 0:
                                nc.scalar.activation(yT[:, s, 4 * q:4 * q + 4, :].rearrange("p t c -> p (t c)"), ps[:, q, :],
                                                     ACT.Copy).then_inc(o_yT.sem, 1)
                                continue
                            for t in range(4):
                                k = 4 * q + t
                                ins = nc.scalar.activation(yT[:, s, k, :], ps[:, q, t * P:(t + 1) * P], ACT.Identity,
                                                           bias=beta[:, k:k + 1], scale=gamma[:, k:k + 1])
                            ins.then_inc(o_yT.sem, 1)
                    extra(j)

            act.wait_ge(consts_in, 16 * CONSTS)
            nc.scalar.activation(router[0][:].rearrange("p k c -> p (k c)"), x_res[:, 0, 0:KT * NE], ACT.Copy)
            nc.scalar.activation(w_dec[0][:].rearrange("p k c -> p (k c)"), x_res[:, 1, :], ACT.Copy).then_inc(init_step, 1)
            with act.Fori(0, B) as b:
                def ln_pair(j, base):
                    for s in range(2):
                        ln_std_of(base + 2 * j + s, s)
                    for s in range(2):
                        ln_hi_of(base + 2 * j + s, 2 * j + s, s)
                with act.Fori(0, NC // 2) as j:
                    ln_pair(j, b * 2 * NC)
                end_phase(act, b, 0)

                raw = w_raw[:, 0:KT * 2 * FG].rearrange("p (k c) -> p k c", k=KT)

                def prep0(g, slot):
                    def do():
                        act.wait_ge(w_raw_in, 16 * (b * RAWS + g + 1))
                        act.wait_ge(f_gu.sem, f_gu.done((b * GRP + g - 2) * NC + NC - 1))
                        split_hi(b * RAWS + g, gu[slot][0][:], raw)
                    return do
                prep0(0, 0)()
                act.wait_ge(rt_dve.sem, rt_dve.done(b * 9 + 2))
                nc.scalar.activation(rt_l[:], rt_l[:], ACT.Exp).then_inc(rt_exp.sem, 1)
                with act.Fori(0, G0 // 2) as i:
                    ffn_group(b, 2 * i, 0, prep0(2 * i + 1, 1))
                    ffn_group(b, 2 * i + 1, 1, prep0(2 * i + 2, 0))
                ffn_group(b, G0 - 1, 0, lambda: None)
                gate_silu(b, G0 - 1)
                end_phase(act, b, 1)

                with act.Fori(0, KVH) as i:
                    def w_prep(idx):
                        act.wait_ge(w_raw_in, 16 * (b * RAWS + G0 + idx + 1))
                        act.wait_ge(a_proj.sem, a_proj.free((b * KVH + idx) * 12 + 11, 12))
                        split_hi(0, w_qkv[0][:], w_raw[:].rearrange("p (k c) -> p k c", k=KT))

                    def rope_act(hf, t):
                        r = ((b * KVH + i) * 2 + hf) * (REP + 1) + t
                        k = (hf * (REP + 1) + t) % 2
                        act.wait_ge(a_rot.sem, a_rot.done(r))
                        nc.scalar.activation(ra[:, k], rb[:, k], ACT.Relu, scale=-1.0).then_inc(a_neg.sem, 1)
                        act.wait_ge(a_neg.sem, a_neg.done(r))
                        nc.scalar.activation(ra[:, k], ra[:, k], ACT.Exp, scale=-1.0).then_inc(a_act.sem, 1)

                    def v_copy(hf):
                        u = (b * KVH + i) * 2 + hf
                        act.wait_ge(a_proj.sem, a_proj.done(u * 6 + 5))
                        act.wait_ge(a_trv.sem, a_trv.free(u, 1))
                        nc.scalar.activation(vT[:], ps[:, 1, :], ACT.Copy).then_inc(a_vT.sem, 1)

                    def kv_copy(hf):
                        u = (b * KVH + i) * 2 + hf
                        m = (b * KVH + i) * NC + 4 * hf + 3
                        act.wait_ge(a_trk.sem, a_trk.done(u))
                        act.wait_ge(a_nd.sem, a_nd.free(m, 8))
                        nc.scalar.activation(k_tok[:, 4 * hf:4 * hf + 4, :], ps[:, 7, :].rearrange("p (c e) -> p c e", e=P), ACT.Copy).then_inc(a_kv.sem, 1)
                        act.wait_ge(a_trv.sem, a_trv.done(u))
                        nc.scalar.activation(v_tok[:, 4 * hf:4 * hf + 4, 0:P], ps[:, 6, :].rearrange("p (c e) -> p c e", e=P), ACT.Copy).then_inc(a_kv.sem, 1)

                    def out_copy(c):
                        m = (b * KVH + i) * NC + c
                        act.wait_ge(a_nd.sem, a_nd.done(m))
                        nd = ps[:, 4:6, 0:2 * (P + 1)].rearrange("p b (h e) -> p b h e", e=P + 1)
                        nc.scalar.activation(y[:, c, bass.ds(i * REP * P, REP * P)].rearrange("p (b h e) -> p b h e", b=2, h=2),
                                             nd[:, :, :, 0:P], ACT.Copy)
                        nc.scalar.activation(den[:, c, bass.ds(i * REP, REP)].rearrange("p (b h) -> p b h", b=2),
                                             nd[:, :, :, P], ACT.Copy).then_inc(a_out.sem, 1)

                    w_prep(i)
                    for t in range(REP + 1):
                        rope_act(0, t)
                    v_copy(0)
                    kv_copy(0)
                    for c in range(NC):
                        if 1 <= c < 3:
                            rope_act(1, 2 * c - 2)
                            rope_act(1, 2 * c - 1)
                        if c == 3:
                            rope_act(1, 4)
                            v_copy(1)
                        out_copy(c)
                        if c == 3:
                            kv_copy(1)
                end_phase(act, b, 2)

                out_proj(b, 0, lambda j: ln_pair(j, (b * 2 + 1) * NC))
                end_phase(act, b, 3)

                def prep1(k):
                    def do():
                        act.wait_ge(f_wf.sem, f_wf.done(b * G1 + k))
                        split_hi(0, gu[k][0][:], gu_f[:])
                    return do
                prep1(0)()
                ffn_group(b, G0, 0, prep1(1))
                ffn_group(b, G0 + 1, 1, lambda: None)
                gate_silu(b, GRP - 1)
                end_phase(act, b, 4)

                act.wait_ge(s_loga.sem, s_loga.done(b))
                nc.scalar.activation(dec_e[:].rearrange("p (h c) -> p h c", h=2), ps[0:SH, 0:2, :], ACT.Exp).then_inc(own_act, 1)
                act.wait_ge(own_act, b + 1)
                nc.scalar.activation(dec_t[:], dec_e[:], ACT.Exp, scale=-1.0).then_inc(s_dec.sem, 1)
                act.wait_ge(dec_out, 16 * (b + 1))
                act.wait_ge(own_pool, b + 1)

                with act.Fori(0, HP // 2) as i:
                    for w in range(2):
                        n = b * HP + 2 * i + w

                        def b_copy(hf):
                            u, m = n * 2 + hf, n * NC + 4 * hf + 3
                            act.wait_ge(s_pb.sem, s_pb.done(u))
                            act.wait_ge(s_sc.sem, s_sc.free(m, 8))
                            nc.scalar.activation(bT[:, hf * HALF:(hf + 1) * HALF], ps[:, 0, :], ACT.Copy).then_inc(s_b.sem, 1)
                            act.wait_ge(s_pc.sem, s_pc.done(u))
                            nc.scalar.activation(cTz[0:64, 0, hf * HALF:(hf + 1) * HALF], ps[0:64, 1, :], ACT.Copy)
                            nc.scalar.activation(cTz[64:P, 1, hf * HALF:(hf + 1) * HALF], ps[64:P, 1, :], ACT.Copy).then_inc(s_c.sem, 1)

                        def btok_copy(hf):
                            u, m = n * 2 + hf, n * NC + 4 * hf + 3
                            act.wait_ge(s_trb.sem, s_trb.done(u))
                            act.wait_ge(s_y.sem, s_y.free(m, 8))
                            nc.scalar.activation(b_tok[:, 4 * hf:4 * hf + 4, :], ps[:, 7, :].rearrange("p (c e) -> p c e", e=P), ACT.Copy).then_inc(s_btok.sem, 1)

                        def xz_copy(c):
                            m = n * NC + c
                            s = c % 2
                            act.wait_ge(s_xz.sem, s_xz.done(m))
                            act.wait_ge(s_y.sem, s_y.free(m, 2))
                            act.wait_ge(s_xd.sem, s_xd.free(m, 2))
                            act.wait_ge(s_out.sem, s_out.free(m, 2))
                            nc.scalar.activation(xz_x[:, s, :].rearrange("p (h c) -> p h c", c=64)[:, 0:4:3, :],
                                                 ps[:, 2 + s, 0:P].rearrange("p (h c) -> p h c", c=64), ACT.Copy)
                            nc.scalar.activation(sz[:, s, :], ps[:, 2 + s, P:2 * P], ACT.Silu).then_inc(s_xcopy.sem, 1)

                        act.wait_ge(w_raw_in, 16 * (b * RAWS + G0 + KVH + G1 + 2 * i + w + 1))
                        act.wait_ge(s_xz.sem, s_xz.free(n * NC + NC - 1, 2 * NC))
                        split_hi(0, w_in[w][0][:], w_raw[:, 0:KT * XZBC].rearrange("p (k c) -> p k c", k=KT))
                        b_copy(0)
                        xz_copy(0)
                        btok_copy(0)
                        for c in range(NC):
                            if c < NC - 1:
                                xz_copy(c + 1)
                            if c == 1:
                                b_copy(1)
                            if c == 3:
                                btok_copy(1)
                end_phase(act, b, 5)
                out_proj(b, 1, lambda j: None)
                end_phase(act, b, 6)

        @block.vector
        def _(dve):
            start(dve, "dve")

            def ln_stats(n, c, s):
                dve.wait_ge(ln_rstd.sem, ln_rstd.free(n, 2))
                settle(dve)
                nc.vector.bn_stats(ln_st[:, s, :], x_res[:, bass.ds(c, 1), :].rearrange("p a d -> p (a d)")).then_inc(ln_stat.sem, 1)
                dve.wait_ge(ln_stat.sem, ln_stat.done(n))
                dve.wait_ge(ln_xn.sem, ln_xn.free(n, 2))
                settle(dve)
                nc.vector.bn_aggr(ln_mv[:, s, :], ln_st[:, s, :]).then_inc(ln_var.sem, 1)

            def ln_norm(n, c, s):
                dve.wait_ge(ln_std.sem, ln_std.done(n))
                nc.vector.reciprocal(ln_rs[:, s, :], ln_sd[:, s, :]).then_inc(ln_rstd.sem, 1)
                dve.wait_ge(ln_rstd.sem, ln_rstd.done(n))
                dve.wait_ge(ln_var.sem, ln_var.done(n))
                dve.wait_ge(ln_tr.sem, ln_tr.free(n, 2))
                nc.vector.tensor_scalar(xn[:, s, :], x_res[:, bass.ds(c, 1), :].rearrange("p a d -> p (a d)"),
                                        ln_mv[:, s, 0:1], ln_rs[:, s, :], ALU.subtract, ALU.mult).then_inc(ln_xn.sem, 1)

            def ln_low(n, c, s):
                dve.wait_ge(ln_hi.sem, ln_hi.done(n))
                nc.vector.tensor_tensor(xnT[1][:, :, bass.ds(c * P, P)], ps[:, 6 + s, 0:DM].rearrange("p (k c) -> p k c", k=KT),
                                        xnT[0][:, :, bass.ds(c * P, P)], ALU.subtract).then_inc(ln_lo.sem, 1)

            def ln_pair(j, base):
                for s in range(2):
                    ln_stats(base + 2 * j + s, 2 * j + s, s)
                for s in range(2):
                    ln_norm(base + 2 * j + s, 2 * j + s, s)
                for s in range(2):
                    ln_low(base + 2 * j + s, 2 * j + s, s)

            def ffn_group(b, g, slot, experts, prep):
                for c in range(NC + 2):
                    if c < NC:
                        n = (b * GRP + g) * NC + c
                        if c == 0 and experts:
                            if slot is not None:
                                dve.wait_ge(f_hid.sem, f_hid.free(n, 1))
                            nc.vector.tensor_copy(combine_g[:, slot], combine[:, bass.ds(2 * g, 2), :]).then_inc(f_cg.sem, 1)
                            dve.wait_ge(f_cg.sem, f_cg.done(b * G0 + g))
                        dve.wait_ge(f_silu.sem, f_silu.done(n))
                        dve.wait_ge(f_tr.sem, f_tr.free(n, 2))
                        up = ps[:, 2 * (c % 2) + 1, :]
                        if experts:
                            for e in range(2):
                                ins = nc.vector.scalar_tensor_tensor(
                                    hid[:, c % 2, e * FE:(e + 1) * FE], up[:, e * FE:(e + 1) * FE], combine_g[:, slot, e, c:c + 1],
                                    silu_g[:, c % 2, e * FE:(e + 1) * FE], ALU.mult, ALU.mult)
                        else:
                            ins = nc.vector.tensor_tensor(hid[:, c % 2, 0:FG], up[:, 0:FG], silu_g[:, c % 2, :], ALU.mult)
                        ins.then_inc(f_hid.sem, 1)
                    if c >= 2:
                        n = (b * GRP + g) * NC + c - 2
                        dve.wait_ge(f_dn.sem, f_dn.done(n))
                        dve.wait_ge(f_acc.sem, f_acc.free(n, 8))
                        nc.vector.tensor_tensor(gate[:, c - 2, :], ps[:, 6 + c % 2, 0:DM], gate[:, c - 2, :], ALU.add).then_inc(f_acc.sem, 1)
                    if c == 3:
                        prep()

            def add_gated(n, c, s):
                dve.wait_ge(o_mm.sem, o_mm.done(n))
                dve.wait_ge(o_res.sem, o_res.free(n, 2))
                nc.vector.tensor_tensor(sg[:, s], ps[:, 4 + s, 0:DM], gate[:, bass.ds(c, 1), :].rearrange("p a d -> p (a d)"), ALU.mult).then_inc(o_sg.sem, 1)
                dve.wait_ge(o_sg.sem, o_sg.done(n))
                xc = x_res[:, bass.ds(c, 1), :].rearrange("p a d -> p (a d)")
                nc.vector.tensor_tensor(xc, sg[:, s], xc, ALU.add).then_inc(o_res.sem, 1)

            nc.vector.memset(ln_eps[:], LN_EPS)
            nc.vector.memset(att_state[:], 0.0)
            nc.vector.memset(ssm_state[:], 0.0)
            nc.vector.memset(combine[:, NE:2 * G0, :], 1.0)
            dve.wait_ge(init_step, 1)
            nc.vector.tensor_tensor(router[1][:].rearrange("p k c -> p (k c)"), x_res[:, 0, 0:KT * NE], router[0][:].rearrange("p k c -> p (k c)"), ALU.subtract)
            nc.vector.tensor_tensor(w_dec[1][:].rearrange("p k c -> p (k c)"), x_res[:, 1, :], w_dec[0][:].rearrange("p k c -> p (k c)"), ALU.subtract).then_inc(init_step, 1)
            with dve.Fori(0, B) as b:
                dve.wait_ge(x_in, 16 * (b + 1))
                settle(dve)
                with dve.Fori(0, NC // 2) as j:
                    ln_pair(j, b * 2 * NC)
                end_phase(dve, b, 0)

                r0 = b * 9

                def routed(k, ins):
                    ins.then_inc(rt_dve.sem, 1)
                    dve.wait_ge(rt_dve.sem, rt_dve.done(r0 + k))
                dve.wait_ge(rt_logits.sem, rt_logits.done(b))
                routed(0, nc.vector.tensor_copy(rt_l[:].rearrange("p c e -> p (c e)"), ps[:, 7, 0:NC * NE]))
                routed(1, nc.vector.tensor_reduce(rt_m[:], rt_l[:], AX.X, ALU.max))
                nc.vector.tensor_tensor(rt_l[:], rt_l[:], rt_m[:].unsqueeze(2).broadcast_to([P, NC, NE]), ALU.subtract).then_inc(rt_dve.sem, 1)
                dve.wait_ge(rt_exp.sem, rt_exp.done(b))
                routed(3, nc.vector.tensor_reduce(rt_s[:], rt_l[:], AX.X, ALU.add))
                routed(4, nc.vector.reciprocal(rt_m[:], rt_s[:]))
                routed(5, nc.vector.tensor_tensor(rt_l[:], rt_l[:], rt_m[:].unsqueeze(2).broadcast_to([P, NC, NE]), ALU.mult))
                rival = rt_l[:].unsqueeze(2).broadcast_to([P, NC, NE, NE])
                score = rt_l[:].unsqueeze(3).broadcast_to([P, NC, NE, NE])
                nc.vector.tensor_tensor(rt_gt[:].rearrange("p (c e) j -> p c e j", c=NC), rival, score, ALU.is_gt)
                routed(6, nc.vector.tensor_tensor(rt_eq[:].rearrange("p (c e) j -> p c e j", c=NC), rival, score, ALU.is_equal))
                first = earlier[:].rearrange("p (e j) -> p e j", e=NE).unsqueeze(1).broadcast_to([P, NC, NE, NE])
                routed(7, nc.vector.tensor_tensor(rt_eq[:].rearrange("p (c e) j -> p c e j", c=NC), rt_eq[:].rearrange("p (c e) j -> p c e j", c=NC), first, ALU.mult))
                routed(8, nc.vector.tensor_tensor(rt_gt[:], rt_gt[:], rt_eq[:], ALU.add))
                nc.vector.tensor_reduce(rt_rank[:], rt_gt[:], AX.X, ALU.add).then_inc(own_dve, 1)
                dve.wait_ge(own_dve, 2 * b + 1)
                nc.vector.scalar_tensor_tensor(combine[:, 0:NE, :].rearrange("p e c -> p c e"), rt_rank[:].rearrange("p (c e) -> p c e", c=NC), 1.5,
                                               rt_l[:], ALU.is_lt, ALU.mult).then_inc(own_dve, 1)
                dve.wait_ge(own_dve, 2 * b + 2)
                dve.wait_ge(gate_zero.sem, gate_zero.done(2 * b))
                settle(dve)

                with dve.Fori(0, G0 // 2) as i:
                    for k in range(2):
                        ffn_group(b, 2 * i + k, k, True, lambda: None)
                ffn_group(b, G0 - 1, 0, True, lambda: None)
                end_phase(dve, b, 1)

                dve.wait_ge(tables_in, 32 * (b + 1))
                settle(dve)
                with dve.Fori(0, KVH) as i:
                    def rope_mul(hf, t):
                        u = (b * KVH + i) * 2 + hf
                        r = u * (REP + 1) + t
                        k = (hf * (REP + 1) + t) % 2
                        toks = slice(hf * HALF, (hf + 1) * HALF)
                        dve.wait_ge(a_proj.sem, a_proj.done(u * 6 + t))
                        dve.wait_ge(a_qk.sem, a_qk.free(r, 2))
                        nc.vector.tensor_tensor(ra[:, k], ps[:, t % 2, :], cos[:, toks], ALU.mult)
                        nc.vector.tensor_tensor(rb[0:64, k], ps[64:P, t % 2, :], sin[0:64, toks], ALU.mult)
                        nc.vector.tensor_tensor(rb[64:P, k], ps[0:64, t % 2, :], sin[64:P, toks], ALU.mult).then_inc(a_mul.sem, 1)

                    def feature(hf, t):
                        u = (b * KVH + i) * 2 + hf
                        r = u * (REP + 1) + t
                        k = (hf * (REP + 1) + t) % 2
                        toks = slice(hf * HALF, (hf + 1) * HALF)
                        if t == 0:
                            m = (b * KVH + i) * NC + 4 * hf + 3
                            dve.wait_ge(a_nd.sem, a_nd.free(m, 8))
                        dve.wait_ge(a_act.sem, a_act.done(r))
                        dst = qT[:, t, toks] if t < REP else kT[:, toks]
                        nc.vector.scalar_tensor_tensor(dst, rb[:, k], 0.0, ra[:, k], ALU.max, ALU.add).then_inc(a_qk.sem, 1)

                    def mask(c):
                        m = (b * KVH + i) * NC + c
                        dve.wait_ge(a_sc.sem, a_sc.done(m))
                        dve.wait_ge(a_nd.sem, a_nd.free(m, 2))
                        nc.vector.tensor_tensor(mt[:, c % 2], ps[:, 2 + c % 2, :], causal4[:], ALU.mult).then_inc(a_mt.sem, 1)

                    def state(c):
                        m = (b * KVH + i) * NC + c
                        nxt = att_state[:, (c + 1) % 2, :]
                        if c == NC - 1:
                            dve.wait_ge(a_nd.sem, a_nd.free(m, 1))
                            dve.wait_ge(a_st.sem, a_st.free(m, 1))
                            nc.vector.memset(nxt, 0.0).then_inc(a_st.sem, 1)
                            return
                        dve.wait_ge(a_up.sem, a_up.done((b * KVH + i) * (NC - 1) + c))
                        dve.wait_ge(a_nd.sem, a_nd.free(m, 1))
                        dve.wait_ge(a_st.sem, a_st.free(m, 1))
                        nc.vector.tensor_tensor(nxt, ps[:, 6, 0:P + 1], att_state[:, c % 2, :], ALU.add).then_inc(a_st.sem, 1)

                    rope_mul(0, 0)
                    for t in range(1, REP + 1):
                        rope_mul(0, t)
                        feature(0, t - 1)
                    feature(0, REP)
                    mask(0)
                    for c in range(NC):
                        if c < 3:
                            rope_mul(1, 2 * c)
                            if c > 0:
                                feature(1, 2 * c - 1)
                            if c < 2:
                                rope_mul(1, 2 * c + 1)
                            feature(1, 2 * c)
                        if c >= 4 and c < NC - 1:
                            mask(c + 1)
                        state(c)
                        if c < 4:
                            mask(c + 1)
                end_phase(dve, b, 2)

                with dve.Fori(0, NC // 2) as j:
                    for s in range(2):
                        c = 2 * j + s
                        n = b * 2 * NC + c
                        dve.wait_ge(o_yn.sem, o_yn.free(4 * n, 8) + 3)
                        nc.vector.tensor_scalar(rin[:, s, :], den[:, bass.ds(c, 1), :].rearrange("p a d -> p (a d)"), DEN_EPS, None, ALU.add).then_inc(rin_step, 1)
                        dve.wait_ge(rin_step, 2 * (b * NC + c) + 1)
                        nc.vector.reciprocal(rin2[:, s, :], rin[:, s, :]).then_inc(rin_step, 1)
                        dve.wait_ge(rin_step, 2 * (b * NC + c) + 2)
                        for q in range(4):
                            dve.wait_ge(o_tr.sem, o_tr.free(4 * n + q, 8))
                            nc.vector.tensor_tensor(yn[:, s, q * HALF:(q + 1) * HALF].rearrange("p (h e) -> p h e", e=P),
                                                    y[:, bass.ds(c, 1), q * HALF:(q + 1) * HALF].rearrange("p a (h e) -> p (a h) e", e=P),
                                                    rin2[:, s, 4 * q:4 * q + 4].unsqueeze(2).broadcast_to([P, 4, P]), ALU.mult).then_inc(o_yn.sem, 1)
                    for s in range(2):
                        add_gated(b * 2 * NC + 2 * j + s, 2 * j + s, s)
                    dve.wait_ge(o_res.sem, o_res.done(b * 2 * NC + 2 * j + 1))
                    ln_pair(j, (b * 2 + 1) * NC)
                end_phase(dve, b, 3)

                def dequant(k):
                    def do():
                        if k == 0:
                            dve.wait_ge(scales_in, 48 * (b + 1))
                        dve.wait_ge(w_raw_in, 16 * (b * RAWS + G0 + KVH + k + 1))
                        dve.wait_ge(w_split.sem, w_split.free(b * RAWS + G0 + KVH + k, 1))
                        for kk in range(KT):
                            ins = nc.vector.scalar_tensor_tensor(
                                gu_f[:, kk], w_raw[:, kk * 2 * FG:(kk + 1) * 2 * FG].bitcast(I32), ZERO_POINT,
                                s_gu[:, k], ALU.subtract, ALU.mult)
                        ins.then_inc(f_wf.sem, 1)
                        dve.wait_ge(dn_in[k], 16 * (b * (4 - k) + 4 - k))
                        nc.vector.scalar_tensor_tensor(dn_f[:, k], dn_raw[:, k].bitcast(I32), ZERO_POINT,
                                                       s_dn[:].unsqueeze(1).broadcast_to([P, DT, DM]), ALU.subtract, ALU.mult).then_inc(dn_made.sem, 1)
                    return do
                dequant(0)()
                dve.wait_ge(gate_zero.sem, gate_zero.done(2 * b + 1))
                ffn_group(b, G0, 0, False, dequant(1))
                ffn_group(b, G0 + 1, 1, False, lambda: None)
                end_phase(dve, b, 4)

                dve.wait_ge(s_dec.sem, s_dec.done(b))
                dve.wait_ge(own_pool, b + 1)
                settle(dve)
                with dve.Fori(0, HP // 2) as i:
                    for w in range(2):
                        n = b * HP + 2 * i + w
                        dve.wait_ge(dec_in, 16 * (n + 1))
                        dve.wait_ge(s_mt.sem, s_mt.free(n * NC, 1))
                        dve.wait_ge(s_st.sem, s_st.free(n * NC, 1))
                        dve.wait_ge(s_xw.sem, s_xw.free(n * NC, 1))
                        dve.wait_ge(s_cp.sem, s_cp.free(n * 2, 1))
                        for h in range(2):
                            q = slice(64 * h, 64 * h + 64)
                            ins = nc.vector.tensor_copy(dstart[q, :].rearrange("p (c t) -> p c t", t=P)[:, :, 0],
                                                        dec[q, h, :].rearrange("p (c t) -> p c t", t=P)[:, :, 0])
                        ins.then_inc(s_prep, 1)
                        dve.wait_ge(s_prep, 2 * n + 1)
                        nc.vector.memset(dec[:].rearrange("p h (c t) -> p (h c) t", t=P)[:, :, 0:1], 0.0).then_inc(s_prep, 1)
                        dve.wait_ge(s_prep, 2 * n + 2)
                        for h in range(2):
                            nc.vector.tensor_tensor_scan(lmat[:, h, :], dec[:, h, :], ident8[:], 0.0, ALU.mult, ALU.add)
                        for h in range(2):
                            q = slice(64 * h, 64 * h + 64)
                            ins = nc.vector.tensor_tensor_scan(pdec[q, :], dec[q, h, :], dstart[q, :], 0.0, ALU.mult, ALU.add)
                        ins.then_inc(s_scan.sem, 1)
                        dve.wait_ge(s_scan.sem, s_scan.done(n))

                        def c_decayed(hf):
                            u, m = n * 2 + hf, n * NC + 4 * hf + 3
                            dve.wait_ge(s_c.sem, s_c.done(u))
                            dve.wait_ge(s_y.sem, s_y.free(m, 8))
                            toks = slice(hf * HALF, (hf + 1) * HALF)
                            nc.vector.tensor_tensor(cTp[:, toks], ps[:, 1, :], pdec[:, toks], ALU.mult).then_inc(s_cp.sem, 1)

                        def x_weighted(c):
                            m = n * NC + c
                            s = c % 2
                            dve.wait_ge(s_xcopy.sem, s_xcopy.done(m))
                            dve.wait_ge(s_y.sem, s_y.free(m, 2))
                            last = lmat[:, :, (c + 1) * P - 1:(c + 1) * P].broadcast_to([P, 2, 64])
                            nc.vector.tensor_tensor(xw[:, s].rearrange("p (h c) -> p h c", c=64), ps[:, 2 + s, 0:P].rearrange("p (h c) -> p h c", c=64),
                                                    last, ALU.mult).then_inc(s_xw.sem, 1)

                        def decayed_scores(c):
                            m = n * NC + c
                            s = c % 2
                            dve.wait_ge(s_sc.sem, s_sc.done(m))
                            dve.wait_ge(s_y.sem, s_y.free(m, 2))
                            nc.vector.tensor_tensor(mt1[:, s].rearrange("p (h c) -> p h c", h=2), ps[:, 4 + s, 0:2 * P].rearrange("p (h c) -> p h c", h=2),
                                                    lmat[:, :, c * P:(c + 1) * P], ALU.mult).then_inc(s_mt.sem, 1)

                        def state(c):
                            m = n * NC + c
                            nxt, cur = (c + 1) % 2, c % 2
                            dve.wait_ge(s_y.sem, s_y.free(m, 1))
                            dve.wait_ge(s_st.sem, s_st.free(m, 1))
                            if c == NC - 1:
                                nc.vector.memset(ssm_state[:, nxt, :], 0.0).then_inc(s_st.sem, 1)
                                return
                            dve.wait_ge(s_up.sem, s_up.done(n * (NC - 1) + c))
                            for h in range(2):
                                q = slice(64 * h, 64 * h + 64)
                                ins = nc.vector.scalar_tensor_tensor(ssm_state[q, nxt, q], ssm_state[q, cur, q], pdec[q, (c + 1) * P - 1:(c + 1) * P],
                                                                     ps[q, 7, q], ALU.mult, ALU.add)
                            ins.then_inc(s_st.sem, 1)

                        def add_skip(c):
                            m = n * NC + c
                            s = c % 2
                            dve.wait_ge(s_y.sem, s_y.done(m))
                            dve.wait_ge(s_xd.sem, s_xd.done(m))
                            dve.wait_ge(s_out.sem, s_out.free(m, 2))
                            nc.vector.tensor_tensor(yg[:, s], ps[:, 6, 0:P], xd[:, s], ALU.add).then_inc(s_yg.sem, 1)

                        c_decayed(0)
                        x_weighted(0)
                        decayed_scores(0)
                        for c in range(NC):
                            if c < NC - 1:
                                x_weighted(c + 1)
                                if c != 3:
                                    decayed_scores(c + 1)
                            state(c)
                            add_skip(c)
                            if c == 1:
                                c_decayed(1)
                            if c == 3:
                                decayed_scores(4)
                end_phase(dve, b, 5)

                with dve.Fori(0, NC // 2) as j:
                    for s in range(2):
                        c = 2 * j + s
                        n = b * NC + c
                        n4 = 4 * ((b * 2 + 1) * NC + c)
                        yc = y[:, bass.ds(c, 1), :].rearrange("p a d -> p (a d)")
                        dve.wait_ge(o_yn.sem, o_yn.free(n4, 8) + 3)
                        settle(dve)
                        for q in range(4):
                            ins = nc.vector.bn_stats(in_st[:, s, 6 * q:6 * q + 6], yc[:, q * HALF:(q + 1) * HALF])
                        ins.then_inc(rin_step2, 1)
                        dve.wait_ge(rin_step2, 2 * n + 1)
                        settle(dve)
                        nc.vector.bn_aggr(in_mv[:, s, :], in_st[:, s, :]).then_inc(o_stat.sem, 1)
                        dve.wait_ge(o_std.sem, o_std.done(n))
                        nc.vector.reciprocal(in_rs[:, s, :], in_sd[:, s, :]).then_inc(rin_step2, 1)
                        dve.wait_ge(rin_step2, 2 * n + 2)
                        for q in range(4):
                            dve.wait_ge(o_tr.sem, o_tr.free(n4 + q, 8))
                            nc.vector.tensor_scalar(yn[:, s, q * HALF:(q + 1) * HALF], yc[:, q * HALF:(q + 1) * HALF],
                                                    in_mv[:, s, 0:1], in_rs[:, s, :], ALU.subtract, ALU.mult).then_inc(o_yn.sem, 1)
                    for s in range(2):
                        add_gated((b * 2 + 1) * NC + 2 * j + s, 2 * j + s, s)
                end_phase(dve, b, 6)


def launch_arrays(inputs):
    f = {k: np.asarray(v) for k, v in inputs.items()}

    def rows_to_k(w):
        return np.ascontiguousarray(w.T).reshape(-1, P, w.shape[0]).transpose(1, 0, 2)

    g = {}
    g["x"] = f["L0_attn_x"]
    Wq, Wk, Wv = f["L0_attn_Wq"], f["L0_attn_Wk"], f["L0_attn_Wv"]
    g["w_qkv"] = np.stack([rows_to_k(np.concatenate([Wq[i * REP * P:(i + 1) * REP * P], Wk[i * P:(i + 1) * P], Wv[i * P:(i + 1) * P]])).reshape(P, -1)
                           for i in range(KVH)])
    g["w_o"] = rows_to_k(f["L0_attn_Wo"])
    g["router"] = np.concatenate([rows_to_k(f["L0_ffn_gate_weight"]).reshape(P, -1), np.zeros((P, DM - KT * NE), np.float32)], 1)

    def groups(gate_up, down):
        gus = np.stack([rows_to_k(x).reshape(P, -1) for x in gate_up])
        dns = np.stack([rows_to_k(np.concatenate([x, np.zeros((DM, DT * P - FG), x.dtype)], 1)).reshape(P, -1) for x in down])
        return gus, dns
    gw, dw = f["L0_ffn_gate_up_weights"], f["L0_ffn_down_weights"]
    sgu, sdn = f["L0_ffn_shared_gate_up"], f["L0_ffn_shared_down"]
    g["gu0"], g["dn0"] = groups(
        [np.concatenate([gw[e, :FE], gw[e + 1, :FE], gw[e, FE:], gw[e + 1, FE:]]) for e in range(0, NE, 2)] + [sgu],
        [np.concatenate([dw[e], dw[e + 1]], 1) for e in range(0, NE, 2)] + [sdn])
    qg, qu, qd = f["L1_ffn_wq_gate"], f["L1_ffn_wq_up"], f["L1_ffn_wq_down"]
    g["gu1"], g["dn1"] = groups(
        [np.concatenate([qg[k * FG:(k + 1) * FG], qu[k * FG:(k + 1) * FG]]) for k in range(G1)],
        [qd[:, k * FG:(k + 1) * FG] for k in range(G1)])
    g["s_gu"] = np.stack([np.concatenate([f["L1_ffn_s_gate"][k * FG:(k + 1) * FG], f["L1_ffn_s_up"][k * FG:(k + 1) * FG]]) for k in range(G1)])
    g["s_dn"] = f["L1_ffn_s_down"].reshape(1, DM)
    W = f["L1_attn_W_in"]
    parts = [W[k * INNER:(k + 1) * INNER] for k in range(4)]
    g["w_in"] = np.stack([rows_to_k(np.concatenate([w[h * P:(h + 1) * P] for w in parts])).reshape(P, -1) for h in range(HP)])
    g["w_dec"] = rows_to_k(np.concatenate([W[4 * INNER:], np.zeros((P - SH, DM), np.float32)])).reshape(P, -1)
    g["w_out"] = rows_to_k(f["L1_attn_W_out"])
    g["gamma"] = np.ascontiguousarray(f["L1_attn_gamma"].reshape(NT, P).T)
    g["beta"] = np.ascontiguousarray(f["L1_attn_beta"].reshape(NT, P).T)
    g["d_skip"] = f["L1_attn_D"].reshape(HP, P)

    eye = np.eye(P, dtype=np.float32)
    g["ident8"] = np.tile(eye, (1, NC))
    g["causal4"] = np.tile(np.triu(np.ones((P, P), np.float32)), (1, REP))
    g["earlier"] = np.tile((np.arange(NE)[None, :] < np.arange(NE)[:, None]).astype(np.float32).reshape(1, -1), (P, 1))
    inv = (np.float32(1.0) / np.power(np.float32(10000.0), np.arange(0, P, 2, dtype=np.float32) / np.float32(P))).astype(np.float32)
    ang = np.outer(np.arange(T, dtype=np.float32), inv).astype(np.float32).astype(np.float64)
    c, s = np.cos(ang).T.astype(np.float32), np.sin(ang).T.astype(np.float32)
    g["cos"] = np.concatenate([c, c])
    g["sin"] = np.concatenate([-s, s])
    return {k: np.ascontiguousarray(v) for k, v in g.items()}


def kernel(**inputs):
    import concourse.bacc as bacc
    from concourse.bass_utils import run_bass_kernel_spmd

    nc = bacc.Bacc("TRN2", target_bir_lowering=False, num_devices=1)
    arrays = launch_arrays(inputs)
    aps = {k: nc.dram_tensor(f"in_{k}", v.shape, mybir.dt.from_np(v.dtype), kind="ExternalInput").ap() for k, v in arrays.items()}
    aps["out"] = nc.dram_tensor("out_x", (B, T, DM), F32, kind="ExternalOutput").ap()
    build(nc, aps)
    r = run_bass_kernel_spmd(nc, [{f"in_{k}": v for k, v in arrays.items()}], core_ids=[0])
    return r.results[0]["out_x"]
```

```python
from contextlib import ExitStack

import numpy as np

import concourse.bass as bass
from concourse import mybir

P = 128
F32 = mybir.dt.float32
F32R = mybir.dt.float32r
I32 = mybir.dt.int32
ALU = mybir.AluOpType
ACT = mybir.ActivationFunctionType
AX = mybir.AxisListType

B = 2
T = 1024
DM = 256
KT = DM // P
NC = T // P
HALF = 512
INNER = 2048
NT = INNER // P

KVH, REP = 4, 4
ROT = REP + 1
QKV = (REP + 2) * P
NE = 8
FE = 176
FG = 2 * FE
G0, G1 = NE // 2 + 1, 2
GRP = G0 + G1
DT = 3

HP = 16
XZBC = 4 * P
SH = 32

LN_EPS = 1e-5
DEN_EPS = 1e-6
ZERO_POINT = 128.0
SPLITS = ((0, 0), (0, 1), (1, 0))
PHASES = 7
CONSTS = 7
RAWS = G0 + KVH + G1 + HP
PARTS = 3


def split_ffn0(b, g):
    return b * (RAWS + (PARTS - 1) * KVH) + g


def split_qkv(b, i, part):
    return split_ffn0(b, G0) + PARTS * i + part


def split_ffn1(b, k):
    return split_qkv(b, KVH, 0) + k


def split_ssm(b, h):
    return split_ffn1(b, G1) + h


class Event:

    def __init__(self, sem, credit):
        self.sem, self.credit = sem, credit

    def done(self, n):
        return n + 1 + self.credit

    def free(self, n, depth):
        return n + 1 + self.credit - depth


def build(nc, a):
    with ExitStack() as ctx:
        events = {}

        def event(name, owner, credit=16):
            e = Event(ctx.enter_context(nc.semaphore(name)), credit)
            events.setdefault(owner, []).append(e)
            return e

        def sem(name):
            return ctx.enter_context(nc.semaphore(name))

        def fixed(name, shape, dt=F32):
            return ctx.enter_context(nc.sbuf_tensor(name, shape, dt))

        x_res = fixed("x_res", [P, NC, DM])
        gate = fixed("gate", [P, NC, DM])
        xnT = [fixed(f"xnT_{s}", [P, KT, T], F32R) for s in ("hi", "lo")]
        ident4 = fixed("ident4", [P, HALF])
        causal = fixed("causal", [P, P])
        earlier = fixed("earlier", [P, NE * NE])
        w_out = fixed("w_out", [P, NT, DM])
        w_raw = fixed("w_raw", [P, KT * QKV])
        dn_raw = fixed("dn_raw", [P, 2, DT, DM])
        xn = fixed("xn", [P, 2, DM])
        router = [fixed(f"router_{s}", [P, KT, NE], F32R) for s in ("hi", "lo")]
        w_dec = [fixed(f"w_dec_{s}", [P, KT, P], F32R) for s in ("hi", "lo")]
        combine = fixed("combine", [P, 2 * G0, NC])
        combine_g = fixed("combine_g", [P, 2, 2, NC])
        den = fixed("den", [P, NC, KVH * REP])
        att_state = fixed("att_state", [P, 2, P + 1])
        ssm_state = fixed("ssm_state", [P, 2, P])
        ln_eps = fixed("ln_eps", [P, 1])
        ln_st = fixed("ln_st", [P, 2, 6])
        ln_mv = fixed("ln_mv", [P, 2, 2])
        ln_sd = fixed("ln_sd", [P, 2, 1])
        ln_rs = fixed("ln_rs", [P, 2, 1])
        in_st = fixed("in_st", [P, 2, 4 * 6])
        in_mv = fixed("in_mv", [P, 2, 2])
        in_sd = fixed("in_sd", [P, 2, 1])
        in_rs = fixed("in_rs", [P, 2, 1])
        gamma = fixed("gamma", [P, NT])
        beta = fixed("beta", [P, NT])

        def group():
            made = ExitStack()

            def shared(name, shape, dt=F32):
                return made.enter_context(nc.sbuf_tensor(name, shape, dt))
            return made, shared

        done, shared = group()
        y = shared("y", [P, NC, INNER])
        y_bytes_end = nc.sbuf_base
        done.close()
        done, shared = group()
        gu = [[shared(f"gu_{s}{k}", [P, KT, 2 * FG], F32R) for s in ("hi", "lo")] for k in range(2)]
        gu_f = shared("gu_f", [P, KT, 2 * FG])
        dn_f = shared("dn_f", [P, 2, DT, DM])
        s_gu = shared("s_gu", [P, 2, 2 * FG])
        s_dn = shared("s_dn", [P, DM])
        silu_g = shared("silu_g", [P, 2, FG])
        hid = shared("hid", [P, 2, DT * P])
        hidT = shared("hidT", [P, 2, DT * P])
        rt_l = shared("rt_l", [P, NC, NE])
        rt_m = shared("rt_m", [P, NC])
        rt_s = shared("rt_s", [P, NC])
        rt_gt = shared("rt_gt", [P, NC * NE, NE])
        rt_eq = shared("rt_eq", [P, NC * NE, NE])
        rt_rank = shared("rt_rank", [P, NC * NE])
        assert nc.sbuf_base <= y_bytes_end
        done.close()
        ctx.enter_context(nc.sbuf_tensor("y_fence", [P, NC * INNER], F32))

        done, shared = group()
        w_qkv = [shared(f"w_qkv_{s}", [P, KT, QKV], F32R) for s in ("hi", "lo")]
        qT = shared("qT", [P, REP, T])
        kT = shared("kT", [P, T])
        k_tok = shared("k_tok", [P, NC, P])
        v_tok = shared("v_tok", [P, NC, P + 1])
        vT = shared("vT", [P, HALF])
        cos = shared("cos", [P, T])
        sin = shared("sin", [P, T])
        ra = shared("ra", [P, 2, HALF])
        rb = shared("rb", [P, 2, HALF])
        mt = shared("mt", [P, 2, REP * P])
        done.close()
        done, shared = group()
        w_in = [[shared(f"w_in_{s}{k}", [P, KT, XZBC], F32R) for s in ("hi", "lo")] for k in range(2)]
        bT = shared("bT", [P, T])
        cTz = shared("cTz", [P, 2, T])
        cTp = shared("cTp", [P, T])
        b_tok = shared("b_tok", [P, NC, P])
        dec = shared("dec", [P, 2, T])
        lmat = shared("lmat", [P, 2, T])
        pdec = shared("pdec", [P, T])
        dstart = shared("dstart", [P, T])
        xz_x = shared("xz_x", [P, 2, 2 * P])
        sz = shared("sz", [P, 2, P])
        xw = shared("xw", [P, 2, P])
        xd = shared("xd", [P, 2, P])
        yg = shared("yg", [P, 2, P])
        mt1 = shared("mt1", [P, 2, 2 * P])
        d_row = shared("d_row", [P, 2, P])
        done.close()
        done, shared = group()
        dec_e = shared("dec_e", [SH, T])
        dec_t = shared("dec_t", [SH, T])
        done.close()
        done, shared = group()
        yn = shared("yn", [P, 2, INNER])
        yT = shared("yT", [P, 2, NT, P])
        sg = shared("sg", [P, 2, DM])
        rin = shared("rin", [P, 2, NT])
        rin2 = shared("rin2", [P, 2, NT])
        done.close()

        ps = ctx.enter_context(nc.psum_tensor("ps", [P, 8, 512], F32))
        dec_dram = nc.dram_tensor("dec_dram", (SH, T), F32, kind="Internal").ap()

        consts_in, x_in, w_raw_in, tables_in = sem("consts_in"), sem("x_in"), sem("w_raw_in"), sem("tables_in")
        dn_in = [sem("dn_in0"), sem("dn_in1")]
        w_out_in, scales_in = sem("w_out_in"), sem("scales_in")
        dec_in, dec_out, d_in = [sem("dec_in0"), sem("dec_in1")], sem("dec_out"), [sem("d_in0"), sem("d_in1")]
        stored = sem("stored")
        phase_end = sem("phase_end")
        init_step, settled = sem("init_step"), sem("settled")
        own_dve, own_act, own_pool = sem("own_dve"), sem("own_act"), sem("own_pool")
        rin_step, rin_step2, s_prep = sem("den_step"), sem("inner_ln_step"), sem("dec_prep")

        w_split = event("w_split", "pool")
        w_hi = event("w_hi", "act")
        ln_stat, ln_var = event("ln_stat", "dve"), event("ln_var", "dve")
        ln_std, ln_rstd = event("ln_std", "act"), event("ln_rstd", "dve")
        ln_xn, ln_tr = event("ln_xn", "dve"), event("ln_tr", "pe")
        ln_hi, ln_lo = event("ln_hi", "act"), event("ln_lo", "dve")
        rt_logits, rt_dve, rt_exp = event("rt_logits", "pe"), event("rt_dve", "dve"), event("rt_exp", "act")
        gate_zero = event("gate_zero", "pool")
        f_wf = event("f_wf", "dve")
        f_gu, f_silu, f_hid = event("f_gu", "pe"), event("f_silu", "act"), event("f_hid", "dve")
        f_tr, f_hidT, f_dn, f_acc = event("f_tr", "pe"), event("f_hidT", "act"), event("f_dn", "pe"), event("f_acc", "dve")
        f_cg = event("f_cg", "dve")
        dn_made = event("dn_made", "dve")
        a_proj = event("a_proj", "pe")
        a_mul, a_rot, a_act, a_qk = event("a_mul", "dve"), event("a_rot", "pool"), event("a_act", "act"), event("a_qk", "dve")
        a_neg = event("a_neg", "act")
        a_vT, a_trk, a_trv, a_kv = event("a_vT", "act"), event("a_trk", "pe"), event("a_trv", "pe"), event("a_kv", "act")
        a_sc, a_mt, a_up, a_st = event("a_sc", "pe"), event("a_mt", "dve"), event("a_up", "pe"), event("a_st", "dve")
        a_nd, a_out = event("a_nd", "pe"), event("a_out", "act")
        s_loga, s_dec = event("s_loga", "pe"), event("s_dec", "act")
        s_scan = event("s_scan", "dve")
        s_pb, s_pc, s_b, s_c = event("s_pb", "pe"), event("s_pc", "pe"), event("s_b", "act"), event("s_c", "act")
        s_cp, s_trb, s_btok = event("s_cp", "dve"), event("s_trb", "pe"), event("s_btok", "act")
        s_xz, s_xcopy, s_xw, s_xd = event("s_xz", "pe"), event("s_xcopy", "act"), event("s_xw", "dve"), event("s_xd", "pool")
        s_sc, s_mt, s_up, s_st = event("s_sc", "pe"), event("s_mt", "dve"), event("s_up", "pe"), event("s_st", "dve")
        s_y, s_yg, s_out = event("s_y", "pe"), event("s_yg", "dve"), event("s_out", "pool")
        o_stat, o_std = event("o_stat", "dve"), event("o_std", "act")
        o_yn, o_tr, o_yT = event("o_yn", "dve"), event("o_tr", "pe"), event("o_yT", "act")
        o_mm, o_sg, o_res = event("o_mm", "pe"), event("o_sg", "dve"), event("o_res", "dve")

        def start(eng, owner):
            for e in events[owner]:
                eng.sem_inc(e.sem, e.credit)

        def end_phase(eng, b, phase):
            eng.drain().then_inc(phase_end, 1)
            eng.wait_ge(phase_end, 4 * (b * PHASES + phase + 1))
            settle(eng)

        def settle(eng):
            eng.sem_inc(settled, 1)

        block = ctx.enter_context(nc.Block())

        @block.sync
        def _(sp):
            def weights(n, src, cols):
                sp.wait_ge(w_split.sem, w_split.done(n - 1))
                sp.dma_start(w_raw[:, 0:cols], src).then_inc(w_raw_in, 16)

            def down(slot, src):
                sp.dma_start(dn_raw[:, slot], src).then_inc(dn_in[slot], 16)

            def down_used(b, g):
                sp.wait_ge(f_dn.sem, f_dn.done((b * GRP + g) * NC + NC - 1))

            def phase_over(b, phase):
                sp.wait_ge(phase_end, 4 * (b * PHASES + phase + 1))
                settle(sp)

            sp.sem_inc(stored, 16)
            for dst, src in ((ident4, a["ident4"]), (causal, a["causal"]), (earlier, a["earlier"]),
                             (gamma, a["gamma"]), (beta, a["beta"])):
                sp.dma_start(dst[:], src).then_inc(consts_in, 16)
            sp.dma_start(x_res[:, 0, :], a["router"]).then_inc(consts_in, 16)
            sp.dma_start(x_res[:, 1, :], a["w_dec"]).then_inc(consts_in, 16)
            sp.wait_ge(init_step, 2)
            with sp.Fori(0, B) as b:
                sp.wait_ge(stored, 16 * (b + 1))
                settle(sp)
                sp.dma_start(x_res[:], a["x"][bass.ds(b, 1)].rearrange("b (c p) d -> p (b c) d", p=P)).then_inc(x_in, 16)
                sp.wait_ge(dn_made.sem, dn_made.done(b * G1 - 1))
                settle(sp)
                with sp.Fori(0, G0 // 2) as i:
                    for k in range(2):
                        weights(split_ffn0(b, 2 * i + k), a["gu0"][bass.ds(2 * i + k, 1)].rearrange("g p c -> p (g c)"), KT * 2 * FG)
                        down_used(b, 2 * i + k - 2)
                        down(k, a["dn0"][bass.ds(2 * i + k, 1)].rearrange("g p (t c) -> p (g t) c", t=DT))
                weights(split_ffn0(b, G0 - 1), a["gu0"][G0 - 1], KT * 2 * FG)
                down_used(b, G0 - 3)
                down(0, a["dn0"][G0 - 1].rearrange("p (t c) -> p t c", t=DT))
                sp.dma_start(cos[:], a["cos"]).then_inc(tables_in, 16)
                sp.dma_start(sin[:], a["sin"]).then_inc(tables_in, 16)
                sp.dma_start(w_out[:], a["w_o"]).then_inc(w_out_in, 16)
                with sp.Fori(0, KVH) as i:
                    weights(split_qkv(b, i, 0), a["w_qkv"][bass.ds(i, 1)].rearrange("g p c -> p (g c)"), KT * QKV)
                for k in range(G1):
                    if k == 0:
                        weights(split_ffn1(b, 0), a["gu1"][0].bitcast(F32), KT * 2 * FG)
                        phase_over(b, 3)
                        sp.dma_start(w_out[:], a["w_out"]).then_inc(w_out_in, 16)
                        for g in range(G1):
                            sp.dma_start(s_gu[:, g, :], a["s_gu"][g:g + 1, :].broadcast_to([P, 2 * FG])).then_inc(scales_in, 16)
                        sp.dma_start(s_dn[:], a["s_dn"].broadcast_to([P, DM])).then_inc(scales_in, 16)
                    else:
                        weights(split_ffn1(b, 1), a["gu1"][1].bitcast(F32), KT * 2 * FG)
                    down_used(b, G0 - 1 - k)
                    down(k, a["dn1"][k].rearrange("p (t c) -> p t c", t=DT).bitcast(F32))
                sp.wait_ge(s_dec.sem, s_dec.done(b))
                sp.dma_start(dec_dram, dec_t[:]).then_inc(dec_out, 16)
                sp.wait_ge(dec_out, 16 * (b + 1))
                settle(sp)
                with sp.Fori(0, HP // 2) as i:
                    for w in range(2):
                        h = 2 * i + w
                        n = b * HP + h
                        weights(split_ssm(b, h), a["w_in"][bass.ds(h, 1)].rearrange("g p c -> p (g c)"), KT * XZBC)
                        sp.wait_ge(s_out.sem, s_out.done((n - 2) * NC + NC - 1))
                        sp.dma_start(d_row[:, w, :], a["d_skip"][bass.ds(h, 1), :].broadcast_to([P, P])).then_inc(d_in[w], 16)
                        for hf in range(2):
                            toks = slice(hf * HALF, (hf + 1) * HALF)
                            sp.wait_ge(s_scan.sem, s_scan.done(2 * n + hf - 2))
                            sp.dma_start(dec[:, :, toks], dec_dram[bass.ds(2 * h, 2), toks].partition_broadcast(P)).then_inc(dec_in[hf], 16)
                phase_over(b, 6)
                sp.dma_start(a["out"][bass.ds(b, 1)].rearrange("b (c p) d -> p (b c) d", p=P), x_res[:]).then_inc(stored, 16)
            sp.wait_ge(stored, 16 * (B + 1))

        @block.gpsimd
        def _(pool):
            start(pool, "pool")

            def split_lo(n, lo, raw, hi):
                pool.wait_ge(w_hi.sem, w_hi.done(n))
                nc.gpsimd.tensor_tensor(lo, raw, hi, ALU.subtract).then_inc(w_split.sem, 1)

            with pool.Fori(0, B) as b:
                nc.gpsimd.memset(gate[:], 0.0)
                nc.gpsimd.memset(hid[:, :, FG:DT * P], 0.0).then_inc(gate_zero.sem, 1)
                raw = w_raw[:, 0:KT * 2 * FG].rearrange("p (k c) -> p k c", k=KT)
                split_lo(split_ffn0(b, 0), gu[0][1][:], raw, gu[0][0][:])
                end_phase(pool, b, 0)
                with pool.Fori(0, G0 // 2) as i:
                    split_lo(split_ffn0(b, 2 * i + 1), gu[1][1][:], raw, gu[1][0][:])
                    split_lo(split_ffn0(b, 2 * i + 2), gu[0][1][:], raw, gu[0][0][:])
                nc.gpsimd.memset(v_tok[:, :, P:P + 1], 1.0)
                raw = w_raw[:].rearrange("p (k c) -> p k c", k=KT)

                def qkv_lo(i, part):
                    cols = slice(part * 2 * P, (part + 1) * 2 * P)
                    split_lo(split_qkv(b, i, part), w_qkv[1][:, :, cols], raw[:, :, cols], w_qkv[0][:, :, cols])
                for part in range(PARTS):
                    qkv_lo(0, part)
                end_phase(pool, b, 1)

                def att_rotate(n, hf, r):
                    step, k = (2 * n + hf) * ROT + r, (hf * ROT + r) % 2
                    pool.wait_ge(a_mul.sem, a_mul.done(step))
                    nc.gpsimd.tensor_tensor(rb[:, k], ra[:, k], rb[:, k], ALU.add).then_inc(a_rot.sem, 1)

                def att_head(i, last):
                    n = b * KVH + i
                    for hf in range(2):
                        lo_parts = [part for part in range(PARTS) if not last and hf == 0]
                        if not last or hf == 0:
                            att_rotate(n + hf, 1 - hf, 1)
                            att_rotate(n + hf, 1 - hf, 2)
                        for part in lo_parts[:1]:
                            qkv_lo(i + 1, part)
                        if not last or hf == 0:
                            att_rotate(n + hf, 1 - hf, 3)
                            att_rotate(n + hf, 1 - hf, 4)
                        for part in lo_parts[1:]:
                            qkv_lo(i + 1, part)
                        if not last:
                            att_rotate(n + 1, hf, 0)
                for r in range(ROT):
                    att_rotate(b * KVH, 0, r)
                att_rotate(b * KVH, 1, 0)
                with pool.Fori(0, KVH - 1) as i:
                    att_head(i, False)
                att_head(KVH - 1, True)
                end_phase(pool, b, 2)
                end_phase(pool, b, 3)

                nc.gpsimd.memset(gate[:], 0.0)
                nc.gpsimd.memset(hid[:, :, FG:DT * P], 0.0).then_inc(gate_zero.sem, 1)
                for k in range(G1):
                    split_lo(split_ffn1(b, k), gu[k][1][:], gu_f[:], gu[k][0][:])
                nc.gpsimd.memset(cTz[:], 0.0)
                nc.gpsimd.memset(xz_x[:, :, 64:192], 0.0)
                nc.gpsimd.memset(dstart[:], 0.0)
                pool.drain().then_inc(own_pool, 1)
                raw = w_raw[:, 0:KT * XZBC].rearrange("p (k c) -> p k c", k=KT)
                split_lo(split_ssm(b, 0), w_in[0][1][:], raw, w_in[0][0][:])
                end_phase(pool, b, 4)

                def ssm_pairs(i, last_pairs):
                    for w in range(2):
                        n = b * HP + 2 * i + w
                        following = w == 0 or not last_pairs
                        for c in range(NC):
                            m, s = n * NC + c, c % 2
                            pool.wait_ge(s_xcopy.sem, s_xcopy.done(m))
                            if c == 0:
                                pool.wait_ge(d_in[w], 16 * (b * (HP // 2) + i + 1))
                            pool.wait_ge(s_yg.sem, s_yg.free(m, 2))
                            nc.gpsimd.tensor_tensor(xd[:, s].rearrange("p (h c) -> p h c", c=64),
                                                    xz_x[:, s, :].rearrange("p (h c) -> p h c", c=64)[:, 0:4:3, :],
                                                    d_row[:, w].rearrange("p (h c) -> p h c", c=64), ALU.mult).then_inc(s_xd.sem, 1)
                            pool.wait_ge(s_yg.sem, s_yg.done(m))
                            nc.gpsimd.tensor_tensor(y[:, c, bass.ds((2 * i + w) * P, P)], yg[:, s], sz[:, s], ALU.mult).then_inc(s_out.sem, 1)
                            if following and c < 4:
                                k, half = c // 2, slice(c % 2 * 2 * P, (c % 2 + 1) * 2 * P)
                                if c == 0:
                                    pool.wait_ge(w_hi.sem, w_hi.done(split_ssm(b, 2 * i + w + 1)))
                                ins = nc.gpsimd.tensor_tensor(w_in[1 - w][1][:, k, half], raw[:, k, half], w_in[1 - w][0][:, k, half], ALU.subtract)
                                if c == 3:
                                    ins.then_inc(w_split.sem, 1)
                with pool.Fori(0, HP // 2 - 1) as i:
                    ssm_pairs(i, False)
                ssm_pairs(HP // 2 - 1, True)
                end_phase(pool, b, 5)
                end_phase(pool, b, 6)

        @block.tensor
        def _(pe):
            start(pe, "pe")

            def three_passes(out, left, right):
                steps = [(k, l, r) for k in range(KT) for l, r in SPLITS]
                for j, (k, l, r) in enumerate(steps):
                    mm = nc.tensor.matmul(out, left(l, k), right(r, k), start=(j == 0), stop=(j == len(steps) - 1))
                return mm

            def ln_transposes(n, s):
                pe.wait_ge(ln_xn.sem, ln_xn.done(n))
                pe.wait_ge(ln_lo.sem, ln_lo.free(n, 2))
                for k in range(KT):
                    mm = nc.tensor.transpose(ps[:, 6 + s, k * P:(k + 1) * P], xn[:, s, k * P:(k + 1) * P], ident4[:, 0:P])
                mm.then_inc(ln_tr.sem, 1)

            def ffn_group(b, g, slot, dn, raw_n, uses):
                def gate_up(c):
                    n = (b * GRP + g) * NC + c
                    if c == 0:
                        pe.wait_ge(w_hi.sem, w_hi.done(raw_n))
                        pe.wait_ge(w_split.sem, w_split.done(raw_n))
                    pe.wait_ge(f_hid.sem, f_hid.free(n, 2))
                    for j in range(2):
                        mm = three_passes(ps[:, 2 * (c % 2) + j, 0:FG],
                                          lambda l, k: xnT[l][:, k, c * P:(c + 1) * P],
                                          lambda r, k: gu[slot][r][:, k, j * FG:(j + 1) * FG])
                    mm.then_inc(f_gu.sem, 1)

                def turn(c):
                    n = (b * GRP + g) * NC + c
                    pe.wait_ge(f_hid.sem, f_hid.done(n))
                    pe.wait_ge(f_hidT.sem, f_hidT.free(n, 2))
                    for t in range(DT):
                        mm = nc.tensor.transpose(ps[:, 4 + c % 2, t * P:(t + 1) * P], hid[:, c % 2, t * P:(t + 1) * P], ident4[:, 0:P])
                    mm.then_inc(f_tr.sem, 1)

                def down(c):
                    n = (b * GRP + g) * NC + c
                    pe.wait_ge(f_hidT.sem, f_hidT.done(n))
                    pe.wait_ge(f_acc.sem, f_acc.free(n, 2))
                    for t in range(DT):
                        mm = nc.tensor.matmul(ps[:, 6 + c % 2, 0:DM], hidT[:, c % 2, t * P:(t + 1) * P], dn[:, slot, t, :],
                                              start=(t == 0), stop=(t == DT - 1))
                    mm.then_inc(f_dn.sem, 1)

                for c in range(NC + 2):
                    if c < NC:
                        gate_up(c)
                    if 1 <= c <= NC:
                        turn(c - 1)
                    if c >= 2:
                        if c == 2:
                            uses()
                        down(c - 2)

            def out_proj(b, layer, extra):
                with pe.Fori(0, NC // 2) as j:
                    for s in range(2):
                        n = (b * 2 + layer) * NC + 2 * j + s
                        for q in range(4):
                            pe.wait_ge(o_yn.sem, o_yn.done(4 * n + q))
                            pe.wait_ge(o_yT.sem, o_yT.free(4 * n + q, 4))
                            for t in range(4):
                                mm = nc.tensor.transpose(ps[:, q, t * P:(t + 1) * P], yn[:, s, (4 * q + t) * P:(4 * q + t + 1) * P], ident4[:, 0:P])
                            mm.then_inc(o_tr.sem, 1)
                    for s in range(2):
                        n = (b * 2 + layer) * NC + 2 * j + s
                        pe.wait_ge(o_yT.sem, o_yT.done(4 * n + 3))
                        pe.wait_ge(o_sg.sem, o_sg.free(n, 2))
                        for t in range(NT):
                            mm = nc.tensor.matmul(ps[:, 4 + s, 0:DM], yT[:, s, t, :], w_out[:, t, :], start=(t == 0), stop=(t == NT - 1))
                        mm.then_inc(o_mm.sem, 1)
                    extra(j)

            pe.wait_ge(consts_in, 16 * CONSTS)
            with pe.Fori(0, B) as b:
                with pe.Fori(0, NC // 2) as j:
                    for s in range(2):
                        ln_transposes(b * 2 * NC + 2 * j + s, s)
                end_phase(pe, b, 0)

                for c in range(NC):
                    mm = three_passes(ps[:, 7, c * NE:(c + 1) * NE], lambda l, k: xnT[l][:, k, c * P:(c + 1) * P],
                                      lambda r, k: router[r][:, k, :])
                mm.then_inc(rt_logits.sem, 1)

                def loaded(slot, count):
                    return lambda: pe.wait_ge(dn_in[slot], 16 * count)
                pe.wait_ge(rt_dve.sem, rt_dve.done(b * 9))
                settle(pe)
                with pe.Fori(0, G0 // 2) as i:
                    for k in range(2):
                        ffn_group(b, 2 * i + k, k, dn_raw, split_ffn0(b, 2 * i + k), loaded(k, b * (4 - k) + i + 1))
                ffn_group(b, G0 - 1, 0, dn_raw, split_ffn0(b, G0 - 1), loaded(0, b * 4 + 3))
                end_phase(pe, b, 1)

                def att_project(n, i, hf, t):
                    u = 2 * n + hf
                    if hf == 0 and t % 2 == 0:
                        pe.wait_ge(w_hi.sem, w_hi.done(split_qkv(b, i, t // 2)))
                        pe.wait_ge(w_split.sem, w_split.done(split_qkv(b, i, t // 2)))
                    if t == 3:
                        pe.wait_ge(a_vT.sem, a_vT.done(u))
                    else:
                        pe.wait_ge(a_mul.sem, a_mul.done(u * ROT + (-2, -1, 0, None, 1, 2)[t]))
                    three_passes(ps[:, t % 2, :], lambda l, k: w_qkv[l][:, k, t * P:(t + 1) * P],
                                 lambda r, k: xnT[r][:, k, hf * HALF:(hf + 1) * HALF]).then_inc(a_proj.sem, 1)

                def v_turn(n, hf):
                    u = 2 * n + hf
                    pe.wait_ge(a_vT.sem, a_vT.done(u))
                    pe.wait_ge(a_kv.sem, a_kv.done(2 * u - 1))
                    for c in range(4):
                        mm = nc.tensor.transpose(ps[:, 7, c * P:(c + 1) * P], vT[:, c * P:(c + 1) * P], ident4[:, 0:P])
                    mm.then_inc(a_trv.sem, 1)

                def k_turn(n, hf):
                    u = 2 * n + hf
                    pe.wait_ge(a_qk.sem, a_qk.done(u * ROT))
                    pe.wait_ge(a_kv.sem, a_kv.done(2 * u))
                    for c in range(4):
                        mm = nc.tensor.transpose(ps[:, 7, c * P:(c + 1) * P], kT[:, (4 * hf + c) * P:(4 * hf + c + 1) * P], ident4[:, 0:P])
                    mm.then_inc(a_trk.sem, 1)

                def att_score(n, c):
                    m = n * NC + c
                    if c % 4 == 0:
                        pe.wait_ge(a_qk.sem, a_qk.done((2 * n + c // 4) * ROT + ROT - 1))
                    pe.wait_ge(a_mt.sem, a_mt.done(m - 2))
                    nc.tensor.matmul(ps[:, 2 + c % 2, :], kT[:, c * P:(c + 1) * P], qT[:, :, c * P:(c + 1) * P],
                                     start=True, stop=True).then_inc(a_sc.sem, 1)

                def att_update(n, c):
                    m = n * NC + c
                    if c % 4 == 0:
                        pe.wait_ge(a_kv.sem, a_kv.done(2 * (2 * n + c // 4) + 1))
                    if c == NC - 1:
                        return
                    pe.wait_ge(a_st.sem, a_st.done(m - 1))
                    nc.tensor.matmul(ps[:, 6, 0:P + 1], k_tok[:, c, :], v_tok[:, c, :], start=True, stop=True).then_inc(a_up.sem, 1)

                def att_numerator(n, c):
                    m = n * NC + c
                    pe.wait_ge(a_mt.sem, a_mt.done(m))
                    pe.wait_ge(a_st.sem, a_st.done(m - 1))
                    pe.wait_ge(a_out.sem, a_out.done(m - 1))
                    for h in range(REP):
                        out = ps[:, 4 + h // 2, (h % 2) * (P + 1):(h % 2 + 1) * (P + 1)]
                        nc.tensor.matmul(out, mt[:, c % 2, h * P:(h + 1) * P], v_tok[:, c, :], start=True, stop=False)
                        mm = nc.tensor.matmul(out, qT[:, h, c * P:(c + 1) * P], att_state[:, c % 2, :], start=False, stop=True)
                    mm.then_inc(a_nd.sem, 1)

                def att_head(i, last):
                    n = b * KVH + i
                    for hf in range(2):
                        q_ahead, kv_ahead = not last or hf == 0, not last
                        nxt = (n + hf, i + hf, 1 - hf)
                        turn = (n + hf, 1 - hf)
                        c = 4 * hf
                        att_score(n, c + 1)
                        if q_ahead:
                            att_project(*nxt, 2)
                            v_turn(*turn)
                        att_update(n, c)
                        att_numerator(n, c)
                        if q_ahead:
                            att_project(*nxt, 3)
                            k_turn(*turn)
                        att_score(n, c + 2)
                        if q_ahead:
                            att_project(*nxt, 4)
                        att_update(n, c + 1)
                        att_numerator(n, c + 1)
                        if q_ahead:
                            att_project(*nxt, 5)
                        att_score(n, c + 3)
                        att_update(n, c + 2)
                        att_numerator(n, c + 2)
                        if kv_ahead:
                            att_project(n + 1, i + 1, hf, 0)
                        att_update(n, c + 3)
                        att_numerator(n, c + 3)
                        if kv_ahead:
                            att_project(n + 1, i + 1, hf, 1)
                        if q_ahead:
                            att_score(n + hf, (c + 4) % NC)

                for t in range(REP + 2):
                    att_project(b * KVH, 0, 0, t)
                v_turn(b * KVH, 0)
                k_turn(b * KVH, 0)
                for t in range(2):
                    att_project(b * KVH, 0, 1, t)
                att_score(b * KVH, 0)
                with pe.Fori(0, KVH - 1) as i:
                    att_head(i, False)
                att_head(KVH - 1, True)
                end_phase(pe, b, 2)

                pe.wait_ge(w_out_in, 16 * (2 * b + 1))

                settle(pe)

                def next_ln(j):
                    for s in range(2):
                        ln_transposes((b * 2 + 1) * NC + 2 * j + s, s)
                out_proj(b, 0, next_ln)
                end_phase(pe, b, 3)

                for hf in range(2):
                    mm = three_passes(ps[:, hf, :], lambda l, k: w_dec[l][:, k, :],
                                      lambda r, k: xnT[r][:, k, hf * HALF:(hf + 1) * HALF])
                mm.then_inc(s_loga.sem, 1)

                def made(k):
                    return lambda: pe.wait_ge(dn_made.sem, dn_made.done(b * G1 + k))
                pe.wait_ge(s_dec.sem, s_dec.done(b))
                for k in range(G1):
                    ffn_group(b, G0 + k, k, dn_f, split_ffn1(b, k), made(k))
                end_phase(pe, b, 4)

                def ssm_weights(h):
                    pe.wait_ge(w_hi.sem, w_hi.done(split_ssm(b, h)))
                    pe.wait_ge(w_split.sem, w_split.done(split_ssm(b, h)))

                def project_b(u, w, hf):
                    pe.wait_ge(s_btok.sem, s_btok.done(u - 1))
                    three_passes(ps[:, 0, :], lambda l, k: w_in[w][l][:, k, 2 * P:3 * P],
                                 lambda r, k: xnT[r][:, k, hf * HALF:(hf + 1) * HALF]).then_inc(s_pb.sem, 1)

                def project_c(u, w, hf):
                    pe.wait_ge(s_cp.sem, s_cp.done(u - 1))
                    three_passes(ps[:, 1, :], lambda l, k: w_in[w][l][:, k, 3 * P:4 * P],
                                 lambda r, k: xnT[r][:, k, hf * HALF:(hf + 1) * HALF]).then_inc(s_pc.sem, 1)

                def b_turn(u, hf):
                    pe.wait_ge(s_b.sem, s_b.done(u))
                    for c in range(4):
                        mm = nc.tensor.transpose(ps[:, 0, c * P:(c + 1) * P], bT[:, (4 * hf + c) * P:(4 * hf + c + 1) * P], ident4[:, 0:P])
                    mm.then_inc(s_trb.sem, 1)

                def project_xz(m, w, c):
                    pe.wait_ge(s_xw.sem, s_xw.free(m, 2))
                    three_passes(ps[:, 2 + c % 2, 0:2 * P], lambda l, k: xnT[l][:, k, c * P:(c + 1) * P],
                                 lambda r, k: w_in[w][r][:, k, 0:2 * P]).then_inc(s_xz.sem, 1)

                def ssm_score(u, m, c):
                    if c % 4 == 0:
                        pe.wait_ge(s_c.sem, s_c.done(u))
                        pe.wait_ge(s_b.sem, s_b.done(u))
                    pe.wait_ge(s_mt.sem, s_mt.free(m, 2))
                    nc.tensor.matmul(ps[:, 4 + c % 2, 0:2 * P], bT[:, c * P:(c + 1) * P], cTz[:, :, c * P:(c + 1) * P],
                                     start=True, stop=True).then_inc(s_sc.sem, 1)

                def ssm_update(u, m, c):
                    if c % 4 == 0:
                        pe.wait_ge(s_btok.sem, s_btok.done(u))
                    if c == NC - 1:
                        return
                    pe.wait_ge(s_xw.sem, s_xw.done(m))
                    pe.wait_ge(s_st.sem, s_st.done(m - 1))
                    nc.tensor.matmul(ps[:, 7, 0:P], b_tok[:, c, :], xw[:, c % 2, :], start=True, stop=True).then_inc(s_up.sem, 1)

                def ssm_outputs(u, m, c):
                    out = ps[:, 6, 0:P]
                    pe.wait_ge(s_mt.sem, s_mt.done(m))
                    pe.wait_ge(s_xcopy.sem, s_xcopy.done(m))
                    pe.wait_ge(s_yg.sem, s_yg.done(m - 1))
                    for h in range(2):
                        nc.tensor.matmul(out, mt1[:, c % 2, h * P:(h + 1) * P], xz_x[:, c % 2, h * P:(h + 1) * P],
                                         start=(h == 0), stop=False)
                    pe.wait_ge(s_cp.sem, s_cp.done(u))
                    pe.wait_ge(s_st.sem, s_st.done(m - 1))
                    nc.tensor.matmul(out, cTp[:, c * P:(c + 1) * P], ssm_state[:, c % 2, :], start=False, stop=True).then_inc(s_y.sem, 1)

                def ssm_pairs(i, last_pairs):
                    for w in range(2):
                        n = b * HP + 2 * i + w
                        for c in range(NC):
                            u, m, hf = 2 * n + c // 4, n * NC + c, c // 4
                            nw, nhf = (w + hf) % 2, 1 - hf
                            ahead = c < NC - 1 or w == 0 or not last_pairs
                            unit_ahead = hf == 0 or w == 0 or not last_pairs
                            if ahead:
                                cw = w if c < NC - 1 else 1 - w
                                project_xz(m + 1, cw, (c + 1) % NC)
                                ssm_score(u + (c % 4 == 3), m + 1, (c + 1) % NC)
                            ssm_update(u, m, c)
                            ssm_outputs(u, m, c)
                            if unit_ahead and c % 4 == 0:
                                if hf == 1:
                                    ssm_weights(2 * i + w + 1)
                                project_b(u + 1, nw, nhf)
                            if unit_ahead and c % 4 == 1:
                                project_c(u + 1, nw, nhf)
                            if unit_ahead and c % 4 == 2:
                                b_turn(u + 1, nhf)

                pe.wait_ge(own_pool, b + 1)
                ssm_weights(0)
                u, m = 2 * b * HP, b * HP * NC
                project_b(u, 0, 0)
                project_c(u, 0, 0)
                project_xz(m, 0, 0)
                b_turn(u, 0)
                ssm_score(u, m, 0)
                with pe.Fori(0, HP // 2 - 1) as i:
                    ssm_pairs(i, False)
                ssm_pairs(HP // 2 - 1, True)
                end_phase(pe, b, 5)

                pe.wait_ge(w_out_in, 16 * (2 * b + 2))
                settle(pe)
                out_proj(b, 1, lambda j: None)
                end_phase(pe, b, 6)

        @block.scalar
        def _(act):
            start(act, "act")

            def split_hi(n, hi, raw):
                nc.scalar.activation(hi, raw, ACT.Copy).then_inc(w_hi.sem, 1)

            def ln_std_of(n, s):
                act.wait_ge(ln_var.sem, ln_var.done(n))
                act.wait_ge(ln_rstd.sem, ln_rstd.free(n, 2))
                nc.scalar.activation(ln_sd[:, s, :], ln_mv[:, s, 1:2], ACT.Sqrt, bias=ln_eps[:, 0:1]).then_inc(ln_std.sem, 1)

            def ln_hi_of(n, c, s):
                act.wait_ge(ln_tr.sem, ln_tr.done(n))
                nc.scalar.activation(xnT[0][:, :, bass.ds(c * P, P)], ps[:, 6 + s, 0:DM].rearrange("p (k c) -> p k c", k=KT),
                                     ACT.Copy).then_inc(ln_hi.sem, 1)

            def ffn_group(b, g, slot, prep):
                for c in range(NC + 1):
                    if c < NC:
                        n = (b * GRP + g) * NC + c
                        act.wait_ge(f_gu.sem, f_gu.done(n))
                        act.wait_ge(f_hid.sem, f_hid.free(n, 2))
                        nc.scalar.activation(silu_g[:, c % 2], ps[:, 2 * (c % 2), 0:FG], ACT.Silu).then_inc(f_silu.sem, 1)
                    if c >= 1:
                        n = (b * GRP + g) * NC + c - 1
                        act.wait_ge(f_tr.sem, f_tr.done(n))
                        act.wait_ge(f_dn.sem, f_dn.free(n, 2))
                        nc.scalar.activation(hidT[:, (c - 1) % 2], ps[:, 4 + (c - 1) % 2, 0:DT * P], ACT.Copy).then_inc(f_hidT.sem, 1)
                    if c == 3:
                        prep()

            def gate_silu(b, g):
                act.wait_ge(f_acc.sem, f_acc.done((b * GRP + g) * NC + NC - 1))
                nc.scalar.activation(gate[:], gate[:], ACT.Silu)

            def out_proj(b, layer, extra):
                with act.Fori(0, NC // 2) as j:
                    if layer == 1:
                        for s in range(2):
                            n = b * NC + 2 * j + s
                            act.wait_ge(o_stat.sem, o_stat.done(n))
                            nc.scalar.activation(in_sd[:, s, :], in_mv[:, s, 1:2], ACT.Sqrt, bias=ln_eps[:, 0:1]).then_inc(o_std.sem, 1)
                    for s in range(2):
                        n = (b * 2 + layer) * NC + 2 * j + s
                        act.wait_ge(o_mm.sem, o_mm.free(n, 2))
                        for q in range(4):
                            act.wait_ge(o_tr.sem, o_tr.done(4 * n + q))
                            if layer == 0:
                                nc.scalar.activation(yT[:, s, 4 * q:4 * q + 4, :].rearrange("p t c -> p (t c)"), ps[:, q, :],
                                                     ACT.Copy).then_inc(o_yT.sem, 1)
                                continue
                            for t in range(4):
                                k = 4 * q + t
                                ins = nc.scalar.activation(yT[:, s, k, :], ps[:, q, t * P:(t + 1) * P], ACT.Identity,
                                                           bias=beta[:, k:k + 1], scale=gamma[:, k:k + 1])
                            ins.then_inc(o_yT.sem, 1)
                    extra(j)

            act.wait_ge(consts_in, 16 * CONSTS)
            nc.scalar.activation(router[0][:].rearrange("p k c -> p (k c)"), x_res[:, 0, 0:KT * NE], ACT.Copy)
            nc.scalar.activation(w_dec[0][:].rearrange("p k c -> p (k c)"), x_res[:, 1, :], ACT.Copy).then_inc(init_step, 1)
            with act.Fori(0, B) as b:
                def ln_pair(j, base):
                    for s in range(2):
                        ln_std_of(base + 2 * j + s, s)
                    for s in range(2):
                        ln_hi_of(base + 2 * j + s, 2 * j + s, s)
                raw = w_raw[:, 0:KT * 2 * FG].rearrange("p (k c) -> p k c", k=KT)

                def prep0(g, slot):
                    def do():
                        act.wait_ge(w_raw_in, 16 * (b * RAWS + g + 1))
                        act.wait_ge(f_gu.sem, f_gu.done((b * GRP + g - 2) * NC + NC - 1))
                        split_hi(0, gu[slot][0][:], raw)
                    return do
                prep0(0, 0)()
                with act.Fori(0, NC // 2) as j:
                    ln_pair(j, b * 2 * NC)
                end_phase(act, b, 0)

                act.wait_ge(rt_dve.sem, rt_dve.done(b * 9 + 2))
                nc.scalar.activation(rt_l[:], rt_l[:], ACT.Exp).then_inc(rt_exp.sem, 1)
                with act.Fori(0, G0 // 2) as i:
                    ffn_group(b, 2 * i, 0, prep0(2 * i + 1, 1))
                    ffn_group(b, 2 * i + 1, 1, prep0(2 * i + 2, 0))

                def qkv_hi(i, part):
                    if part == 0:
                        act.wait_ge(w_raw_in, 16 * (b * RAWS + G0 + i + 1))
                    act.wait_ge(a_proj.sem, a_proj.done((b * KVH + i) * 2 * (REP + 2) - (REP + 1) + 2 * part))
                    cols = slice(part * 2 * P, (part + 1) * 2 * P)
                    split_hi(0, w_qkv[0][:, :, cols], w_raw[:].rearrange("p (k c) -> p k c", k=KT)[:, :, cols])

                def first_head():
                    for part in range(PARTS):
                        qkv_hi(0, part)
                ffn_group(b, G0 - 1, 0, first_head)
                gate_silu(b, G0 - 1)
                end_phase(act, b, 1)

                def rope_act(n, hf, r):
                    step, k = (2 * n + hf) * ROT + r, (hf * ROT + r) % 2
                    act.wait_ge(a_rot.sem, a_rot.done(step))
                    nc.scalar.activation(ra[:, k], rb[:, k], ACT.Relu, scale=-1.0).then_inc(a_neg.sem, 1)
                    act.wait_ge(a_neg.sem, a_neg.done(step))
                    nc.scalar.activation(ra[:, k], ra[:, k], ACT.Exp, scale=-1.0).then_inc(a_act.sem, 1)

                def v_copy(n, hf):
                    u = 2 * n + hf
                    act.wait_ge(a_proj.sem, a_proj.done(u * (REP + 2) + 1))
                    act.wait_ge(a_trv.sem, a_trv.done(u - 1))
                    nc.scalar.activation(vT[:], ps[:, 1, :], ACT.Copy).then_inc(a_vT.sem, 1)

                def v_tok_copy(n, hf):
                    u = 2 * n + hf
                    act.wait_ge(a_trv.sem, a_trv.done(u))
                    act.wait_ge(a_nd.sem, a_nd.done(4 * u - 5))
                    nc.scalar.activation(v_tok[:, 4 * hf:4 * hf + 4, 0:P], ps[:, 7, :].rearrange("p (c e) -> p c e", e=P), ACT.Copy).then_inc(a_kv.sem, 1)

                def k_tok_copy(n, hf):
                    act.wait_ge(a_trk.sem, a_trk.done(2 * n + hf))
                    nc.scalar.activation(k_tok[:, 4 * hf:4 * hf + 4, :], ps[:, 7, :].rearrange("p (c e) -> p c e", e=P), ACT.Copy).then_inc(a_kv.sem, 1)

                def out_copy(n, i, c):
                    act.wait_ge(a_nd.sem, a_nd.done(n * NC + c))
                    nd = ps[:, 4:6, 0:2 * (P + 1)].rearrange("p b (h e) -> p b h e", e=P + 1)
                    nc.scalar.activation(y[:, c, bass.ds(i * REP * P, REP * P)].rearrange("p (b h e) -> p b h e", b=2, h=2),
                                         nd[:, :, :, 0:P], ACT.Copy)
                    nc.scalar.activation(den[:, c, bass.ds(i * REP, REP)].rearrange("p (b h) -> p b h", b=2),
                                         nd[:, :, :, P], ACT.Copy).then_inc(a_out.sem, 1)

                def att_head(i, last):
                    n = b * KVH + i
                    for hf in range(2):
                        q_ahead, kv_ahead = not last or hf == 0, not last
                        nxt = (n + hf, 1 - hf)
                        c = 4 * hf
                        split = not last and hf == 0
                        if q_ahead:
                            v_tok_copy(*nxt)
                            rope_act(*nxt, 1)
                        out_copy(n, i, c)
                        if q_ahead:
                            k_tok_copy(*nxt)
                            rope_act(*nxt, 2)
                        if split:
                            qkv_hi(i + 1, 0)
                        if q_ahead:
                            rope_act(*nxt, 3)
                        out_copy(n, i, c + 1)
                        if q_ahead:
                            rope_act(*nxt, 4)
                        if split:
                            qkv_hi(i + 1, 1)
                        out_copy(n, i, c + 2)
                        if split:
                            qkv_hi(i + 1, 2)
                        if kv_ahead:
                            rope_act(n + 1, hf, 0)
                        out_copy(n, i, c + 3)
                        if kv_ahead:
                            v_copy(n + 1, hf)
                rope_act(b * KVH, 0, 0)
                v_copy(b * KVH, 0)
                for r in range(1, ROT):
                    rope_act(b * KVH, 0, r)
                v_tok_copy(b * KVH, 0)
                k_tok_copy(b * KVH, 0)
                rope_act(b * KVH, 1, 0)
                v_copy(b * KVH, 1)
                with act.Fori(0, KVH - 1) as i:
                    att_head(i, False)
                att_head(KVH - 1, True)
                end_phase(act, b, 2)

                out_proj(b, 0, lambda j: ln_pair(j, (b * 2 + 1) * NC))
                end_phase(act, b, 3)

                act.wait_ge(s_loga.sem, s_loga.done(b))
                nc.scalar.activation(dec_e[:].rearrange("p (h c) -> p h c", h=2), ps[0:SH, 0:2, :], ACT.Exp).then_inc(own_act, 1)
                act.wait_ge(own_act, b + 1)
                nc.scalar.activation(dec_t[:], dec_e[:], ACT.Exp, scale=-1.0).then_inc(s_dec.sem, 1)

                def prep1(k):
                    def do():
                        act.wait_ge(f_wf.sem, f_wf.done(b * G1 + k))
                        split_hi(0, gu[k][0][:], gu_f[:])
                    return do

                def ssm_prep(h, w):
                    act.wait_ge(w_raw_in, 16 * (b * RAWS + G0 + KVH + G1 + h + 1))
                    act.wait_ge(s_xz.sem, s_xz.done((b * HP + h - 1) * NC - 1))
                    split_hi(0, w_in[w][0][:], w_raw[:, 0:KT * XZBC].rearrange("p (k c) -> p k c", k=KT))

                def first_pair():
                    act.wait_ge(dec_out, 16 * (b + 1))
                    ssm_prep(0, 0)
                prep1(0)()
                ffn_group(b, G0, 0, prep1(1))
                ffn_group(b, G0 + 1, 1, first_pair)
                gate_silu(b, GRP - 1)
                act.wait_ge(own_pool, b + 1)
                settle(act)
                end_phase(act, b, 4)

                def b_copy(u, hf):
                    act.wait_ge(s_pb.sem, s_pb.done(u))
                    act.wait_ge(s_sc.sem, s_sc.done(4 * u - 5))
                    nc.scalar.activation(bT[:, hf * HALF:(hf + 1) * HALF], ps[:, 0, :], ACT.Copy).then_inc(s_b.sem, 1)

                def c_copy(u, hf):
                    act.wait_ge(s_pc.sem, s_pc.done(u))
                    act.wait_ge(s_sc.sem, s_sc.done(4 * u - 5))
                    nc.scalar.activation(cTz[0:64, 0, hf * HALF:(hf + 1) * HALF], ps[0:64, 1, :], ACT.Copy)
                    nc.scalar.activation(cTz[64:P, 1, hf * HALF:(hf + 1) * HALF], ps[64:P, 1, :], ACT.Copy).then_inc(s_c.sem, 1)

                def btok_copy(u, hf):
                    act.wait_ge(s_trb.sem, s_trb.done(u))
                    act.wait_ge(s_y.sem, s_y.done(4 * u - 5))
                    nc.scalar.activation(b_tok[:, 4 * hf:4 * hf + 4, :], ps[:, 0, :].rearrange("p (c e) -> p c e", e=P), ACT.Copy).then_inc(s_btok.sem, 1)

                def xz_copy(m, c):
                    s = c % 2
                    act.wait_ge(s_xz.sem, s_xz.done(m))
                    act.wait_ge(s_y.sem, s_y.free(m, 2))
                    act.wait_ge(s_xd.sem, s_xd.free(m, 2))
                    nc.scalar.activation(xz_x[:, s, :].rearrange("p (h c) -> p h c", c=64)[:, 0:4:3, :],
                                         ps[:, 2 + s, 0:P].rearrange("p (h c) -> p h c", c=64), ACT.Copy)
                    act.wait_ge(s_out.sem, s_out.free(m, 2))
                    nc.scalar.activation(sz[:, s, :], ps[:, 2 + s, P:2 * P], ACT.Silu).then_inc(s_xcopy.sem, 1)

                def ssm_pairs(i, last_pairs):
                    for w in range(2):
                        n = b * HP + 2 * i + w
                        for c in range(NC):
                            u, m, hf = 2 * n + c // 4, n * NC + c, c // 4
                            unit_ahead = hf == 0 or w == 0 or not last_pairs
                            if c < NC - 1 or w == 0 or not last_pairs:
                                xz_copy(m + 1, (c + 1) % NC)
                            if c == 0 and (w == 0 or not last_pairs):
                                ssm_prep(2 * i + w + 1, 1 - w)
                            if unit_ahead and c % 4 == 1:
                                b_copy(u + 1, 1 - hf)
                            if unit_ahead and c % 4 == 2:
                                c_copy(u + 1, 1 - hf)
                            if unit_ahead and c % 4 == 3:
                                btok_copy(u + 1, 1 - hf)
                u = 2 * b * HP
                b_copy(u, 0)
                c_copy(u, 0)
                xz_copy(u * 4, 0)
                btok_copy(u, 0)
                with act.Fori(0, HP // 2 - 1) as i:
                    ssm_pairs(i, False)
                ssm_pairs(HP // 2 - 1, True)
                end_phase(act, b, 5)
                out_proj(b, 1, lambda j: None)
                end_phase(act, b, 6)

        @block.vector
        def _(dve):
            start(dve, "dve")

            def ln_stats(n, c, s):
                dve.wait_ge(ln_rstd.sem, ln_rstd.free(n, 2))
                settle(dve)
                nc.vector.bn_stats(ln_st[:, s, :], x_res[:, bass.ds(c, 1), :].rearrange("p a d -> p (a d)")).then_inc(ln_stat.sem, 1)
                dve.wait_ge(ln_stat.sem, ln_stat.done(n))
                dve.wait_ge(ln_xn.sem, ln_xn.free(n, 2))
                settle(dve)
                nc.vector.bn_aggr(ln_mv[:, s, :], ln_st[:, s, :]).then_inc(ln_var.sem, 1)

            def ln_norm(n, c, s):
                dve.wait_ge(ln_std.sem, ln_std.done(n))
                nc.vector.reciprocal(ln_rs[:, s, :], ln_sd[:, s, :]).then_inc(ln_rstd.sem, 1)
                dve.wait_ge(ln_rstd.sem, ln_rstd.done(n))
                dve.wait_ge(ln_var.sem, ln_var.done(n))
                dve.wait_ge(ln_tr.sem, ln_tr.free(n, 2))
                nc.vector.tensor_scalar(xn[:, s, :], x_res[:, bass.ds(c, 1), :].rearrange("p a d -> p (a d)"),
                                        ln_mv[:, s, 0:1], ln_rs[:, s, :], ALU.subtract, ALU.mult).then_inc(ln_xn.sem, 1)

            def ln_low(n, c, s):
                dve.wait_ge(ln_hi.sem, ln_hi.done(n))
                nc.vector.tensor_tensor(xnT[1][:, :, bass.ds(c * P, P)], ps[:, 6 + s, 0:DM].rearrange("p (k c) -> p k c", k=KT),
                                        xnT[0][:, :, bass.ds(c * P, P)], ALU.subtract).then_inc(ln_lo.sem, 1)

            def ln_pair(j, base):
                for s in range(2):
                    ln_stats(base + 2 * j + s, 2 * j + s, s)
                for s in range(2):
                    ln_norm(base + 2 * j + s, 2 * j + s, s)
                for s in range(2):
                    ln_low(base + 2 * j + s, 2 * j + s, s)

            def ffn_group(b, g, slot, experts, prep):
                for c in range(NC + 2):
                    if c < NC:
                        n = (b * GRP + g) * NC + c
                        if c == 0 and experts:
                            if slot is not None:
                                dve.wait_ge(f_hid.sem, f_hid.free(n, 1))
                            nc.vector.tensor_copy(combine_g[:, slot], combine[:, bass.ds(2 * g, 2), :]).then_inc(f_cg.sem, 1)
                            dve.wait_ge(f_cg.sem, f_cg.done(b * G0 + g))
                        dve.wait_ge(f_silu.sem, f_silu.done(n))
                        dve.wait_ge(f_tr.sem, f_tr.free(n, 2))
                        up = ps[:, 2 * (c % 2) + 1, :]
                        if experts:
                            for e in range(2):
                                ins = nc.vector.scalar_tensor_tensor(
                                    hid[:, c % 2, e * FE:(e + 1) * FE], up[:, e * FE:(e + 1) * FE], combine_g[:, slot, e, c:c + 1],
                                    silu_g[:, c % 2, e * FE:(e + 1) * FE], ALU.mult, ALU.mult)
                        else:
                            ins = nc.vector.tensor_tensor(hid[:, c % 2, 0:FG], up[:, 0:FG], silu_g[:, c % 2, :], ALU.mult)
                        ins.then_inc(f_hid.sem, 1)
                    if c >= 2:
                        n = (b * GRP + g) * NC + c - 2
                        dve.wait_ge(f_dn.sem, f_dn.done(n))
                        dve.wait_ge(f_acc.sem, f_acc.free(n, 8))
                        nc.vector.tensor_tensor(gate[:, c - 2, :], ps[:, 6 + c % 2, 0:DM], gate[:, c - 2, :], ALU.add).then_inc(f_acc.sem, 1)
                    if c == 3:
                        prep()

            def add_gated(n, c, s):
                dve.wait_ge(o_mm.sem, o_mm.done(n))
                dve.wait_ge(o_res.sem, o_res.free(n, 2))
                nc.vector.tensor_tensor(sg[:, s], ps[:, 4 + s, 0:DM], gate[:, bass.ds(c, 1), :].rearrange("p a d -> p (a d)"), ALU.mult).then_inc(o_sg.sem, 1)
                dve.wait_ge(o_sg.sem, o_sg.done(n))
                xc = x_res[:, bass.ds(c, 1), :].rearrange("p a d -> p (a d)")
                nc.vector.tensor_tensor(xc, sg[:, s], xc, ALU.add).then_inc(o_res.sem, 1)

            nc.vector.memset(ln_eps[:], LN_EPS)
            nc.vector.memset(att_state[:], 0.0)
            nc.vector.memset(ssm_state[:], 0.0)
            nc.vector.memset(combine[:, NE:2 * G0, :], 1.0)
            dve.wait_ge(init_step, 1)
            nc.vector.tensor_tensor(router[1][:].rearrange("p k c -> p (k c)"), x_res[:, 0, 0:KT * NE], router[0][:].rearrange("p k c -> p (k c)"), ALU.subtract)
            nc.vector.tensor_tensor(w_dec[1][:].rearrange("p k c -> p (k c)"), x_res[:, 1, :], w_dec[0][:].rearrange("p k c -> p (k c)"), ALU.subtract).then_inc(init_step, 1)
            with dve.Fori(0, B) as b:
                dve.wait_ge(x_in, 16 * (b + 1))
                settle(dve)
                with dve.Fori(0, NC // 2) as j:
                    ln_pair(j, b * 2 * NC)
                end_phase(dve, b, 0)

                r0 = b * 9

                def routed(k, ins):
                    ins.then_inc(rt_dve.sem, 1)
                    dve.wait_ge(rt_dve.sem, rt_dve.done(r0 + k))
                dve.wait_ge(rt_logits.sem, rt_logits.done(b))
                routed(0, nc.vector.tensor_copy(rt_l[:].rearrange("p c e -> p (c e)"), ps[:, 7, 0:NC * NE]))
                routed(1, nc.vector.tensor_reduce(rt_m[:], rt_l[:], AX.X, ALU.max))
                nc.vector.tensor_tensor(rt_l[:], rt_l[:], rt_m[:].unsqueeze(2).broadcast_to([P, NC, NE]), ALU.subtract).then_inc(rt_dve.sem, 1)
                dve.wait_ge(rt_exp.sem, rt_exp.done(b))
                routed(3, nc.vector.tensor_reduce(rt_s[:], rt_l[:], AX.X, ALU.add))
                routed(4, nc.vector.reciprocal(rt_m[:], rt_s[:]))
                routed(5, nc.vector.tensor_tensor(rt_l[:], rt_l[:], rt_m[:].unsqueeze(2).broadcast_to([P, NC, NE]), ALU.mult))
                rival = rt_l[:].unsqueeze(2).broadcast_to([P, NC, NE, NE])
                score = rt_l[:].unsqueeze(3).broadcast_to([P, NC, NE, NE])
                nc.vector.tensor_tensor(rt_gt[:].rearrange("p (c e) j -> p c e j", c=NC), rival, score, ALU.is_gt)
                routed(6, nc.vector.tensor_tensor(rt_eq[:].rearrange("p (c e) j -> p c e j", c=NC), rival, score, ALU.is_equal))
                first = earlier[:].rearrange("p (e j) -> p e j", e=NE).unsqueeze(1).broadcast_to([P, NC, NE, NE])
                routed(7, nc.vector.tensor_tensor(rt_eq[:].rearrange("p (c e) j -> p c e j", c=NC), rt_eq[:].rearrange("p (c e) j -> p c e j", c=NC), first, ALU.mult))
                routed(8, nc.vector.tensor_tensor(rt_gt[:], rt_gt[:], rt_eq[:], ALU.add))
                nc.vector.tensor_reduce(rt_rank[:], rt_gt[:], AX.X, ALU.add).then_inc(own_dve, 1)
                dve.wait_ge(own_dve, 2 * b + 1)
                nc.vector.scalar_tensor_tensor(combine[:, 0:NE, :].rearrange("p e c -> p c e"), rt_rank[:].rearrange("p (c e) -> p c e", c=NC), 1.5,
                                               rt_l[:], ALU.is_lt, ALU.mult).then_inc(own_dve, 1)
                dve.wait_ge(own_dve, 2 * b + 2)
                dve.wait_ge(gate_zero.sem, gate_zero.done(2 * b))
                settle(dve)

                with dve.Fori(0, G0 // 2) as i:
                    for k in range(2):
                        ffn_group(b, 2 * i + k, k, True, lambda: None)
                ffn_group(b, G0 - 1, 0, True, lambda: None)
                end_phase(dve, b, 1)

                dve.wait_ge(tables_in, 32 * (b + 1))
                settle(dve)
                def rope_mul(n, hf, r):
                    u = 2 * n + hf
                    t, k = (0 if r == 0 else r + 1), (hf * ROT + r) % 2
                    toks = slice(hf * HALF, (hf + 1) * HALF)
                    dve.wait_ge(a_proj.sem, a_proj.done(u * (REP + 2) + t))
                    dve.wait_ge(a_qk.sem, a_qk.done(u * ROT + r - 2))
                    nc.vector.tensor_tensor(ra[:, k], ps[:, t % 2, :], cos[:, toks], ALU.mult)
                    nc.vector.tensor_tensor(rb[0:64, k], ps[64:P, t % 2, :], sin[0:64, toks], ALU.mult)
                    nc.vector.tensor_tensor(rb[64:P, k], ps[0:64, t % 2, :], sin[64:P, toks], ALU.mult).then_inc(a_mul.sem, 1)

                def feature(n, hf, r):
                    u = 2 * n + hf
                    k = (hf * ROT + r) % 2
                    toks = slice(hf * HALF, (hf + 1) * HALF)
                    if r == 0:
                        dve.wait_ge(a_sc.sem, a_sc.done(4 * u - 5))
                    if r == 1:
                        dve.wait_ge(a_nd.sem, a_nd.done(4 * u - 5))
                    dve.wait_ge(a_act.sem, a_act.done(u * ROT + r))
                    dst = kT[:, toks] if r == 0 else qT[:, r - 1, toks]
                    nc.vector.scalar_tensor_tensor(dst, rb[:, k], 0.0, ra[:, k], ALU.max, ALU.add).then_inc(a_qk.sem, 1)

                def mask(n, c):
                    m = n * NC + c
                    dve.wait_ge(a_sc.sem, a_sc.done(m))
                    dve.wait_ge(a_nd.sem, a_nd.done(m - 2))
                    nc.vector.tensor_tensor(mt[:, c % 2].rearrange("p (h t) -> p h t", h=REP), ps[:, 2 + c % 2, :].rearrange("p (h t) -> p h t", h=REP),
                                            causal[:].unsqueeze(1).broadcast_to([P, REP, P]), ALU.mult).then_inc(a_mt.sem, 1)

                def att_next_state(n, c):
                    m = n * NC + c
                    nxt = att_state[:, (c + 1) % 2, :]
                    dve.wait_ge(a_nd.sem, a_nd.done(m - 1))
                    dve.wait_ge(a_st.sem, a_st.done(m - 1))
                    if c == NC - 1:
                        nc.vector.memset(nxt, 0.0).then_inc(a_st.sem, 1)
                        return
                    dve.wait_ge(a_up.sem, a_up.done(n * (NC - 1) + c))
                    nc.vector.tensor_tensor(nxt, ps[:, 6, 0:P + 1], att_state[:, c % 2, :], ALU.add).then_inc(a_st.sem, 1)

                def att_head(i, last):
                    n = b * KVH + i
                    for hf in range(2):
                        q_ahead, kv_ahead = not last or hf == 0, not last
                        nxt = (n + hf, 1 - hf)
                        c = 4 * hf
                        mask(n, c + 1)
                        if q_ahead:
                            rope_mul(*nxt, 1)
                        att_next_state(n, c)
                        if q_ahead:
                            rope_mul(*nxt, 2)
                            feature(*nxt, 1)
                        mask(n, c + 2)
                        if q_ahead:
                            rope_mul(*nxt, 3)
                            feature(*nxt, 2)
                        att_next_state(n, c + 1)
                        if q_ahead:
                            rope_mul(*nxt, 4)
                            feature(*nxt, 3)
                        mask(n, c + 3)
                        att_next_state(n, c + 2)
                        if q_ahead:
                            feature(*nxt, 4)
                        if kv_ahead:
                            rope_mul(n + 1, hf, 0)
                        att_next_state(n, c + 3)
                        if kv_ahead:
                            feature(n + 1, hf, 0)
                        if q_ahead:
                            mask(n + hf, (c + 4) % NC)
                rope_mul(b * KVH, 0, 0)
                for r in range(1, ROT):
                    rope_mul(b * KVH, 0, r)
                    feature(b * KVH, 0, r - 1)
                feature(b * KVH, 0, REP)
                rope_mul(b * KVH, 1, 0)
                mask(b * KVH, 0)
                feature(b * KVH, 1, 0)
                with dve.Fori(0, KVH - 1) as i:
                    att_head(i, False)
                att_head(KVH - 1, True)
                end_phase(dve, b, 2)

                with dve.Fori(0, NC // 2) as j:
                    for s in range(2):
                        c = 2 * j + s
                        n = b * 2 * NC + c
                        dve.wait_ge(o_yn.sem, o_yn.free(4 * n, 8) + 3)
                        nc.vector.tensor_scalar(rin[:, s, :], den[:, bass.ds(c, 1), :].rearrange("p a d -> p (a d)"), DEN_EPS, None, ALU.add).then_inc(rin_step, 1)
                        dve.wait_ge(rin_step, 2 * (b * NC + c) + 1)
                        nc.vector.reciprocal(rin2[:, s, :], rin[:, s, :]).then_inc(rin_step, 1)
                        dve.wait_ge(rin_step, 2 * (b * NC + c) + 2)
                        for q in range(4):
                            dve.wait_ge(o_tr.sem, o_tr.free(4 * n + q, 8))
                            nc.vector.tensor_tensor(yn[:, s, q * HALF:(q + 1) * HALF].rearrange("p (h e) -> p h e", e=P),
                                                    y[:, bass.ds(c, 1), q * HALF:(q + 1) * HALF].rearrange("p a (h e) -> p (a h) e", e=P),
                                                    rin2[:, s, 4 * q:4 * q + 4].unsqueeze(2).broadcast_to([P, 4, P]), ALU.mult).then_inc(o_yn.sem, 1)
                    for s in range(2):
                        add_gated(b * 2 * NC + 2 * j + s, 2 * j + s, s)
                    dve.wait_ge(o_res.sem, o_res.done(b * 2 * NC + 2 * j + 1))
                    ln_pair(j, (b * 2 + 1) * NC)
                end_phase(dve, b, 3)

                def dequant(k):
                    def do():
                        if k == 0:
                            dve.wait_ge(scales_in, 48 * (b + 1))
                        dve.wait_ge(w_raw_in, 16 * (b * RAWS + G0 + KVH + k + 1))
                        dve.wait_ge(w_split.sem, w_split.done(split_ffn1(b, k) - 1))
                        for kk in range(KT):
                            ins = nc.vector.scalar_tensor_tensor(
                                gu_f[:, kk], w_raw[:, kk * 2 * FG:(kk + 1) * 2 * FG].bitcast(I32), ZERO_POINT,
                                s_gu[:, k], ALU.subtract, ALU.mult)
                        ins.then_inc(f_wf.sem, 1)
                        dve.wait_ge(dn_in[k], 16 * (b * (4 - k) + 4 - k))
                        nc.vector.scalar_tensor_tensor(dn_f[:, k], dn_raw[:, k].bitcast(I32), ZERO_POINT,
                                                       s_dn[:].unsqueeze(1).broadcast_to([P, DT, DM]), ALU.subtract, ALU.mult).then_inc(dn_made.sem, 1)
                    return do
                dequant(0)()
                dve.wait_ge(gate_zero.sem, gate_zero.done(2 * b + 1))
                ffn_group(b, G0, 0, False, dequant(1))
                ffn_group(b, G0 + 1, 1, False, lambda: None)
                def decay_start(n, hf):
                    u = 2 * n + hf
                    toks = slice(hf * HALF, (hf + 1) * HALF)
                    dve.wait_ge(dec_in[hf], 16 * (n + 1))
                    dve.wait_ge(s_scan.sem, s_scan.done(u - 2))
                    for h in range(2):
                        q = slice(64 * h, 64 * h + 64)
                        ins = nc.vector.tensor_copy(dstart[q, toks].rearrange("p (c t) -> p c t", t=P)[:, :, 0],
                                                    dec[q, h, toks].rearrange("p (c t) -> p c t", t=P)[:, :, 0])
                    ins.then_inc(s_prep, 1)
                    dve.wait_ge(s_prep, 2 * u + 1)
                    nc.vector.memset(dec[:, :, toks].rearrange("p h (c t) -> p h c t", t=P)[:, :, :, 0:1], 0.0).then_inc(s_prep, 1)

                def decay_scan(n, hf, h):
                    u = 2 * n + hf
                    toks = slice(hf * HALF, (hf + 1) * HALF)
                    dve.wait_ge(s_prep, 2 * u + 2)
                    if h == 0:
                        dve.wait_ge(s_mt.sem, s_mt.done(4 * u - 5))
                        dve.wait_ge(s_xw.sem, s_xw.done(4 * u - 5))
                    nc.vector.tensor_tensor_scan(lmat[:, h, toks], dec[:, h, toks], ident4[:, 0:HALF], 0.0, ALU.mult, ALU.add)

                def decay_from_start(n, hf):
                    u = 2 * n + hf
                    toks = slice(hf * HALF, (hf + 1) * HALF)
                    dve.wait_ge(s_st.sem, s_st.done(4 * u - 5))
                    dve.wait_ge(s_cp.sem, s_cp.done(u - 2))
                    for h in range(2):
                        q = slice(64 * h, 64 * h + 64)
                        ins = nc.vector.tensor_tensor_scan(pdec[q, toks], dec[q, h, toks], dstart[q, toks], 0.0, ALU.mult, ALU.add)
                    ins.then_inc(s_scan.sem, 1)

                def c_decayed(n, hf):
                    u = 2 * n + hf
                    toks = slice(hf * HALF, (hf + 1) * HALF)
                    dve.wait_ge(s_scan.sem, s_scan.done(u))
                    dve.wait_ge(s_c.sem, s_c.done(u))
                    dve.wait_ge(s_y.sem, s_y.done(4 * u - 5))
                    nc.vector.tensor_tensor(cTp[:, toks], ps[:, 1, :], pdec[:, toks], ALU.mult).then_inc(s_cp.sem, 1)

                def x_weighted(m, c):
                    s = c % 2
                    dve.wait_ge(s_xcopy.sem, s_xcopy.done(m))
                    dve.wait_ge(s_y.sem, s_y.free(m, 2))
                    last = lmat[:, :, (c + 1) * P - 1:(c + 1) * P].broadcast_to([P, 2, 64])
                    nc.vector.tensor_tensor(xw[:, s].rearrange("p (h c) -> p h c", c=64), ps[:, 2 + s, 0:P].rearrange("p (h c) -> p h c", c=64),
                                            last, ALU.mult).then_inc(s_xw.sem, 1)

                def decayed_scores(m, c):
                    s = c % 2
                    dve.wait_ge(s_sc.sem, s_sc.done(m))
                    dve.wait_ge(s_y.sem, s_y.free(m, 2))
                    nc.vector.tensor_tensor(mt1[:, s].rearrange("p (h c) -> p h c", h=2), ps[:, 4 + s, 0:2 * P].rearrange("p (h c) -> p h c", h=2),
                                            lmat[:, :, c * P:(c + 1) * P], ALU.mult).then_inc(s_mt.sem, 1)

                def ssm_next_state(n, m, c):
                    nxt, cur = (c + 1) % 2, c % 2
                    dve.wait_ge(s_y.sem, s_y.done(m - 1))
                    dve.wait_ge(s_st.sem, s_st.done(m - 1))
                    if c == NC - 1:
                        nc.vector.memset(ssm_state[:, nxt, :], 0.0).then_inc(s_st.sem, 1)
                        return
                    dve.wait_ge(s_up.sem, s_up.done(n * (NC - 1) + c))
                    for h in range(2):
                        q = slice(64 * h, 64 * h + 64)
                        ins = nc.vector.scalar_tensor_tensor(ssm_state[q, nxt, q], ssm_state[q, cur, q], pdec[q, (c + 1) * P - 1:(c + 1) * P],
                                                             ps[q, 7, q], ALU.mult, ALU.add)
                    ins.then_inc(s_st.sem, 1)

                def add_skip(m, c):
                    s = c % 2
                    dve.wait_ge(s_y.sem, s_y.done(m))
                    dve.wait_ge(s_xd.sem, s_xd.done(m))
                    dve.wait_ge(s_out.sem, s_out.free(m, 2))
                    nc.vector.tensor_tensor(yg[:, s], ps[:, 6, 0:P], xd[:, s], ALU.add).then_inc(s_yg.sem, 1)

                def ssm_pairs(i, last_pairs):
                    for w in range(2):
                        n = b * HP + 2 * i + w
                        for c in range(NC):
                            m, hf = n * NC + c, c // 4
                            unit_ahead = hf == 0 or w == 0 or not last_pairs
                            if c < NC - 1 or w == 0 or not last_pairs:
                                x_weighted(m + 1, (c + 1) % NC)
                                decayed_scores(m + 1, (c + 1) % NC)
                            ssm_next_state(n, m, c)
                            add_skip(m, c)
                            if not unit_ahead:
                                continue
                            after = (n + hf, 1 - hf)
                            if c % 4 == 0:
                                decay_start(*after)
                                decay_scan(*after, 0)
                            if c % 4 == 1:
                                decay_scan(*after, 1)
                            if c % 4 == 2:
                                decay_from_start(*after)
                                c_decayed(*after)
                dve.wait_ge(own_pool, b + 1)
                decay_start(b * HP, 0)
                for h in range(2):
                    decay_scan(b * HP, 0, h)
                decay_from_start(b * HP, 0)
                end_phase(dve, b, 4)
                c_decayed(b * HP, 0)
                x_weighted(b * HP * NC, 0)
                decayed_scores(b * HP * NC, 0)
                with dve.Fori(0, HP // 2 - 1) as i:
                    ssm_pairs(i, False)
                ssm_pairs(HP // 2 - 1, True)
                end_phase(dve, b, 5)

                with dve.Fori(0, NC // 2) as j:
                    for s in range(2):
                        c = 2 * j + s
                        n = b * NC + c
                        n4 = 4 * ((b * 2 + 1) * NC + c)
                        yc = y[:, bass.ds(c, 1), :].rearrange("p a d -> p (a d)")
                        dve.wait_ge(o_yn.sem, o_yn.free(n4, 8) + 3)
                        settle(dve)
                        for q in range(4):
                            ins = nc.vector.bn_stats(in_st[:, s, 6 * q:6 * q + 6], yc[:, q * HALF:(q + 1) * HALF])
                        ins.then_inc(rin_step2, 1)
                        dve.wait_ge(rin_step2, 2 * n + 1)
                        settle(dve)
                        nc.vector.bn_aggr(in_mv[:, s, :], in_st[:, s, :]).then_inc(o_stat.sem, 1)
                        dve.wait_ge(o_std.sem, o_std.done(n))
                        nc.vector.reciprocal(in_rs[:, s, :], in_sd[:, s, :]).then_inc(rin_step2, 1)
                        dve.wait_ge(rin_step2, 2 * n + 2)
                        for q in range(4):
                            dve.wait_ge(o_tr.sem, o_tr.free(n4 + q, 8))
                            nc.vector.tensor_scalar(yn[:, s, q * HALF:(q + 1) * HALF], yc[:, q * HALF:(q + 1) * HALF],
                                                    in_mv[:, s, 0:1], in_rs[:, s, :], ALU.subtract, ALU.mult).then_inc(o_yn.sem, 1)
                    for s in range(2):
                        add_gated((b * 2 + 1) * NC + 2 * j + s, 2 * j + s, s)
                end_phase(dve, b, 6)


def launch_arrays(inputs):
    f = {k: np.asarray(v) for k, v in inputs.items()}

    def rows_to_k(w):
        return np.ascontiguousarray(w.T).reshape(-1, P, w.shape[0]).transpose(1, 0, 2)

    g = {}
    g["x"] = f["L0_attn_x"]
    Wq, Wk, Wv = f["L0_attn_Wq"], f["L0_attn_Wk"], f["L0_attn_Wv"]
    g["w_qkv"] = np.stack([rows_to_k(np.concatenate([Wk[i * P:(i + 1) * P], Wv[i * P:(i + 1) * P], Wq[i * REP * P:(i + 1) * REP * P]])).reshape(P, -1)
                           for i in range(KVH)])
    g["w_o"] = rows_to_k(f["L0_attn_Wo"])
    g["router"] = np.concatenate([rows_to_k(f["L0_ffn_gate_weight"]).reshape(P, -1), np.zeros((P, DM - KT * NE), np.float32)], 1)

    def groups(gate_up, down):
        gus = np.stack([rows_to_k(x).reshape(P, -1) for x in gate_up])
        dns = np.stack([rows_to_k(np.concatenate([x, np.zeros((DM, DT * P - FG), x.dtype)], 1)).reshape(P, -1) for x in down])
        return gus, dns
    gw, dw = f["L0_ffn_gate_up_weights"], f["L0_ffn_down_weights"]
    sgu, sdn = f["L0_ffn_shared_gate_up"], f["L0_ffn_shared_down"]
    g["gu0"], g["dn0"] = groups(
        [np.concatenate([gw[e, :FE], gw[e + 1, :FE], gw[e, FE:], gw[e + 1, FE:]]) for e in range(0, NE, 2)] + [sgu],
        [np.concatenate([dw[e], dw[e + 1]], 1) for e in range(0, NE, 2)] + [sdn])
    qg, qu, qd = f["L1_ffn_wq_gate"], f["L1_ffn_wq_up"], f["L1_ffn_wq_down"]
    g["gu1"], g["dn1"] = groups(
        [np.concatenate([qg[k * FG:(k + 1) * FG], qu[k * FG:(k + 1) * FG]]) for k in range(G1)],
        [qd[:, k * FG:(k + 1) * FG] for k in range(G1)])
    g["s_gu"] = np.stack([np.concatenate([f["L1_ffn_s_gate"][k * FG:(k + 1) * FG], f["L1_ffn_s_up"][k * FG:(k + 1) * FG]]) for k in range(G1)])
    g["s_dn"] = f["L1_ffn_s_down"].reshape(1, DM)
    W = f["L1_attn_W_in"]
    parts = [W[k * INNER:(k + 1) * INNER] for k in range(4)]
    g["w_in"] = np.stack([rows_to_k(np.concatenate([w[h * P:(h + 1) * P] for w in parts])).reshape(P, -1) for h in range(HP)])
    g["w_dec"] = rows_to_k(np.concatenate([W[4 * INNER:], np.zeros((P - SH, DM), np.float32)])).reshape(P, -1)
    g["w_out"] = rows_to_k(f["L1_attn_W_out"])
    g["gamma"] = np.ascontiguousarray(f["L1_attn_gamma"].reshape(NT, P).T)
    g["beta"] = np.ascontiguousarray(f["L1_attn_beta"].reshape(NT, P).T)
    g["d_skip"] = f["L1_attn_D"].reshape(HP, P)

    eye = np.eye(P, dtype=np.float32)
    g["ident4"] = np.tile(eye, (1, HALF // P))
    g["causal"] = np.triu(np.ones((P, P), np.float32))
    g["earlier"] = np.tile((np.arange(NE)[None, :] < np.arange(NE)[:, None]).astype(np.float32).reshape(1, -1), (P, 1))
    inv = (np.float32(1.0) / np.power(np.float32(10000.0), np.arange(0, P, 2, dtype=np.float32) / np.float32(P))).astype(np.float32)
    ang = np.outer(np.arange(T, dtype=np.float32), inv).astype(np.float32).astype(np.float64)
    c, s = np.cos(ang).T.astype(np.float32), np.sin(ang).T.astype(np.float32)
    g["cos"] = np.concatenate([c, c])
    g["sin"] = np.concatenate([-s, s])
    return {k: np.ascontiguousarray(v) for k, v in g.items()}


def kernel(**inputs):
    import concourse.bacc as bacc
    from concourse.bass_utils import run_bass_kernel_spmd

    nc = bacc.Bacc("TRN2", target_bir_lowering=False, num_devices=1)
    arrays = launch_arrays(inputs)
    aps = {k: nc.dram_tensor(f"in_{k}", v.shape, mybir.dt.from_np(v.dtype), kind="ExternalInput").ap() for k, v in arrays.items()}
    aps["out"] = nc.dram_tensor("out_x", (B, T, DM), F32, kind="ExternalOutput").ap()
    build(nc, aps)
    r = run_bass_kernel_spmd(nc, [{f"in_{k}": v for k, v in arrays.items()}], core_ids=[0])
    return r.results[0]["out_x"]
```

```python
from contextlib import ExitStack

import numpy as np

import concourse.bass as bass
from concourse import mybir

P = 128
F32 = mybir.dt.float32
F32R = mybir.dt.float32r
I32 = mybir.dt.int32
ALU = mybir.AluOpType
ACT = mybir.ActivationFunctionType
AX = mybir.AxisListType

B = 2
T = 1024
DM = 256
KT = DM // P
NC = T // P
HALF = 512
INNER = 2048
NT = INNER // P

KVH, REP = 4, 4
ROT = REP + 1
QKV = (REP + 2) * P
NE = 8
FE = 176
FG = 2 * FE
G0, G1 = NE // 2 + 1, 2
GRP = G0 + G1
DT = 3

HP = 16
XZBC = 4 * P
EARLY = 3
SH = 32

LN_EPS = 1e-5
DEN_EPS = 1e-6
ZERO_POINT = 128.0
SPLITS = ((0, 0), (0, 1), (1, 0))
PHASES = 7
CONSTS = 7
RAWS = G0 + KVH + G1 + HP
PARTS = 3


def split_ffn0(b, g):
    return b * (RAWS + (PARTS - 1) * KVH) + g


def split_qkv(b, i, part):
    return split_ffn0(b, G0) + PARTS * i + part


def split_ffn1(b, k):
    return split_qkv(b, KVH, 0) + k


def split_ssm(b, h):
    return split_ffn1(b, G1) + h


class Event:

    def __init__(self, sem, credit):
        self.sem, self.credit = sem, credit

    def done(self, n):
        return n + 1 + self.credit

    def free(self, n, depth):
        return n + 1 + self.credit - depth


def following(g, c, steps):
    return (g, c + steps) if c + steps < NC else (g + 1, c + steps - NC)


def build(nc, a):
    with ExitStack() as ctx:
        events = {}

        def event(name, owner, credit=16):
            e = Event(ctx.enter_context(nc.semaphore(name)), credit)
            events.setdefault(owner, []).append(e)
            return e

        def sem(name):
            return ctx.enter_context(nc.semaphore(name))

        def fixed(name, shape, dt=F32):
            return ctx.enter_context(nc.sbuf_tensor(name, shape, dt))

        x_res = fixed("x_res", [P, NC, DM])
        gate = fixed("gate", [P, NC, DM])
        xnT = [fixed(f"xnT_{s}", [P, KT, T], F32R) for s in ("hi", "lo")]
        ident4 = fixed("ident4", [P, HALF])
        causal = fixed("causal", [P, P])
        earlier = fixed("earlier", [P, NE * NE])
        w_out = fixed("w_out", [P, NT, DM])
        w_raw = fixed("w_raw", [P, KT * QKV])
        dn_raw = fixed("dn_raw", [P, 2, DT, DM])
        xn = fixed("xn", [P, 2, DM])
        router = [fixed(f"router_{s}", [P, KT, NE], F32R) for s in ("hi", "lo")]
        w_dec = [fixed(f"w_dec_{s}", [P, KT, P], F32R) for s in ("hi", "lo")]
        combine = fixed("combine", [P, 2 * G0, NC])
        combine_g = fixed("combine_g", [P, 2, 2, NC])
        den = fixed("den", [P, NC, KVH * REP])
        att_state = fixed("att_state", [P, 2, P + 1])
        ssm_state = fixed("ssm_state", [P, 2, P])
        ln_st = fixed("ln_st", [P, NC, 6])
        ln_mv = fixed("ln_mv", [P, NC, 2])
        ln_sd = fixed("ln_sd", [P, NC, 1])
        ln_rs = fixed("ln_rs", [P, NC, 1])
        eps = fixed("eps", [P, 1])
        in_st = fixed("in_st", [P, 2, 4 * 6])
        in_mv = fixed("in_mv", [P, 2, 2])
        in_sd = fixed("in_sd", [P, 2, 1])
        in_rs = fixed("in_rs", [P, 2, 1])
        gamma = fixed("gamma", [P, NT])
        beta = fixed("beta", [P, NT])

        def group():
            made = ExitStack()

            def shared(name, shape, dt=F32):
                return made.enter_context(nc.sbuf_tensor(name, shape, dt))
            return made, shared

        done, shared = group()
        y = shared("y", [P, NC, INNER])
        y_bytes_end = nc.sbuf_base
        done.close()
        done, shared = group()
        gu = [[shared(f"gu_{s}{k}", [P, KT, 2 * FG], F32R) for s in ("hi", "lo")] for k in range(2)]
        dn = [[shared(f"dn_{s}{k}", [P, DT, DM], F32R) for s in ("hi", "lo")] for k in range(2)]
        dn_f = shared("dn_f", [P, DT, DM])
        s_gu1 = shared("s_gu1", [P, 2 * FG])
        silu_g = shared("silu_g", [P, 2, FG])
        hid = shared("hid", [P, 2, DT * P])
        hidT = [shared(f"hidT_{s}", [P, 2, DT * P], F32R) for s in ("hi", "lo")]
        rt_l = shared("rt_l", [P, NC, NE])
        rt_T = shared("rt_T", [NE, T])
        rt_m = shared("rt_m", [P, NC])
        rt_s = shared("rt_s", [P, NC])
        rt_gt = shared("rt_gt", [P, NC * NE, NE])
        rt_eq = shared("rt_eq", [P, NC * NE, NE])
        rt_rank = shared("rt_rank", [P, NC * NE])
        assert nc.sbuf_base <= y_bytes_end
        done.close()
        ctx.enter_context(nc.sbuf_tensor("y_place", [P, NC * INNER], F32))

        done, shared = group()
        w_qkv = [shared(f"w_qkv_{s}", [P, KT, QKV], F32R) for s in ("hi", "lo")]
        qT = shared("qT", [P, REP, T])
        kT = shared("kT", [P, T])
        k_tok = shared("k_tok", [P, NC, P])
        v_tok = shared("v_tok", [P, NC, P + 1])
        vT = shared("vT", [P, HALF])
        cos = shared("cos", [P, T])
        sin = shared("sin", [P, T])
        ra = shared("ra", [P, 2, HALF])
        rb = shared("rb", [P, 2, HALF])
        mt = shared("mt", [P, 2, REP * P])
        done.close()
        done, shared = group()
        w_in = [[shared(f"w_in_{s}0", [P, KT, XZBC], F32R) for s in ("hi", "lo")]]
        cTz = shared("cTz", [P, 2, T])
        dec = shared("dec", [P, 2, T])
        lmat = shared("lmat", [P, 2, T])
        pdec = shared("pdec", [P, T])
        dstart = shared("dstart", [P, T])
        xz_x = shared("xz_x", [P, 2, 2 * P])
        d_row = shared("d_row", [P, 2, P])
        ssm_early_end = nc.sbuf_base
        w_in.append([shared(f"w_in_{s}1", [P, KT, XZBC], F32R) for s in ("hi", "lo")])
        bT = shared("bT", [P, T])
        cTp = shared("cTp", [P, T])
        b_tok = shared("b_tok", [P, NC, P])
        sz = shared("sz", [P, 2, P])
        xw = shared("xw", [P, 2, P])
        xd = shared("xd", [P, 2, P])
        yg = shared("yg", [P, 2, P])
        mt1 = shared("mt1", [P, 2, 2 * P])
        done.close()
        done, shared = group()
        dec_e = shared("dec_e", [SH, T])
        dec_t = shared("dec_t", [SH, T])
        done.close()
        done, shared = group()
        pad = (ssm_early_end - nc.sbuf_base) // 4
        shared("below", [P, pad])
        gu1 = [shared(f"gu1_{s}", [P, KT, 2 * FG], F32R) for s in ("hi", "lo")]
        gu_f = shared("gu_f", [P, KT, 2 * FG])
        s_gu0 = shared("s_gu0", [P, 2 * FG])
        s_dn = shared("s_dn", [P, DM])
        done.close()
        done, shared = group()
        yn = shared("yn", [P, 2, INNER])
        yT = shared("yT", [P, 2, NT, P])
        sg = shared("sg", [P, 2, DM])
        rin = shared("rin", [P, 2, NT])
        rin2 = shared("rin2", [P, 2, NT])
        assert nc.sbuf_base <= ssm_early_end
        done.close()

        ps = ctx.enter_context(nc.psum_tensor("ps", [P, 8, 512], F32))
        dec_dram = nc.dram_tensor("dec_dram", (SH, T), F32, kind="Internal").ap()

        consts_in, w_raw_in, tables_in = sem("consts_in"), sem("w_raw_in"), sem("tables_in")
        x_in = [sem(f"x_in{j}") for j in range(NC // 2)]
        dn_in = [sem("dn_in0"), sem("dn_in1")]
        w_out_in, scale0_in, scales_in = sem("w_out_in"), sem("scale0_in"), sem("scales_in")
        dec_in, dec_out, d_in = [sem("dec_in0"), sem("dec_in1")], sem("dec_out"), [sem("d_in0"), sem("d_in1")]
        stored = [sem(f"stored{j}") for j in range(NC // 2)]
        phase_end = sem("phase_end")
        init_step, settled = sem("init_step"), sem("settled")
        own_dve, own_act, own_pool = sem("own_dve"), sem("own_act"), sem("own_pool")
        rin_step, rin_step2, s_prep = sem("den_step"), sem("inner_ln_step"), sem("dec_prep")

        w_split = event("w_split", "pool")
        w_hi = event("w_hi", "act")
        ln_stat, ln_var = event("ln_stat", "dve"), event("ln_var", "dve")
        ln_std, ln_rstd = event("ln_std", "act"), event("ln_rstd", "dve")
        ln_xn, ln_tr = event("ln_xn", "dve"), event("ln_tr", "pe")
        ln_hi, ln_lo = event("ln_hi", "act"), event("ln_lo", "dve")
        rt_mm, rt_copy = event("rt_mm", "pe"), event("rt_copy", "act")
        rt_logits, rt_dve, rt_exp = event("rt_logits", "pe"), event("rt_dve", "dve"), event("rt_exp", "act")
        gate_zero = event("gate_zero", "pool")
        f_wf = event("f_wf", "dve")
        f_gu, f_silu, f_hid = event("f_gu", "pe"), event("f_silu", "act"), event("f_hid", "dve")
        f_tr, f_hidT, f_dn, f_acc = event("f_tr", "pe"), event("f_hidT", "act"), event("f_dn", "pe"), event("f_acc", "dve")
        f_cg = event("f_cg", "dve")
        f_low = event("f_low", "dve")
        dn_made, dn_hi, dn_lo = event("dn_made", "dve"), event("dn_hi", "act"), event("dn_lo", "dve")
        a_proj = event("a_proj", "pe")
        a_mul, a_rot, a_act, a_qk = event("a_mul", "dve"), event("a_rot", "pool"), event("a_act", "act"), event("a_qk", "dve")
        a_neg = event("a_neg", "act")
        a_vT, a_trk, a_trv, a_kv = event("a_vT", "act"), event("a_trk", "pe"), event("a_trv", "pe"), event("a_kv", "act")
        a_sc, a_mt, a_up, a_st = event("a_sc", "pe"), event("a_mt", "dve"), event("a_up", "pe"), event("a_st", "dve")
        a_nd, a_out = event("a_nd", "pe"), event("a_out", "act")
        s_loga, s_dec = event("s_loga", "pe"), event("s_dec", "act")
        s_scan = event("s_scan", "dve")
        s_pb, s_pc, s_b, s_c = event("s_pb", "pe"), event("s_pc", "pe"), event("s_b", "act"), event("s_c", "act")
        s_cp, s_trb, s_btok = event("s_cp", "dve"), event("s_trb", "pe"), event("s_btok", "act")
        s_xz, s_xcopy, s_xw, s_xd = event("s_xz", "pe"), event("s_xcopy", "act"), event("s_xw", "dve"), event("s_xd", "pool")
        s_sc, s_mt, s_up, s_st = event("s_sc", "pe"), event("s_mt", "dve"), event("s_up", "pe"), event("s_st", "dve")
        s_y, s_yg, s_out = event("s_y", "pe"), event("s_yg", "dve"), event("s_out", "pool")
        o_var, o_std, o_rstd = event("o_var", "dve"), event("o_std", "act"), event("o_rstd", "dve")
        o_yn, o_tr, o_yT = event("o_yn", "dve"), event("o_tr", "pe"), event("o_yT", "act")
        o_mm, o_sg, o_res = event("o_mm", "pe"), event("o_sg", "dve"), event("o_res", "dve")

        def start(eng, owner):
            for e in events[owner]:
                eng.sem_inc(e.sem, e.credit)

        def end_phase(eng, b, phase):
            eng.drain().then_inc(phase_end, 1)
            eng.wait_ge(phase_end, 4 * (b * PHASES + phase + 1))
            settle(eng)

        def settle(eng):
            eng.sem_inc(settled, 1)

        block = ctx.enter_context(nc.Block())

        @block.sync
        def _(sp):
            def weights(n, src, cols):
                sp.wait_ge(w_split.sem, w_split.done(n - 1))
                sp.dma_start(w_raw[:, 0:cols], src).then_inc(w_raw_in, 16)

            def down(slot, src):
                sp.dma_start(dn_raw[:, slot], src).then_inc(dn_in[slot], 16)

            def down_split(b, g):
                sp.wait_ge(dn_lo.sem, dn_lo.done(b * GRP + g))

            def phase_over(b, phase):
                sp.wait_ge(phase_end, 4 * (b * PHASES + phase + 1))
                settle(sp)

            for j in range(NC // 2):
                sp.sem_inc(stored[j], 16)
            for dst, src in ((ident4, a["ident4"]), (causal, a["causal"]), (earlier, a["earlier"]),
                             (gamma, a["gamma"]), (beta, a["beta"])):
                sp.dma_start(dst[:], src).then_inc(consts_in, 16)
            sp.dma_start(gate[:, 0, :], a["router"]).then_inc(consts_in, 16)
            sp.dma_start(gate[:, 1, :], a["w_dec"]).then_inc(consts_in, 16)
            with sp.Fori(0, B) as b:
                for j in range(NC // 2):
                    sp.wait_ge(stored[j], 16 * (b + 1))
                    settle(sp)
                    sp.dma_start(x_res[:, 2 * j:2 * j + 2, :],
                                 a["x"][bass.ds(b, 1), 2 * j * P:(2 * j + 2) * P].rearrange("b (c p) d -> p (b c) d", p=P)).then_inc(x_in[j], 16)
                with sp.Fori(0, G0 // 2) as i:
                    for k in range(2):
                        weights(split_ffn0(b, 2 * i + k), a["gu0"][bass.ds(2 * i + k, 1)].rearrange("g p c -> p (g c)"), KT * 2 * FG)
                        down_split(b, 2 * i + k - 2)
                        down(k, a["dn0"][bass.ds(2 * i + k, 1)].rearrange("g p (t c) -> p (g t) c", t=DT))
                weights(split_ffn0(b, G0 - 1), a["gu0"][G0 - 1], KT * 2 * FG)
                down_split(b, G0 - 3)
                down(0, a["dn0"][G0 - 1].rearrange("p (t c) -> p t c", t=DT))
                sp.dma_start(cos[:], a["cos"]).then_inc(tables_in, 16)
                sp.dma_start(sin[:], a["sin"]).then_inc(tables_in, 16)
                sp.dma_start(w_out[:], a["w_o"]).then_inc(w_out_in, 16)
                with sp.Fori(0, KVH) as i:
                    weights(split_qkv(b, i, 0), a["w_qkv"][bass.ds(i, 1)].rearrange("g p c -> p (g c)"), KT * QKV)
                for k in range(G1):
                    if k == 0:
                        weights(split_ffn1(b, 0), a["gu1"][0].bitcast(F32), KT * 2 * FG)
                        down_split(b, G0 - 1)
                        down(0, a["dn1"][0].rearrange("p (t c) -> p t c", t=DT).bitcast(F32))
                        phase_over(b, 2)
                        sp.dma_start(s_dn[:], a["s_dn"].broadcast_to([P, DM])).then_inc(scale0_in, 16)
                        sp.dma_start(s_gu0[:], a["s_gu"][0:1, :].broadcast_to([P, 2 * FG])).then_inc(scale0_in, 16)
                        phase_over(b, 3)
                        sp.dma_start(w_out[:], a["w_out"]).then_inc(w_out_in, 16)
                        sp.dma_start(s_gu1[:], a["s_gu"][1:2, :].broadcast_to([P, 2 * FG])).then_inc(scales_in, 16)
                    else:
                        weights(split_ffn1(b, 1), a["gu1"][1].bitcast(F32), KT * 2 * FG)
                        down_split(b, G0 - 2)
                        down(1, a["dn1"][1].rearrange("p (t c) -> p t c", t=DT).bitcast(F32))
                sp.wait_ge(s_dec.sem, s_dec.done(b))
                sp.dma_start(dec_dram, dec_t[:]).then_inc(dec_out, 16)
                sp.wait_ge(dec_out, 16 * (b + 1))
                settle(sp)
                with sp.Fori(0, HP // 2) as i:
                    for w in range(2):
                        h = 2 * i + w
                        n = b * HP + h
                        weights(split_ssm(b, h), a["w_in"][bass.ds(h, 1)].rearrange("g p c -> p (g c)"), KT * XZBC)
                        sp.wait_ge(s_out.sem, s_out.done((n - 2) * NC + NC - 1))
                        sp.dma_start(d_row[:, w, :], a["d_skip"][bass.ds(h, 1), :].broadcast_to([P, P])).then_inc(d_in[w], 16)
                        for hf in range(2):
                            toks = slice(hf * HALF, (hf + 1) * HALF)
                            sp.wait_ge(s_scan.sem, s_scan.done(2 * n + hf - 2))
                            sp.dma_start(dec[:, :, toks], dec_dram[bass.ds(2 * h, 2), toks].partition_broadcast(P)).then_inc(dec_in[hf], 16)
                for j in range(NC // 2):
                    sp.wait_ge(o_res.sem, o_res.done((b * 2 + 1) * NC + 2 * j + 1))
                    settle(sp)
                    sp.dma_start(a["out"][bass.ds(b, 1), 2 * j * P:(2 * j + 2) * P].rearrange("b (c p) d -> p (b c) d", p=P),
                                 x_res[:, 2 * j:2 * j + 2, :]).then_inc(stored[j], 16)
            for j in range(NC // 2):
                sp.wait_ge(stored[j], 16 * (B + 1))

        @block.gpsimd
        def _(pool):
            start(pool, "pool")

            def split_lo(n, lo, raw, hi):
                pool.wait_ge(w_hi.sem, w_hi.done(n))
                nc.gpsimd.tensor_tensor(lo, raw, hi, ALU.subtract).then_inc(w_split.sem, 1)

            with pool.Fori(0, B) as b:
                pool.wait_ge(init_step, 2)
                nc.gpsimd.memset(gate[:], 0.0)
                nc.gpsimd.memset(hid[:, :, FG:DT * P], 0.0).then_inc(gate_zero.sem, 1)
                raw = w_raw[:, 0:KT * 2 * FG].rearrange("p (k c) -> p k c", k=KT)
                split_lo(split_ffn0(b, 0), gu[0][1][:], raw, gu[0][0][:])
                end_phase(pool, b, 0)
                with pool.Fori(0, G0 // 2) as i:
                    split_lo(split_ffn0(b, 2 * i + 1), gu[1][1][:], raw, gu[1][0][:])
                    split_lo(split_ffn0(b, 2 * i + 2), gu[0][1][:], raw, gu[0][0][:])
                nc.gpsimd.memset(v_tok[:, :, P:P + 1], 1.0)
                raw = w_raw[:].rearrange("p (k c) -> p k c", k=KT)

                def qkv_lo(i, part):
                    cols = slice(part * 2 * P, (part + 1) * 2 * P)
                    split_lo(split_qkv(b, i, part), w_qkv[1][:, :, cols], raw[:, :, cols], w_qkv[0][:, :, cols])
                for part in range(PARTS):
                    qkv_lo(0, part)
                end_phase(pool, b, 1)

                def att_rotate(n, hf, r):
                    step, k = (2 * n + hf) * ROT + r, (hf * ROT + r) % 2
                    pool.wait_ge(a_mul.sem, a_mul.done(step))
                    nc.gpsimd.tensor_tensor(rb[:, k], ra[:, k], rb[:, k], ALU.add).then_inc(a_rot.sem, 1)

                def att_head(i, last):
                    n = b * KVH + i
                    for hf in range(2):
                        if not last or hf == 0:
                            for r in range(1, ROT):
                                if r == ROT - 1 and not last and hf == 0:
                                    qkv_lo(i + 1, 0)
                                att_rotate(n + hf, 1 - hf, r)
                        if not last and hf == 0:
                            for part in range(1, PARTS):
                                qkv_lo(i + 1, part)
                        if not last:
                            att_rotate(n + 1, hf, 0)
                for r in range(ROT):
                    att_rotate(b * KVH, 0, r)
                att_rotate(b * KVH, 1, 0)
                with pool.Fori(0, KVH - 1) as i:
                    att_head(i, False)
                att_head(KVH - 1, True)
                end_phase(pool, b, 2)
                split_lo(split_ffn1(b, 0), gu1[1][:], gu_f[:], gu1[0][:])
                end_phase(pool, b, 3)

                nc.gpsimd.memset(gate[:], 0.0)
                nc.gpsimd.memset(hid[:, :, FG:DT * P], 0.0).then_inc(gate_zero.sem, 1)
                split_lo(split_ffn1(b, 1), gu[1][1][:], gu_f[:], gu[1][0][:])
                nc.gpsimd.memset(cTz[:], 0.0)
                nc.gpsimd.memset(xz_x[:, :, 64:192], 0.0)
                nc.gpsimd.memset(dstart[:], 0.0)
                pool.drain().then_inc(own_pool, 1)
                raw = w_raw[:, 0:KT * XZBC].rearrange("p (k c) -> p k c", k=KT)
                split_lo(split_ssm(b, 0), w_in[0][1][:], raw, w_in[0][0][:])
                end_phase(pool, b, 4)

                def ssm_pairs(i, last_pairs):
                    for w in range(2):
                        n = b * HP + 2 * i + w
                        following = w == 0 or not last_pairs
                        for c in range(NC):
                            m, s = n * NC + c, c % 2
                            pool.wait_ge(s_xcopy.sem, s_xcopy.done(m))
                            if c == 0:
                                pool.wait_ge(d_in[w], 16 * (b * (HP // 2) + i + 1))
                            pool.wait_ge(s_yg.sem, s_yg.free(m, 2))
                            nc.gpsimd.tensor_tensor(xd[:, s].rearrange("p (h c) -> p h c", c=64),
                                                    xz_x[:, s, :].rearrange("p (h c) -> p h c", c=64)[:, 0:4:3, :],
                                                    d_row[:, w].rearrange("p (h c) -> p h c", c=64), ALU.mult).then_inc(s_xd.sem, 1)
                            pool.wait_ge(s_yg.sem, s_yg.done(m))
                            nc.gpsimd.tensor_tensor(y[:, c, bass.ds((2 * i + w) * P, P)], yg[:, s], sz[:, s], ALU.mult).then_inc(s_out.sem, 1)
                            if following and c < 4:
                                k, half = c // 2, slice(c % 2 * 2 * P, (c % 2 + 1) * 2 * P)
                                if c == 0:
                                    pool.wait_ge(w_hi.sem, w_hi.done(split_ssm(b, 2 * i + w + 1)))
                                ins = nc.gpsimd.tensor_tensor(w_in[1 - w][1][:, k, half], raw[:, k, half], w_in[1 - w][0][:, k, half], ALU.subtract)
                                if c == 3:
                                    ins.then_inc(w_split.sem, 1)
                with pool.Fori(0, HP // 2 - 1) as i:
                    ssm_pairs(i, False)
                ssm_pairs(HP // 2 - 1, True)
                end_phase(pool, b, 5)
                end_phase(pool, b, 6)

        @block.tensor
        def _(pe):
            start(pe, "pe")

            def three_passes(out, left, right):
                steps = [(k, l, r) for k in range(KT) for l, r in SPLITS]
                for j, (k, l, r) in enumerate(steps):
                    mm = nc.tensor.matmul(out, left(l, k), right(r, k), start=(j == 0), stop=(j == len(steps) - 1))
                return mm

            def ln_transposes(n, s):
                pe.wait_ge(ln_xn.sem, ln_xn.done(n))
                pe.wait_ge(ln_lo.sem, ln_lo.free(n, 2))
                for k in range(KT):
                    mm = nc.tensor.transpose(ps[:, 6 + s, k * P:(k + 1) * P], xn[:, s, k * P:(k + 1) * P], ident4[:, 0:P])
                mm.then_inc(ln_tr.sem, 1)

            def gate_up(b, g, c, weights, split):
                n = (b * GRP + g) * NC + c
                if c == 0:
                    pe.wait_ge(w_hi.sem, w_hi.done(split))
                    pe.wait_ge(w_split.sem, w_split.done(split))
                pe.wait_ge(f_hid.sem, f_hid.done(n - 2))
                for j in range(2):
                    mm = three_passes(ps[:, 2 * (c % 2) + j, 0:FG],
                                      lambda l, k: xnT[l][:, k, c * P:(c + 1) * P],
                                      lambda r, k: weights[r][:, k, j * FG:(j + 1) * FG])
                mm.then_inc(f_gu.sem, 1)

            def hid_turn(b, g, c):
                n = (b * GRP + g) * NC + c
                pe.wait_ge(f_hid.sem, f_hid.done(n))
                pe.wait_ge(f_low.sem, f_low.done(n - 2))
                for t in range(DT):
                    mm = nc.tensor.transpose(ps[:, 4 + c % 2, t * P:(t + 1) * P], hid[:, c % 2, t * P:(t + 1) * P], ident4[:, 0:P])
                mm.then_inc(f_tr.sem, 1)

            def down(b, g, c, slot):
                n = (b * GRP + g) * NC + c
                if c == 0:
                    pe.wait_ge(dn_lo.sem, dn_lo.done(b * GRP + g))
                    pe.wait_ge(dn_hi.sem, dn_hi.done(b * GRP + g))
                pe.wait_ge(f_hidT.sem, f_hidT.done(n))
                pe.wait_ge(f_low.sem, f_low.done(n))
                pe.wait_ge(f_acc.sem, f_acc.done(n - 2))
                steps = [(t, l, r) for t in range(DT) for l, r in SPLITS]
                for j, (t, l, r) in enumerate(steps):
                    mm = nc.tensor.matmul(ps[:, 6 + c % 2, 0:DM], hidT[l][:, c % 2, t * P:(t + 1) * P], dn[slot][r][:, t, :],
                                          start=(j == 0), stop=(j == len(steps) - 1))
                mm.then_inc(f_dn.sem, 1)

            def ffn_group(b, g, slot, weights, split, last=False):
                for c in range(NC):
                    if c + 2 < NC or not last:
                        g2, c2 = following(g, c, 2)
                        gate_up(b, g2, c2, weights[c + 2 >= NC], split + (c + 2 >= NC))
                    if c + 1 < NC or not last:
                        hid_turn(b, *following(g, c, 1))
                    down(b, g, c, slot)

            def out_proj(b, layer):
                def turn(c, s):
                    n = (b * 2 + layer) * NC + c
                    for q in range(4):
                        pe.wait_ge(o_yn.sem, o_yn.done(4 * n + q))
                        pe.wait_ge(o_yT.sem, o_yT.done(4 * n + q - 4))
                        for t in range(4):
                            mm = nc.tensor.transpose(ps[:, q, t * P:(t + 1) * P], yn[:, s, (4 * q + t) * P:(4 * q + t + 1) * P], ident4[:, 0:P])
                        mm.then_inc(o_tr.sem, 1)

                def project(c, s):
                    n = (b * 2 + layer) * NC + c
                    pe.wait_ge(o_yT.sem, o_yT.done(4 * n + 3))
                    pe.wait_ge(o_sg.sem, o_sg.done(n - 2))
                    for t in range(NT):
                        mm = nc.tensor.matmul(ps[:, 4 + s, 0:DM], yT[:, s, t, :], w_out[:, t, :], start=(t == 0), stop=(t == NT - 1))
                    mm.then_inc(o_mm.sem, 1)

                def step(c, s, first=False, last=False):
                    if not last:
                        turn(c + 1, 1 - s)
                    project(c, s)
                    if layer == 0 and not first:
                        ln_transposes((b * 2 + 1) * NC + c - 1, 1 - s)
                turn(0, 0)
                step(0, 0, first=True)
                step(1, 1)
                with pe.Fori(1, NC // 2 - 1) as j:
                    for s in range(2):
                        step(2 * j + s, s)
                step(NC - 2, 0)
                step(NC - 1, 1, last=True)
                if layer == 0:
                    ln_transposes((b * 2 + 1) * NC + NC - 1, 1)

            pe.wait_ge(consts_in, 16 * CONSTS)
            with pe.Fori(0, B) as b:
                for c in range(NC):
                    ln_transposes(b * 2 * NC + c, c % 2)
                end_phase(pe, b, 0)

                for hf in range(2):
                    mm = three_passes(ps[0:NE, 6 + hf, :], lambda l, k: router[l][:, k, :],
                                      lambda r, k: xnT[r][:, k, hf * HALF:(hf + 1) * HALF])
                mm.then_inc(rt_mm.sem, 1)
                gate_up(b, 0, 0, gu[0], split_ffn0(b, 0))
                pe.wait_ge(rt_copy.sem, rt_copy.done(b))
                settle(pe)
                for c in range(NC):
                    mm = nc.tensor.transpose(ps[:, 5, c * NE:(c + 1) * NE], rt_T[:, c * P:(c + 1) * P], ident4[0:NE, 0:NE])
                mm.then_inc(rt_logits.sem, 1)
                gate_up(b, 0, 1, gu[0], split_ffn0(b, 0))
                hid_turn(b, 0, 0)
                pe.wait_ge(rt_dve.sem, rt_dve.done(b * 9))
                settle(pe)
                with pe.Fori(0, G0 // 2) as i:
                    for k in range(2):
                        ffn_group(b, 2 * i + k, k, (gu[k], gu[1 - k]), split_ffn0(b, 2 * i + k))
                ffn_group(b, G0 - 1, 0, gu, split_ffn0(b, G0 - 1), last=True)
                end_phase(pe, b, 1)

                def att_project(n, i, hf, t):
                    u = 2 * n + hf
                    if hf == 0 and t % 2 == 0:
                        pe.wait_ge(w_hi.sem, w_hi.done(split_qkv(b, i, t // 2)))
                        pe.wait_ge(w_split.sem, w_split.done(split_qkv(b, i, t // 2)))
                    if t == 3:
                        pe.wait_ge(a_vT.sem, a_vT.done(u))
                    else:
                        pe.wait_ge(a_mul.sem, a_mul.done(u * ROT + (-2, -1, 0, None, 1, 2)[t]))
                    three_passes(ps[:, t % 2, :], lambda l, k: w_qkv[l][:, k, t * P:(t + 1) * P],
                                 lambda r, k: xnT[r][:, k, hf * HALF:(hf + 1) * HALF]).then_inc(a_proj.sem, 1)

                def v_turn(n, hf):
                    u = 2 * n + hf
                    pe.wait_ge(a_vT.sem, a_vT.done(u))
                    pe.wait_ge(a_kv.sem, a_kv.done(2 * u - 1))
                    for c in range(4):
                        mm = nc.tensor.transpose(ps[:, 7, c * P:(c + 1) * P], vT[:, c * P:(c + 1) * P], ident4[:, 0:P])
                    mm.then_inc(a_trv.sem, 1)

                def k_turn(n, hf):
                    u = 2 * n + hf
                    pe.wait_ge(a_qk.sem, a_qk.done(u * ROT))
                    pe.wait_ge(a_kv.sem, a_kv.done(2 * u))
                    for c in range(4):
                        mm = nc.tensor.transpose(ps[:, 7, c * P:(c + 1) * P], kT[:, (4 * hf + c) * P:(4 * hf + c + 1) * P], ident4[:, 0:P])
                    mm.then_inc(a_trk.sem, 1)

                def att_score(n, c):
                    m = n * NC + c
                    if c % 4 == 0:
                        pe.wait_ge(a_qk.sem, a_qk.done((2 * n + c // 4) * ROT + ROT - 1))
                    pe.wait_ge(a_mt.sem, a_mt.done(m - 2))
                    nc.tensor.matmul(ps[:, 2 + c % 2, :], kT[:, c * P:(c + 1) * P], qT[:, :, c * P:(c + 1) * P],
                                     start=True, stop=True).then_inc(a_sc.sem, 1)

                def att_update(n, c):
                    m = n * NC + c
                    if c % 4 == 0:
                        pe.wait_ge(a_kv.sem, a_kv.done(2 * (2 * n + c // 4) + 1))
                    if c == NC - 1:
                        return
                    pe.wait_ge(a_st.sem, a_st.done(m - 1))
                    nc.tensor.matmul(ps[:, 6, 0:P + 1], k_tok[:, c, :], v_tok[:, c, :], start=True, stop=True).then_inc(a_up.sem, 1)

                def att_numerator(n, c):
                    m = n * NC + c
                    pe.wait_ge(a_mt.sem, a_mt.done(m))
                    pe.wait_ge(a_st.sem, a_st.done(m - 1))
                    pe.wait_ge(a_out.sem, a_out.done(m - 1))
                    for h in range(REP):
                        out = ps[:, 4 + h // 2, (h % 2) * (P + 1):(h % 2 + 1) * (P + 1)]
                        nc.tensor.matmul(out, mt[:, c % 2, h * P:(h + 1) * P], v_tok[:, c, :], start=True, stop=False)
                        mm = nc.tensor.matmul(out, qT[:, h, c * P:(c + 1) * P], att_state[:, c % 2, :], start=False, stop=True)
                    mm.then_inc(a_nd.sem, 1)

                def att_head(i, last):
                    n = b * KVH + i
                    for hf in range(2):
                        q_ahead, kv_ahead = not last or hf == 0, not last
                        nxt = (n + hf, i + hf, 1 - hf)
                        turn = (n + hf, 1 - hf)
                        c = 4 * hf
                        att_score(n, c + 1)
                        if q_ahead:
                            att_project(*nxt, 2)
                        att_update(n, c)
                        att_numerator(n, c)
                        if q_ahead:
                            v_turn(*turn)
                            att_project(*nxt, 3)
                        att_score(n, c + 2)
                        if q_ahead:
                            att_project(*nxt, 4)
                        att_update(n, c + 1)
                        att_numerator(n, c + 1)
                        if q_ahead:
                            k_turn(*turn)
                            att_project(*nxt, 5)
                        att_score(n, c + 3)
                        att_update(n, c + 2)
                        att_numerator(n, c + 2)
                        if kv_ahead:
                            att_project(n + 1, i + 1, hf, 0)
                        att_update(n, c + 3)
                        att_numerator(n, c + 3)
                        if kv_ahead:
                            att_project(n + 1, i + 1, hf, 1)
                        if q_ahead:
                            att_score(n + hf, (c + 4) % NC)

                for t in range(REP + 2):
                    att_project(b * KVH, 0, 0, t)
                v_turn(b * KVH, 0)
                att_project(b * KVH, 0, 1, 0)
                k_turn(b * KVH, 0)
                att_project(b * KVH, 0, 1, 1)
                att_score(b * KVH, 0)
                with pe.Fori(0, KVH - 1) as i:
                    att_head(i, False)
                att_head(KVH - 1, True)
                end_phase(pe, b, 2)

                pe.wait_ge(w_out_in, 16 * (2 * b + 1))
                settle(pe)
                out_proj(b, 0)
                end_phase(pe, b, 3)

                for hf in range(2):
                    mm = three_passes(ps[:, 6 + hf, :], lambda l, k: w_dec[l][:, k, :],
                                      lambda r, k: xnT[r][:, k, hf * HALF:(hf + 1) * HALF])
                mm.then_inc(s_loga.sem, 1)

                gate_up(b, G0, 0, gu1, split_ffn1(b, 0))
                gate_up(b, G0, 1, gu1, split_ffn1(b, 0))
                pe.wait_ge(s_dec.sem, s_dec.done(b))
                hid_turn(b, G0, 0)
                for k in range(G1):
                    ffn_group(b, G0 + k, k, (gu1, gu[1])[k:], split_ffn1(b, k), last=(k == G1 - 1))
                end_phase(pe, b, 4)

                def ssm_weights(h):
                    pe.wait_ge(w_hi.sem, w_hi.done(split_ssm(b, h)))
                    pe.wait_ge(w_split.sem, w_split.done(split_ssm(b, h)))

                def project_b(u, w, hf):
                    pe.wait_ge(s_btok.sem, s_btok.done(u - 1))
                    three_passes(ps[:, 0, :], lambda l, k: w_in[w][l][:, k, 2 * P:3 * P],
                                 lambda r, k: xnT[r][:, k, hf * HALF:(hf + 1) * HALF]).then_inc(s_pb.sem, 1)

                def project_c(u, w, hf):
                    pe.wait_ge(s_cp.sem, s_cp.done(u - 1))
                    three_passes(ps[:, 1, :], lambda l, k: w_in[w][l][:, k, 3 * P:4 * P],
                                 lambda r, k: xnT[r][:, k, hf * HALF:(hf + 1) * HALF]).then_inc(s_pc.sem, 1)

                def b_turn(u, hf):
                    pe.wait_ge(s_b.sem, s_b.done(u))
                    for c in range(4):
                        mm = nc.tensor.transpose(ps[:, 0, c * P:(c + 1) * P], bT[:, (4 * hf + c) * P:(4 * hf + c + 1) * P], ident4[:, 0:P])
                    mm.then_inc(s_trb.sem, 1)

                def project_xz(m, w, c):
                    pe.wait_ge(s_xw.sem, s_xw.free(m, 2))
                    three_passes(ps[:, 2 + c % 2, 0:2 * P], lambda l, k: xnT[l][:, k, c * P:(c + 1) * P],
                                 lambda r, k: w_in[w][r][:, k, 0:2 * P]).then_inc(s_xz.sem, 1)

                def ssm_score(u, m, c):
                    if c % 4 == 0:
                        pe.wait_ge(s_c.sem, s_c.done(u))
                        pe.wait_ge(s_b.sem, s_b.done(u))
                    pe.wait_ge(s_mt.sem, s_mt.free(m, 2))
                    nc.tensor.matmul(ps[:, 4 + c % 2, 0:2 * P], bT[:, c * P:(c + 1) * P], cTz[:, :, c * P:(c + 1) * P],
                                     start=True, stop=True).then_inc(s_sc.sem, 1)

                def ssm_update(u, m, c):
                    if c % 4 == 0:
                        pe.wait_ge(s_btok.sem, s_btok.done(u))
                    if c == NC - 1:
                        return
                    pe.wait_ge(s_xw.sem, s_xw.done(m))
                    pe.wait_ge(s_st.sem, s_st.done(m - 1))
                    nc.tensor.matmul(ps[:, 7, 0:P], b_tok[:, c, :], xw[:, c % 2, :], start=True, stop=True).then_inc(s_up.sem, 1)

                def ssm_outputs(u, m, c):
                    out = ps[:, 6, 0:P]
                    pe.wait_ge(s_mt.sem, s_mt.done(m))
                    pe.wait_ge(s_xcopy.sem, s_xcopy.done(m))
                    pe.wait_ge(s_yg.sem, s_yg.done(m - 1))
                    for h in range(2):
                        nc.tensor.matmul(out, mt1[:, c % 2, h * P:(h + 1) * P], xz_x[:, c % 2, h * P:(h + 1) * P],
                                         start=(h == 0), stop=False)
                    pe.wait_ge(s_cp.sem, s_cp.done(u))
                    pe.wait_ge(s_st.sem, s_st.done(m - 1))
                    nc.tensor.matmul(out, cTp[:, c * P:(c + 1) * P], ssm_state[:, c % 2, :], start=False, stop=True).then_inc(s_y.sem, 1)

                def ssm_pairs(i, last_pairs):
                    for w in range(2):
                        n = b * HP + 2 * i + w
                        for c in range(NC):
                            u, m, hf = 2 * n + c // 4, n * NC + c, c // 4
                            nw, nhf = (w + hf) % 2, 1 - hf
                            ahead = c < NC - 1 or w == 0 or not last_pairs
                            unit_ahead = hf == 0 or w == 0 or not last_pairs
                            if ahead:
                                cw = w if c < NC - 1 else 1 - w
                                project_xz(m + 1, cw, (c + 1) % NC)
                                ssm_score(u + (c % 4 == 3), m + 1, (c + 1) % NC)
                            ssm_update(u, m, c)
                            ssm_outputs(u, m, c)
                            if unit_ahead and c % 4 == 0:
                                if hf == 1:
                                    ssm_weights(2 * i + w + 1)
                                project_b(u + 1, nw, nhf)
                            if unit_ahead and c % 4 == 1:
                                project_c(u + 1, nw, nhf)
                            if unit_ahead and c % 4 == 2:
                                b_turn(u + 1, nhf)

                pe.wait_ge(own_pool, b + 1)
                ssm_weights(0)
                u, m = 2 * b * HP, b * HP * NC
                project_b(u, 0, 0)
                project_c(u, 0, 0)
                project_xz(m, 0, 0)
                b_turn(u, 0)
                ssm_score(u, m, 0)
                with pe.Fori(0, HP // 2 - 1) as i:
                    ssm_pairs(i, False)
                ssm_pairs(HP // 2 - 1, True)
                end_phase(pe, b, 5)

                pe.wait_ge(w_out_in, 16 * (2 * b + 2))
                settle(pe)
                out_proj(b, 1)
                end_phase(pe, b, 6)

        @block.scalar
        def _(act):
            start(act, "act")

            def split_hi(hi, raw):
                nc.scalar.activation(hi, raw, ACT.Copy).then_inc(w_hi.sem, 1)

            def ln_std_of(n, slot):
                act.wait_ge(ln_var.sem, ln_var.done(n))
                nc.scalar.activation(ln_sd[:, slot, :], ln_mv[:, slot, 1:2], ACT.Sqrt, bias=eps[:, 0:1]).then_inc(ln_std.sem, 1)

            def ln_hi_of(n, c, s):
                act.wait_ge(ln_tr.sem, ln_tr.done(n))
                nc.scalar.activation(xnT[0][:, :, bass.ds(c * P, P)], ps[:, 6 + s, 0:DM].rearrange("p (k c) -> p k c", k=KT),
                                     ACT.Copy).then_inc(ln_hi.sem, 1)

            def gate_act(b, g, c):
                n = (b * GRP + g) * NC + c
                act.wait_ge(f_gu.sem, f_gu.done(n))
                act.wait_ge(f_hid.sem, f_hid.done(n - 2))
                nc.scalar.activation(silu_g[:, c % 2], ps[:, 2 * (c % 2), 0:FG], ACT.Silu).then_inc(f_silu.sem, 1)

            def hidT_copy(b, g, c):
                n = (b * GRP + g) * NC + c
                act.wait_ge(f_tr.sem, f_tr.done(n))
                act.wait_ge(f_dn.sem, f_dn.done(n - 2))
                nc.scalar.activation(hidT[0][:, c % 2], ps[:, 4 + c % 2, 0:DT * P], ACT.Copy).then_inc(f_hidT.sem, 1)

            def ffn_start(b, g):
                gate_act(b, g, 0)
                gate_act(b, g, 1)
                hidT_copy(b, g, 0)

            def ffn_group(b, g, beside, last=False):
                for c in range(NC):
                    if c + 2 < NC or not last:
                        gate_act(b, *following(g, c, 2))
                    if c + 1 < NC or not last:
                        hidT_copy(b, *following(g, c, 1))
                    if c in beside:
                        beside[c]()

            def down_hi(b, g, slot, source):
                act.wait_ge(f_dn.sem, f_dn.done((b * GRP + g - 2) * NC + NC - 1))
                nc.scalar.activation(dn[slot][0][:], source, ACT.Copy).then_inc(dn_hi.sem, 1)

            def ffn1_down_hi(b, k):
                act.wait_ge(dn_made.sem, dn_made.done(b * G1 + k))
                down_hi(b, G0 + k, k, dn_f[:])

            def gate_silu(b, g):
                act.wait_ge(f_acc.sem, f_acc.done((b * GRP + g) * NC + NC - 1))
                nc.scalar.activation(gate[:], gate[:], ACT.Silu)

            def ffn1_hi(b, k, weights):
                act.wait_ge(f_wf.sem, f_wf.done(b * G1 + k))
                split_hi(weights[0][:], gu_f[:])

            def out_proj(b, layer):
                def inner_std(c, s):
                    act.wait_ge(o_var.sem, o_var.done(b * NC + c))
                    nc.scalar.activation(in_sd[:, s, :], in_mv[:, s, 1:2], ACT.Sqrt, bias=eps[:, 0:1]).then_inc(o_std.sem, 1)

                def turned(c, s, between):
                    n = (b * 2 + layer) * NC + c
                    act.wait_ge(o_mm.sem, o_mm.done(n - 2))
                    for q in range(4):
                        if q == 2:
                            between()
                        act.wait_ge(o_tr.sem, o_tr.done(4 * n + q))
                        if layer == 0:
                            nc.scalar.activation(yT[:, s, 4 * q:4 * q + 4, :].rearrange("p t c -> p (t c)"), ps[:, q, :],
                                                 ACT.Copy).then_inc(o_yT.sem, 1)
                            continue
                        for t in range(4):
                            k = 4 * q + t
                            ins = nc.scalar.activation(yT[:, s, k, :], ps[:, q, t * P:(t + 1) * P], ACT.Identity,
                                                       bias=beta[:, k:k + 1], scale=gamma[:, k:k + 1])
                        ins.then_inc(o_yT.sem, 1)

                def step(c, s, first=False, roots_left=True, last=False):
                    n1 = (b * 2 + 1) * NC + c - 1

                    def root():
                        if layer == 1 and roots_left:
                            inner_std(c + 2, s)
                        if layer == 0 and not first:
                            ln_std_of(n1, 1 - s)
                    if last:
                        root()
                    else:
                        turned(c + 1, 1 - s, root)
                    if layer == 0 and not first:
                        ln_hi_of(n1, c - 1, 1 - s)
                if layer == 1:
                    inner_std(0, 0)
                    turned(0, 0, lambda: inner_std(1, 1))
                else:
                    turned(0, 0, lambda: None)
                step(0, 0, first=True)
                step(1, 1)
                with act.Fori(1, NC // 2 - 1) as j:
                    for s in range(2):
                        step(2 * j + s, s)
                step(NC - 2, 0, roots_left=False)
                if layer == 0:
                    ffn1_hi(b, 0, gu1)
                step(NC - 1, 1, roots_left=False, last=True)
                if layer == 0:
                    ln_std_of((b * 2 + 1) * NC + NC - 1, 1)
                    ln_hi_of((b * 2 + 1) * NC + NC - 1, NC - 1, 1)

            act.wait_ge(consts_in, 16 * CONSTS)
            nc.scalar.activation(router[0][:].rearrange("p k c -> p (k c)"), gate[:, 0, 0:KT * NE], ACT.Copy)
            nc.scalar.activation(w_dec[0][:].rearrange("p k c -> p (k c)"), gate[:, 1, :], ACT.Copy).then_inc(init_step, 1)
            with act.Fori(0, B) as b:
                raw = w_raw[:, 0:KT * 2 * FG].rearrange("p (k c) -> p k c", k=KT)

                def prep0(g, slot, loads):
                    def do():
                        act.wait_ge(w_raw_in, 16 * (b * RAWS + g + 1))
                        act.wait_ge(f_gu.sem, f_gu.done((b * GRP + g - 2) * NC + NC - 1))
                        split_hi(gu[slot][0][:], raw)
                        act.wait_ge(dn_in[slot], 16 * (b * (4 - slot) + loads))
                        down_hi(b, g, slot, dn_raw[:, slot])
                    return do
                for c in range(NC):
                    ln_std_of(b * 2 * NC + c, c)
                for c in range(NC):
                    ln_hi_of(b * 2 * NC + c, c, c % 2)
                    if c == 0:
                        prep0(0, 0, 1)()
                end_phase(act, b, 0)

                act.wait_ge(rt_mm.sem, rt_mm.done(b))
                nc.scalar.activation(rt_T[:].rearrange("p (h t) -> p h t", h=2), ps[0:NE, 6:8, :], ACT.Copy).then_inc(rt_copy.sem, 1)
                act.wait_ge(rt_dve.sem, rt_dve.done(b * 9 + 2))
                nc.scalar.activation(rt_l[:], rt_l[:], ACT.Exp).then_inc(rt_exp.sem, 1)
                ffn_start(b, 0)
                with act.Fori(0, G0 // 2) as i:
                    ffn_group(b, 2 * i, {1: prep0(2 * i + 1, 1, i + 1)})
                    ffn_group(b, 2 * i + 1, {1: prep0(2 * i + 2, 0, i + 2)})

                def qkv_hi(i, part):
                    if part == 0:
                        act.wait_ge(w_raw_in, 16 * (b * RAWS + G0 + i + 1))
                    act.wait_ge(a_proj.sem, a_proj.done((b * KVH + i) * 2 * (REP + 2) - (REP + 1) + 2 * part))
                    cols = slice(part * 2 * P, (part + 1) * 2 * P)
                    split_hi(w_qkv[0][:, :, cols], w_raw[:].rearrange("p (k c) -> p k c", k=KT)[:, :, cols])

                def first_head():
                    for part in range(PARTS):
                        qkv_hi(0, part)
                ffn_group(b, G0 - 1, {1: first_head}, last=True)
                end_phase(act, b, 1)

                def rope_act(n, hf, r):
                    step, k = (2 * n + hf) * ROT + r, (hf * ROT + r) % 2
                    act.wait_ge(a_rot.sem, a_rot.done(step))
                    nc.scalar.activation(ra[:, k], rb[:, k], ACT.Relu, scale=-1.0).then_inc(a_neg.sem, 1)
                    act.wait_ge(a_neg.sem, a_neg.done(step))
                    nc.scalar.activation(ra[:, k], ra[:, k], ACT.Exp, scale=-1.0).then_inc(a_act.sem, 1)

                def v_copy(n, hf):
                    u = 2 * n + hf
                    act.wait_ge(a_proj.sem, a_proj.done(u * (REP + 2) + 1))
                    act.wait_ge(a_trv.sem, a_trv.done(u - 1))
                    nc.scalar.activation(vT[:], ps[:, 1, :], ACT.Copy).then_inc(a_vT.sem, 1)

                def v_tok_copy(n, hf):
                    u = 2 * n + hf
                    act.wait_ge(a_trv.sem, a_trv.done(u))
                    act.wait_ge(a_nd.sem, a_nd.done(4 * u - 5))
                    nc.scalar.activation(v_tok[:, 4 * hf:4 * hf + 4, 0:P], ps[:, 7, :].rearrange("p (c e) -> p c e", e=P), ACT.Copy).then_inc(a_kv.sem, 1)

                def k_tok_copy(n, hf):
                    act.wait_ge(a_trk.sem, a_trk.done(2 * n + hf))
                    nc.scalar.activation(k_tok[:, 4 * hf:4 * hf + 4, :], ps[:, 7, :].rearrange("p (c e) -> p c e", e=P), ACT.Copy).then_inc(a_kv.sem, 1)

                def out_copy(n, i, c):
                    act.wait_ge(a_nd.sem, a_nd.done(n * NC + c))
                    nd = ps[:, 4:6, 0:2 * (P + 1)].rearrange("p b (h e) -> p b h e", e=P + 1)
                    nc.scalar.activation(y[:, c, bass.ds(i * REP * P, REP * P)].rearrange("p (b h e) -> p b h e", b=2, h=2),
                                         nd[:, :, :, 0:P], ACT.Copy)
                    nc.scalar.activation(den[:, c, bass.ds(i * REP, REP)].rearrange("p (b h) -> p b h", b=2),
                                         nd[:, :, :, P], ACT.Copy).then_inc(a_out.sem, 1)

                def att_head(i, last):
                    n = b * KVH + i
                    for hf in range(2):
                        q_ahead, kv_ahead = not last or hf == 0, not last
                        nxt = (n + hf, 1 - hf)
                        c = 4 * hf
                        split = not last and hf == 0
                        if q_ahead:
                            rope_act(*nxt, 1)
                        out_copy(n, i, c)
                        if q_ahead:
                            v_tok_copy(*nxt)
                            rope_act(*nxt, 2)
                        out_copy(n, i, c + 1)
                        if q_ahead:
                            k_tok_copy(*nxt)
                        if split:
                            qkv_hi(i + 1, 0)
                        if q_ahead:
                            rope_act(*nxt, 3)
                        out_copy(n, i, c + 2)
                        if q_ahead:
                            rope_act(*nxt, 4)
                        if split:
                            qkv_hi(i + 1, 1)
                            qkv_hi(i + 1, 2)
                        out_copy(n, i, c + 3)
                        if kv_ahead:
                            rope_act(n + 1, hf, 0)
                            v_copy(n + 1, hf)
                rope_act(b * KVH, 0, 0)
                v_copy(b * KVH, 0)
                for r in range(1, ROT):
                    rope_act(b * KVH, 0, r)
                    if r == 1:
                        gate_silu(b, G0 - 1)
                    if r == 3:
                        v_tok_copy(b * KVH, 0)
                k_tok_copy(b * KVH, 0)
                rope_act(b * KVH, 1, 0)
                v_copy(b * KVH, 1)
                with act.Fori(0, KVH - 1) as i:
                    att_head(i, False)
                att_head(KVH - 1, True)
                end_phase(act, b, 2)

                out_proj(b, 0)
                end_phase(act, b, 3)

                ffn1_down_hi(b, 0)
                act.wait_ge(s_loga.sem, s_loga.done(b))
                nc.scalar.activation(dec_e[:].rearrange("p (h c) -> p h c", h=2), ps[0:SH, 6:8, :], ACT.Exp).then_inc(own_act, 1)
                act.wait_ge(own_act, b + 1)
                nc.scalar.activation(dec_t[:], dec_e[:], ACT.Exp, scale=-1.0).then_inc(s_dec.sem, 1)

                def ssm_prep(h, w):
                    act.wait_ge(w_raw_in, 16 * (b * RAWS + G0 + KVH + G1 + h + 1))
                    act.wait_ge(s_xz.sem, s_xz.done((b * HP + h - 1) * NC - 1))
                    split_hi(w_in[w][0][:], w_raw[:, 0:KT * XZBC].rearrange("p (k c) -> p k c", k=KT))

                def first_pair():
                    act.wait_ge(dec_out, 16 * (b + 1))
                    ssm_prep(0, 0)
                ffn_start(b, G0)

                def second_group():
                    ffn1_hi(b, 1, gu[1])
                    ffn1_down_hi(b, 1)
                ffn_group(b, G0, {1: second_group})
                ffn_group(b, G0 + 1, {1: first_pair}, last=True)
                act.wait_ge(own_pool, b + 1)
                settle(act)
                end_phase(act, b, 4)

                def b_copy(u, hf):
                    act.wait_ge(s_pb.sem, s_pb.done(u))
                    act.wait_ge(s_sc.sem, s_sc.done(4 * u - 5))
                    nc.scalar.activation(bT[:, hf * HALF:(hf + 1) * HALF], ps[:, 0, :], ACT.Copy).then_inc(s_b.sem, 1)

                def c_copy(u, hf):
                    act.wait_ge(s_pc.sem, s_pc.done(u))
                    act.wait_ge(s_sc.sem, s_sc.done(4 * u - 5))
                    nc.scalar.activation(cTz[0:64, 0, hf * HALF:(hf + 1) * HALF], ps[0:64, 1, :], ACT.Copy)
                    nc.scalar.activation(cTz[64:P, 1, hf * HALF:(hf + 1) * HALF], ps[64:P, 1, :], ACT.Copy).then_inc(s_c.sem, 1)

                def btok_copy(u, hf):
                    act.wait_ge(s_trb.sem, s_trb.done(u))
                    act.wait_ge(s_y.sem, s_y.done(4 * u - 5))
                    nc.scalar.activation(b_tok[:, 4 * hf:4 * hf + 4, :], ps[:, 0, :].rearrange("p (c e) -> p c e", e=P), ACT.Copy).then_inc(s_btok.sem, 1)

                def xz_copy(m, c):
                    s = c % 2
                    act.wait_ge(s_xz.sem, s_xz.done(m))
                    act.wait_ge(s_y.sem, s_y.free(m, 2))
                    act.wait_ge(s_xd.sem, s_xd.free(m, 2))
                    nc.scalar.activation(xz_x[:, s, :].rearrange("p (h c) -> p h c", c=64)[:, 0:4:3, :],
                                         ps[:, 2 + s, 0:P].rearrange("p (h c) -> p h c", c=64), ACT.Copy)
                    act.wait_ge(s_out.sem, s_out.free(m, 2))
                    nc.scalar.activation(sz[:, s, :], ps[:, 2 + s, P:2 * P], ACT.Silu).then_inc(s_xcopy.sem, 1)

                def ssm_pairs(i, last_pairs):
                    for w in range(2):
                        n = b * HP + 2 * i + w
                        for c in range(NC):
                            u, m, hf = 2 * n + c // 4, n * NC + c, c // 4
                            unit_ahead = hf == 0 or w == 0 or not last_pairs
                            if c < NC - 1 or w == 0 or not last_pairs:
                                xz_copy(m + 1, (c + 1) % NC)
                            if c == 0 and (w == 0 or not last_pairs):
                                ssm_prep(2 * i + w + 1, 1 - w)
                            if unit_ahead and c % 4 == 1:
                                b_copy(u + 1, 1 - hf)
                            if unit_ahead and c % 4 == 2:
                                c_copy(u + 1, 1 - hf)
                            if unit_ahead and c % 4 == 3:
                                btok_copy(u + 1, 1 - hf)
                u = 2 * b * HP
                b_copy(u, 0)
                c_copy(u, 0)
                xz_copy(u * 4, 0)
                btok_copy(u, 0)
                gate_silu(b, GRP - 1)
                with act.Fori(0, HP // 2 - 1) as i:
                    ssm_pairs(i, False)
                ssm_pairs(HP // 2 - 1, True)
                end_phase(act, b, 5)
                out_proj(b, 1)
                end_phase(act, b, 6)

        @block.vector
        def _(dve):
            start(dve, "dve")

            def chunk(t, c):
                return t[:, bass.ds(c, 1), :].rearrange("p a d -> p (a d)")

            def ln_stats(n, c, slot, before):
                dve.wait_ge(ln_var.sem, ln_var.done(before))
                settle(dve)
                nc.vector.bn_stats(ln_st[:, slot, :], chunk(x_res, c)).then_inc(ln_stat.sem, 1)

            def ln_variance(n, slot, before):
                dve.wait_ge(ln_stat.sem, ln_stat.done(n))
                dve.wait_ge(ln_xn.sem, ln_xn.done(before))
                settle(dve)
                nc.vector.bn_aggr(ln_mv[:, slot, :], ln_st[:, slot, :]).then_inc(ln_var.sem, 1)

            def ln_root(n, slot):
                dve.wait_ge(ln_std.sem, ln_std.done(n))
                nc.vector.reciprocal(ln_rs[:, slot, :], ln_sd[:, slot, :]).then_inc(ln_rstd.sem, 1)

            def ln_norm(n, c, slot, s):
                dve.wait_ge(ln_rstd.sem, ln_rstd.done(n))
                dve.wait_ge(ln_tr.sem, ln_tr.done(n - 2))
                nc.vector.tensor_scalar(xn[:, s, :], chunk(x_res, c), ln_mv[:, slot, 0:1], ln_rs[:, slot, :],
                                        ALU.subtract, ALU.mult).then_inc(ln_xn.sem, 1)

            def ln_low(n, c, s):
                dve.wait_ge(ln_hi.sem, ln_hi.done(n))
                nc.vector.tensor_tensor(xnT[1][:, :, bass.ds(c * P, P)], ps[:, 6 + s, 0:DM].rearrange("p (k c) -> p k c", k=KT),
                                        xnT[0][:, :, bass.ds(c * P, P)], ALU.subtract).then_inc(ln_lo.sem, 1)

            def hidden(b, g, c, slot, experts):
                n = (b * GRP + g) * NC + c
                if c == 0 and experts:
                    dve.wait_ge(f_hid.sem, f_hid.done(n - 1))
                    nc.vector.tensor_copy(combine_g[:, slot], combine[:, bass.ds(2 * g, 2), :]).then_inc(f_cg.sem, 1)
                    dve.wait_ge(f_cg.sem, f_cg.done(b * G0 + g))
                dve.wait_ge(f_silu.sem, f_silu.done(n))
                dve.wait_ge(f_tr.sem, f_tr.done(n - 2))
                up = ps[:, 2 * (c % 2) + 1, :]
                if experts:
                    for e in range(2):
                        ins = nc.vector.scalar_tensor_tensor(
                            hid[:, c % 2, e * FE:(e + 1) * FE], up[:, e * FE:(e + 1) * FE], combine_g[:, slot, e, c:c + 1],
                            silu_g[:, c % 2, e * FE:(e + 1) * FE], ALU.mult, ALU.mult)
                else:
                    ins = nc.vector.tensor_tensor(hid[:, c % 2, 0:FG], up[:, 0:FG], silu_g[:, c % 2, :], ALU.mult)
                ins.then_inc(f_hid.sem, 1)

            def hidT_low(b, g, c):
                n = (b * GRP + g) * NC + c
                dve.wait_ge(f_hidT.sem, f_hidT.done(n))
                dve.wait_ge(f_dn.sem, f_dn.done(n - 2))
                nc.vector.tensor_tensor(hidT[1][:, c % 2], ps[:, 4 + c % 2, 0:DT * P], hidT[0][:, c % 2], ALU.subtract).then_inc(f_low.sem, 1)

            def down_low(b, g, slot, source):
                dve.wait_ge(dn_hi.sem, dn_hi.done(b * GRP + g))
                nc.vector.tensor_tensor(dn[slot][1][:], source, dn[slot][0][:], ALU.subtract).then_inc(dn_lo.sem, 1)

            def ffn_start(b, g, experts):
                for c in range(2):
                    hidden(b, g, c, 0, experts)
                hidT_low(b, g, 0)

            def ffn_group(b, g, slot, experts, beside, last=False):
                for c in range(NC):
                    if c + 2 < NC or not last:
                        g2, c2 = following(g, c, 2)
                        hidden(b, g2, c2, slot if c + 2 < NC else 1 - slot, experts)
                    if c + 1 < NC or not last:
                        hidT_low(b, *following(g, c, 1))
                    n = (b * GRP + g) * NC + c
                    dve.wait_ge(f_dn.sem, f_dn.done(n))
                    dve.wait_ge(f_acc.sem, f_acc.done(n - NC))
                    nc.vector.tensor_tensor(gate[:, c, :], ps[:, 6 + c % 2, 0:DM], gate[:, c, :], ALU.add).then_inc(f_acc.sem, 1)
                    if c in beside:
                        beside[c]()

            def dequant_up(b, k, scale):
                dve.wait_ge(w_raw_in, 16 * (b * RAWS + G0 + KVH + k + 1))
                dve.wait_ge(w_split.sem, w_split.done(split_ffn1(b, k) - 1))
                for kk in range(KT):
                    ins = nc.vector.scalar_tensor_tensor(
                        gu_f[:, kk], w_raw[:, kk * 2 * FG:(kk + 1) * 2 * FG].bitcast(I32), ZERO_POINT,
                        scale[:], ALU.subtract, ALU.mult)
                ins.then_inc(f_wf.sem, 1)

            def out_proj(b, layer, normalise, normalise_first):
                def add_gated(c, s):
                    n = (b * 2 + layer) * NC + c
                    dve.wait_ge(o_mm.sem, o_mm.done(n))
                    dve.wait_ge(o_res.sem, o_res.done(n - 2))
                    nc.vector.tensor_tensor(sg[:, s], ps[:, 4 + s, 0:DM], chunk(gate, c), ALU.mult).then_inc(o_sg.sem, 1)
                    dve.wait_ge(o_sg.sem, o_sg.done(n))
                    nc.vector.tensor_tensor(chunk(x_res, c), sg[:, s], chunk(x_res, c), ALU.add).then_inc(o_res.sem, 1)

                def step(c, s, first=False, last=False):
                    n1 = (b * 2 + 1) * NC + c
                    if not last:
                        normalise(c + 2, s)
                    add_gated(c, s)
                    if layer == 0:
                        dve.wait_ge(o_res.sem, o_res.done(b * 2 * NC + c))
                        ln_stats(n1, c, s, n1 - 2)
                        ln_variance(n1, s, n1 - 2)
                        if not first:
                            ln_low(n1 - 1, c - 1, 1 - s)
                        ln_root(n1, s)
                        ln_norm(n1, c, s, s)
                for c in range(2):
                    normalise_first(c, c)
                step(0, 0, first=True)
                step(1, 1)
                with dve.Fori(1, NC // 2 - 1) as j:
                    for s in range(2):
                        step(2 * j + s, s)
                if layer == 0:
                    dve.wait_ge(scale0_in, 32 * (b + 1))
                    dequant_up(b, 0, s_gu0)
                step(NC - 2, 0, last=True)
                step(NC - 1, 1, last=True)
                if layer == 0:
                    ln_low((b * 2 + 1) * NC + NC - 1, NC - 1, 1)

            nc.vector.memset(eps[:], LN_EPS)
            nc.vector.memset(att_state[:], 0.0)
            nc.vector.memset(ssm_state[:], 0.0)
            nc.vector.memset(combine[:, NE:2 * G0, :], 1.0)
            dve.wait_ge(init_step, 1)
            nc.vector.tensor_tensor(router[1][:].rearrange("p k c -> p (k c)"), gate[:, 0, 0:KT * NE], router[0][:].rearrange("p k c -> p (k c)"), ALU.subtract)
            nc.vector.tensor_tensor(w_dec[1][:].rearrange("p k c -> p (k c)"), gate[:, 1, :], w_dec[0][:].rearrange("p k c -> p (k c)"), ALU.subtract).then_inc(init_step, 1)
            with dve.Fori(0, B) as b:
                n0 = b * 2 * NC
                for c in range(NC):
                    if c % 2 == 0:
                        dve.wait_ge(x_in[c // 2], 16 * (b + 1))
                    ln_stats(n0 + c, c, c, n0 - 1)
                    if c > 0:
                        ln_variance(n0 + c - 1, c - 1, n0 - 1)
                ln_variance(n0 + NC - 1, NC - 1, n0 - 1)
                for c in range(NC):
                    ln_root(n0 + c, c)
                    ln_norm(n0 + c, c, c, c % 2)
                    if c > 1:
                        ln_low(n0 + c - 2, c - 2, c % 2)
                for c in (NC - 2, NC - 1):
                    ln_low(n0 + c, c, c % 2)
                end_phase(dve, b, 0)
                down_low(b, 0, 0, dn_raw[:, 0])

                r0 = b * 9

                def routed(k, ins):
                    ins.then_inc(rt_dve.sem, 1)
                    dve.wait_ge(rt_dve.sem, rt_dve.done(r0 + k))
                dve.wait_ge(rt_logits.sem, rt_logits.done(b))
                routed(0, nc.vector.tensor_copy(rt_l[:].rearrange("p c e -> p (c e)"), ps[:, 5, 0:NC * NE]))
                routed(1, nc.vector.tensor_reduce(rt_m[:], rt_l[:], AX.X, ALU.max))
                nc.vector.tensor_tensor(rt_l[:], rt_l[:], rt_m[:].unsqueeze(2).broadcast_to([P, NC, NE]), ALU.subtract).then_inc(rt_dve.sem, 1)
                dve.wait_ge(rt_exp.sem, rt_exp.done(b))
                routed(3, nc.vector.tensor_reduce(rt_s[:], rt_l[:], AX.X, ALU.add))
                routed(4, nc.vector.reciprocal(rt_m[:], rt_s[:]))
                routed(5, nc.vector.tensor_tensor(rt_l[:], rt_l[:], rt_m[:].unsqueeze(2).broadcast_to([P, NC, NE]), ALU.mult))
                rival = rt_l[:].unsqueeze(2).broadcast_to([P, NC, NE, NE])
                score = rt_l[:].unsqueeze(3).broadcast_to([P, NC, NE, NE])
                nc.vector.tensor_tensor(rt_gt[:].rearrange("p (c e) j -> p c e j", c=NC), rival, score, ALU.is_gt)
                routed(6, nc.vector.tensor_tensor(rt_eq[:].rearrange("p (c e) j -> p c e j", c=NC), rival, score, ALU.is_equal))
                first = earlier[:].rearrange("p (e j) -> p e j", e=NE).unsqueeze(1).broadcast_to([P, NC, NE, NE])
                routed(7, nc.vector.tensor_tensor(rt_eq[:].rearrange("p (c e) j -> p c e j", c=NC), rt_eq[:].rearrange("p (c e) j -> p c e j", c=NC), first, ALU.mult))
                routed(8, nc.vector.tensor_tensor(rt_gt[:], rt_gt[:], rt_eq[:], ALU.add))
                nc.vector.tensor_reduce(rt_rank[:], rt_gt[:], AX.X, ALU.add).then_inc(own_dve, 1)
                dve.wait_ge(own_dve, 2 * b + 1)
                nc.vector.scalar_tensor_tensor(combine[:, 0:NE, :].rearrange("p e c -> p c e"), rt_rank[:].rearrange("p (c e) -> p c e", c=NC), 1.5,
                                               rt_l[:], ALU.is_lt, ALU.mult).then_inc(own_dve, 1)
                dve.wait_ge(own_dve, 2 * b + 2)
                dve.wait_ge(gate_zero.sem, gate_zero.done(2 * b))
                settle(dve)

                ffn_start(b, 0, True)
                with dve.Fori(0, G0 // 2) as i:
                    for k in range(2):
                        ffn_group(b, 2 * i + k, k, True, {1: lambda: down_low(b, 2 * i + k + 1, 1 - k, dn_raw[:, 1 - k])})
                ffn_group(b, G0 - 1, 0, True, {}, last=True)
                end_phase(dve, b, 1)

                dve.wait_ge(tables_in, 32 * (b + 1))
                settle(dve)
                def rope_mul(n, hf, r):
                    u = 2 * n + hf
                    t, k = (0 if r == 0 else r + 1), (hf * ROT + r) % 2
                    toks = slice(hf * HALF, (hf + 1) * HALF)
                    dve.wait_ge(a_proj.sem, a_proj.done(u * (REP + 2) + t))
                    dve.wait_ge(a_qk.sem, a_qk.done(u * ROT + r - 2))
                    nc.vector.tensor_tensor(ra[:, k], ps[:, t % 2, :], cos[:, toks], ALU.mult)
                    nc.vector.tensor_tensor(rb[0:64, k], ps[64:P, t % 2, :], sin[0:64, toks], ALU.mult)
                    nc.vector.tensor_tensor(rb[64:P, k], ps[0:64, t % 2, :], sin[64:P, toks], ALU.mult).then_inc(a_mul.sem, 1)

                def feature(n, hf, r):
                    u = 2 * n + hf
                    k = (hf * ROT + r) % 2
                    toks = slice(hf * HALF, (hf + 1) * HALF)
                    if r == 0:
                        dve.wait_ge(a_sc.sem, a_sc.done(4 * u - 5))
                    if r == 1:
                        dve.wait_ge(a_nd.sem, a_nd.done(4 * u - 5))
                    dve.wait_ge(a_act.sem, a_act.done(u * ROT + r))
                    dst = kT[:, toks] if r == 0 else qT[:, r - 1, toks]
                    nc.vector.scalar_tensor_tensor(dst, rb[:, k], 0.0, ra[:, k], ALU.max, ALU.add).then_inc(a_qk.sem, 1)

                def mask(n, c):
                    m = n * NC + c
                    dve.wait_ge(a_sc.sem, a_sc.done(m))
                    dve.wait_ge(a_nd.sem, a_nd.done(m - 2))
                    nc.vector.tensor_tensor(mt[:, c % 2].rearrange("p (h t) -> p h t", h=REP), ps[:, 2 + c % 2, :].rearrange("p (h t) -> p h t", h=REP),
                                            causal[:].unsqueeze(1).broadcast_to([P, REP, P]), ALU.mult).then_inc(a_mt.sem, 1)

                def att_next_state(n, c):
                    m = n * NC + c
                    nxt = att_state[:, (c + 1) % 2, :]
                    dve.wait_ge(a_nd.sem, a_nd.done(m - 1))
                    dve.wait_ge(a_st.sem, a_st.done(m - 1))
                    if c == NC - 1:
                        nc.vector.memset(nxt, 0.0).then_inc(a_st.sem, 1)
                        return
                    dve.wait_ge(a_up.sem, a_up.done(n * (NC - 1) + c))
                    nc.vector.tensor_tensor(nxt, ps[:, 6, 0:P + 1], att_state[:, c % 2, :], ALU.add).then_inc(a_st.sem, 1)

                def att_head(i, last):
                    n = b * KVH + i
                    for hf in range(2):
                        q_ahead, kv_ahead = not last or hf == 0, not last
                        nxt = (n + hf, 1 - hf)
                        c = 4 * hf
                        mask(n, c + 1)
                        if q_ahead:
                            rope_mul(*nxt, 1)
                        att_next_state(n, c)
                        if q_ahead:
                            rope_mul(*nxt, 2)
                            feature(*nxt, 1)
                        mask(n, c + 2)
                        if q_ahead:
                            rope_mul(*nxt, 3)
                            feature(*nxt, 2)
                        att_next_state(n, c + 1)
                        if q_ahead:
                            rope_mul(*nxt, 4)
                            feature(*nxt, 3)
                        mask(n, c + 3)
                        att_next_state(n, c + 2)
                        if q_ahead:
                            feature(*nxt, 4)
                        if kv_ahead:
                            rope_mul(n + 1, hf, 0)
                        att_next_state(n, c + 3)
                        if q_ahead:
                            mask(n + hf, (c + 4) % NC)
                        if kv_ahead:
                            feature(n + 1, hf, 0)
                rope_mul(b * KVH, 0, 0)
                for r in range(1, ROT):
                    rope_mul(b * KVH, 0, r)
                    feature(b * KVH, 0, r - 1)
                feature(b * KVH, 0, REP)
                rope_mul(b * KVH, 1, 0)
                mask(b * KVH, 0)
                feature(b * KVH, 1, 0)
                with dve.Fori(0, KVH - 1) as i:
                    att_head(i, False)
                att_head(KVH - 1, True)
                end_phase(dve, b, 2)

                def divided(c, s):
                    n = b * 2 * NC + c
                    dve.wait_ge(o_yn.sem, o_yn.done(4 * n - 5))
                    nc.vector.tensor_scalar(rin[:, s, :], chunk(den, c), DEN_EPS, None, ALU.add).then_inc(rin_step, 1)
                    dve.wait_ge(rin_step, 2 * (b * NC + c) + 1)
                    nc.vector.reciprocal(rin2[:, s, :], rin[:, s, :]).then_inc(rin_step, 1)
                    dve.wait_ge(rin_step, 2 * (b * NC + c) + 2)
                    dve.wait_ge(o_tr.sem, o_tr.done(4 * n - 5))
                    for q in range(4):
                        nc.vector.tensor_tensor(yn[:, s, q * HALF:(q + 1) * HALF].rearrange("p (h e) -> p h e", e=P),
                                                chunk(y, c)[:, q * HALF:(q + 1) * HALF].rearrange("p (h e) -> p h e", e=P),
                                                rin2[:, s, 4 * q:4 * q + 4].unsqueeze(2).broadcast_to([P, 4, P]), ALU.mult).then_inc(o_yn.sem, 1)
                out_proj(b, 0, divided, divided)
                end_phase(dve, b, 3)

                def dequant_down(k):
                    dve.wait_ge(dn_in[k], 16 * (b * (4 - k) + 4 - k))
                    dve.wait_ge(dn_lo.sem, dn_lo.done(b * GRP + G0 + k - 1))
                    nc.vector.scalar_tensor_tensor(dn_f[:], dn_raw[:, k].bitcast(I32), ZERO_POINT,
                                                   s_dn[:].unsqueeze(1).broadcast_to([P, DT, DM]), ALU.subtract, ALU.mult).then_inc(dn_made.sem, 1)
                    down_low(b, G0 + k, k, dn_f[:])

                def second_group():
                    dve.wait_ge(scales_in, 16 * (b + 1))
                    dequant_up(b, 1, s_gu1)
                    dequant_down(1)
                dve.wait_ge(gate_zero.sem, gate_zero.done(2 * b + 1))
                dequant_down(0)
                ffn_start(b, G0, False)
                ffn_group(b, G0, 0, False, {1: second_group})
                def decay_start(n, hf):
                    u = 2 * n + hf
                    toks = slice(hf * HALF, (hf + 1) * HALF)
                    dve.wait_ge(dec_in[hf], 16 * (n + 1))
                    dve.wait_ge(s_scan.sem, s_scan.done(u - 2))
                    for h in range(2):
                        q = slice(64 * h, 64 * h + 64)
                        ins = nc.vector.tensor_copy(dstart[q, toks].rearrange("p (c t) -> p c t", t=P)[:, :, 0],
                                                    dec[q, h, toks].rearrange("p (c t) -> p c t", t=P)[:, :, 0])
                    ins.then_inc(s_prep, 1)
                    dve.wait_ge(s_prep, 2 * u + 1)
                    nc.vector.memset(dec[:, :, toks].rearrange("p h (c t) -> p h c t", t=P)[:, :, :, 0:1], 0.0).then_inc(s_prep, 1)

                def decay_scan(n, hf, h):
                    u = 2 * n + hf
                    toks = slice(hf * HALF, (hf + 1) * HALF)
                    dve.wait_ge(s_prep, 2 * u + 2)
                    if h == 0:
                        dve.wait_ge(s_mt.sem, s_mt.done(4 * u - 5))
                        dve.wait_ge(s_xw.sem, s_xw.done(4 * u - 5))
                    nc.vector.tensor_tensor_scan(lmat[:, h, toks], dec[:, h, toks], ident4[:, 0:HALF], 0.0, ALU.mult, ALU.add)

                def decay_from_start(n, hf):
                    u = 2 * n + hf
                    toks = slice(hf * HALF, (hf + 1) * HALF)
                    dve.wait_ge(s_st.sem, s_st.done(4 * u - 5))
                    dve.wait_ge(s_cp.sem, s_cp.done(u - 2))
                    for h in range(2):
                        q = slice(64 * h, 64 * h + 64)
                        ins = nc.vector.tensor_tensor_scan(pdec[q, toks], dec[q, h, toks], dstart[q, toks], 0.0, ALU.mult, ALU.add)
                    ins.then_inc(s_scan.sem, 1)

                def c_decayed(n, hf):
                    u = 2 * n + hf
                    toks = slice(hf * HALF, (hf + 1) * HALF)
                    dve.wait_ge(s_scan.sem, s_scan.done(u))
                    dve.wait_ge(s_c.sem, s_c.done(u))
                    dve.wait_ge(s_y.sem, s_y.done(4 * u - 5))
                    nc.vector.tensor_tensor(cTp[:, toks], ps[:, 1, :], pdec[:, toks], ALU.mult).then_inc(s_cp.sem, 1)

                def x_weighted(m, c):
                    s = c % 2
                    dve.wait_ge(s_xcopy.sem, s_xcopy.done(m))
                    dve.wait_ge(s_y.sem, s_y.free(m, 2))
                    last = lmat[:, :, (c + 1) * P - 1:(c + 1) * P].broadcast_to([P, 2, 64])
                    nc.vector.tensor_tensor(xw[:, s].rearrange("p (h c) -> p h c", c=64), ps[:, 2 + s, 0:P].rearrange("p (h c) -> p h c", c=64),
                                            last, ALU.mult).then_inc(s_xw.sem, 1)

                def decayed_scores(m, c):
                    s = c % 2
                    dve.wait_ge(s_sc.sem, s_sc.done(m))
                    dve.wait_ge(s_y.sem, s_y.free(m, 2))
                    nc.vector.tensor_tensor(mt1[:, s].rearrange("p (h c) -> p h c", h=2), ps[:, 4 + s, 0:2 * P].rearrange("p (h c) -> p h c", h=2),
                                            lmat[:, :, c * P:(c + 1) * P], ALU.mult).then_inc(s_mt.sem, 1)

                def ssm_next_state(n, m, c):
                    nxt, cur = (c + 1) % 2, c % 2
                    dve.wait_ge(s_y.sem, s_y.done(m - 1))
                    dve.wait_ge(s_st.sem, s_st.done(m - 1))
                    if c == NC - 1:
                        nc.vector.memset(ssm_state[:, nxt, :], 0.0).then_inc(s_st.sem, 1)
                        return
                    dve.wait_ge(s_up.sem, s_up.done(n * (NC - 1) + c))
                    for h in range(2):
                        q = slice(64 * h, 64 * h + 64)
                        ins = nc.vector.scalar_tensor_tensor(ssm_state[q, nxt, q], ssm_state[q, cur, q], pdec[q, (c + 1) * P - 1:(c + 1) * P],
                                                             ps[q, 7, q], ALU.mult, ALU.add)
                    ins.then_inc(s_st.sem, 1)

                def inner_stats(c, s, q):
                    return nc.vector.bn_stats(in_st[:, s, 6 * q:6 * q + 6], chunk(y, c)[:, q * HALF:(q + 1) * HALF])

                def add_skip(m, c):
                    s = c % 2
                    dve.wait_ge(s_y.sem, s_y.done(m))
                    dve.wait_ge(s_xd.sem, s_xd.done(m))
                    dve.wait_ge(s_out.sem, s_out.free(m, 2))
                    nc.vector.tensor_tensor(yg[:, s], ps[:, 6, 0:P], xd[:, s], ALU.add).then_inc(s_yg.sem, 1)

                def ssm_pairs(i, last_pairs):
                    for w in range(2):
                        n = b * HP + 2 * i + w
                        for c in range(NC):
                            m, hf = n * NC + c, c // 4
                            unit_ahead = hf == 0 or w == 0 or not last_pairs
                            if c < NC - 1 or w == 0 or not last_pairs:
                                x_weighted(m + 1, (c + 1) % NC)
                                decayed_scores(m + 1, (c + 1) % NC)
                            ssm_next_state(n, m, c)
                            add_skip(m, c)
                            if last_pairs and w == 1 and c < 2 * EARLY:
                                dve.wait_ge(s_out.sem, s_out.done((b * HP + 4 * EARLY) * NC - 1))
                                dve.wait_ge(o_yn.sem, o_yn.done(4 * (b * 2 + 1) * NC - 1))
                                settle(dve)
                                inner_stats(c // EARLY, c // EARLY, c % EARLY)
                            if not unit_ahead:
                                continue
                            after = (n + hf, 1 - hf)
                            if c % 4 == 0:
                                decay_start(*after)
                                decay_scan(*after, 0)
                            if c % 4 == 1:
                                decay_scan(*after, 1)
                            if c % 4 == 2:
                                decay_from_start(*after)
                                c_decayed(*after)
                def first_decay():
                    dve.wait_ge(own_pool, b + 1)
                    decay_start(b * HP, 0)
                    decay_scan(b * HP, 0, 0)
                ffn_group(b, G0 + 1, 1, False, {3: first_decay, 4: lambda: decay_scan(b * HP, 0, 1),
                                                5: lambda: decay_from_start(b * HP, 0)}, last=True)
                end_phase(dve, b, 4)
                c_decayed(b * HP, 0)
                x_weighted(b * HP * NC, 0)
                decayed_scores(b * HP * NC, 0)
                with dve.Fori(0, HP // 2 - 1) as i:
                    ssm_pairs(i, False)
                ssm_pairs(HP // 2 - 1, True)
                end_phase(dve, b, 5)

                def normalised(c, s, from_quarter=0):
                    n = b * NC + c
                    n4 = 4 * ((b * 2 + 1) * NC + c)
                    dve.wait_ge(o_yn.sem, o_yn.done(n4 - 5))
                    settle(dve)
                    for q in range(from_quarter, 4):
                        ins = inner_stats(c, s, q)
                    ins.then_inc(rin_step2, 1)
                    dve.wait_ge(rin_step2, n + 1)
                    settle(dve)
                    nc.vector.bn_aggr(in_mv[:, s, :], in_st[:, s, :]).then_inc(o_var.sem, 1)
                    dve.wait_ge(o_std.sem, o_std.done(n))
                    nc.vector.reciprocal(in_rs[:, s, :], in_sd[:, s, :]).then_inc(o_rstd.sem, 1)
                    dve.wait_ge(o_rstd.sem, o_rstd.done(n))
                    dve.wait_ge(o_tr.sem, o_tr.done(n4 - 5))
                    for q in range(4):
                        nc.vector.tensor_scalar(yn[:, s, q * HALF:(q + 1) * HALF], chunk(y, c)[:, q * HALF:(q + 1) * HALF],
                                                in_mv[:, s, 0:1], in_rs[:, s, :], ALU.subtract, ALU.mult).then_inc(o_yn.sem, 1)
                out_proj(b, 1, normalised, lambda c, s: normalised(c, s, from_quarter=EARLY))
                end_phase(dve, b, 6)


def launch_arrays(inputs):
    f = {k: np.asarray(v) for k, v in inputs.items()}

    def rows_to_k(w):
        return np.ascontiguousarray(w.T).reshape(-1, P, w.shape[0]).transpose(1, 0, 2)

    g = {}
    g["x"] = f["L0_attn_x"]
    Wq, Wk, Wv = f["L0_attn_Wq"], f["L0_attn_Wk"], f["L0_attn_Wv"]
    g["w_qkv"] = np.stack([rows_to_k(np.concatenate([Wk[i * P:(i + 1) * P], Wv[i * P:(i + 1) * P], Wq[i * REP * P:(i + 1) * REP * P]])).reshape(P, -1)
                           for i in range(KVH)])
    g["w_o"] = rows_to_k(f["L0_attn_Wo"])
    g["router"] = np.concatenate([rows_to_k(f["L0_ffn_gate_weight"]).reshape(P, -1), np.zeros((P, DM - KT * NE), np.float32)], 1)

    def groups(gate_up, down):
        gus = np.stack([rows_to_k(x).reshape(P, -1) for x in gate_up])
        dns = np.stack([rows_to_k(np.concatenate([x, np.zeros((DM, DT * P - FG), x.dtype)], 1)).reshape(P, -1) for x in down])
        return gus, dns
    gw, dw = f["L0_ffn_gate_up_weights"], f["L0_ffn_down_weights"]
    sgu, sdn = f["L0_ffn_shared_gate_up"], f["L0_ffn_shared_down"]
    g["gu0"], g["dn0"] = groups(
        [np.concatenate([gw[e, :FE], gw[e + 1, :FE], gw[e, FE:], gw[e + 1, FE:]]) for e in range(0, NE, 2)] + [sgu],
        [np.concatenate([dw[e], dw[e + 1]], 1) for e in range(0, NE, 2)] + [sdn])
    qg, qu, qd = f["L1_ffn_wq_gate"], f["L1_ffn_wq_up"], f["L1_ffn_wq_down"]
    g["gu1"], g["dn1"] = groups(
        [np.concatenate([qg[k * FG:(k + 1) * FG], qu[k * FG:(k + 1) * FG]]) for k in range(G1)],
        [qd[:, k * FG:(k + 1) * FG] for k in range(G1)])
    g["s_gu"] = np.stack([np.concatenate([f["L1_ffn_s_gate"][k * FG:(k + 1) * FG], f["L1_ffn_s_up"][k * FG:(k + 1) * FG]]) for k in range(G1)])
    g["s_dn"] = f["L1_ffn_s_down"].reshape(1, DM)
    W = f["L1_attn_W_in"]
    parts = [W[k * INNER:(k + 1) * INNER] for k in range(4)]
    g["w_in"] = np.stack([rows_to_k(np.concatenate([w[h * P:(h + 1) * P] for w in parts])).reshape(P, -1) for h in range(HP)])
    g["w_dec"] = rows_to_k(np.concatenate([W[4 * INNER:], np.zeros((P - SH, DM), np.float32)])).reshape(P, -1)
    g["w_out"] = rows_to_k(f["L1_attn_W_out"])
    g["gamma"] = np.ascontiguousarray(f["L1_attn_gamma"].reshape(NT, P).T)
    g["beta"] = np.ascontiguousarray(f["L1_attn_beta"].reshape(NT, P).T)
    g["d_skip"] = f["L1_attn_D"].reshape(HP, P)

    eye = np.eye(P, dtype=np.float32)
    g["ident4"] = np.tile(eye, (1, HALF // P))
    g["causal"] = np.triu(np.ones((P, P), np.float32))
    g["earlier"] = np.tile((np.arange(NE)[None, :] < np.arange(NE)[:, None]).astype(np.float32).reshape(1, -1), (P, 1))
    inv = (np.float32(1.0) / np.power(np.float32(10000.0), np.arange(0, P, 2, dtype=np.float32) / np.float32(P))).astype(np.float32)
    ang = np.outer(np.arange(T, dtype=np.float32), inv).astype(np.float32).astype(np.float64)
    c, s = np.cos(ang).T.astype(np.float32), np.sin(ang).T.astype(np.float32)
    g["cos"] = np.concatenate([c, c])
    g["sin"] = np.concatenate([-s, s])
    return {k: np.ascontiguousarray(v) for k, v in g.items()}


def kernel(**inputs):
    import concourse.bacc as bacc
    from concourse.bass_utils import run_bass_kernel_spmd

    nc = bacc.Bacc("TRN2", target_bir_lowering=False, num_devices=1)
    arrays = launch_arrays(inputs)
    aps = {k: nc.dram_tensor(f"in_{k}", v.shape, mybir.dt.from_np(v.dtype), kind="ExternalInput").ap() for k, v in arrays.items()}
    aps["out"] = nc.dram_tensor("out_x", (B, T, DM), F32, kind="ExternalOutput").ap()
    build(nc, aps)
    r = run_bass_kernel_spmd(nc, [{f"in_{k}": v for k, v in arrays.items()}], core_ids=[0])
    return r.results[0]["out_x"]
```
